# Optimizing a Trainium2 kernel written in Bass

```python
import numpy as np
import jax
import jax.numpy as jnp

def _softmax(x, axis=-1):
    return jax.nn.softmax(x, axis=axis)

def _gelu(x):
    return jax.nn.gelu(x, approximate=True)

def _silu(x):
    return jax.nn.silu(x)

def _sigmoid(x):
    return jax.nn.sigmoid(x)

def _layernorm(x, axis=-1, eps=1e-05):
    m = jnp.mean(x, axis=axis, keepdims=True)
    v = jnp.var(x, axis=axis, keepdims=True)
    return (x - m) / jnp.sqrt(v + eps)

def _scatter_add(tgt, idx, src, axis=0):
    return tgt.at[idx].add(src)

def _segment_sum(src, seg, n):
    return jax.ops.segment_sum(src, seg, n)
kernel_name = 'mk_gnn_resnorm_d2_gnn_r8_c708e9'

def setup_inputs(seed: int=0):
    np.random.seed(seed)
    _w = jnp.asarray

    def _rec_inputs():
        import jax
        import jax.numpy as jnp
        _gk = jax.random.key(seed)
        x = -0.0003713 + 1 * jax.random.normal(jax.random.fold_in(_gk, 1), (12500, 128), jnp.float32)
        src = jax.random.randint(jax.random.fold_in(_gk, 2), (200000,), 0, 12500, jnp.int32)
        dst = jnp.minimum((12500 * jax.random.uniform(jax.random.fold_in(_gk, 3), (200000,)) ** 2.0).astype(jnp.int32), 99999)
        _o = jnp.argsort(dst, stable=True)
        src = src[_o]
        dst = dst[_o]
        edge_attr3_1x32 = jax.random.uniform(jax.random.fold_in(_gk, 12), (200000, 1, 32), jnp.float32, 0.0, 1)
        edge_type_5 = jax.random.randint(jax.random.fold_in(_gk, 14), (200000,), 0, 5, jnp.int32)
        edge_weight1 = jax.random.uniform(jax.random.fold_in(_gk, 15), (200000, 1), jnp.float32, 0.0, 1)
        return (x, src, dst, edge_attr3_1x32, edge_type_5, edge_weight1)
    x, src, dst, edge_attr3_1x32, edge_type_5, edge_weight1 = _rec_inputs()

    def _L0_gnn_setup():
        import jax, jax.numpy as jnp
        import numpy as np
        N, E, D, T = (12500, 200000, 128, 5)
        EPS = 1e-05

        def _bn(x, gamma, beta):
            mu = jnp.mean(x, axis=0)
            var = jnp.mean((x - mu) ** 2, axis=0)
            return gamma * (x - mu) * jax.lax.rsqrt(var + EPS) + beta

        def _round(x, w, b, gamma, beta, src, dst, etype):
            h = jax.nn.relu(_bn(x, gamma, beta))
            h = jnp.einsum('nd,od->no', h, w) + b
            h3 = h.reshape(N, T, D)
            msg = h3[src, etype]
            return jax.ops.segment_sum(msg, dst, num_segments=N)
        key = jax.random.key(seed)
        ks = jax.random.split(key, 8)
        scale = 1.0 / np.sqrt(D)
        return {'features': jax.random.normal(ks[0], (N, D), dtype=jnp.float32), 'src': jax.random.randint(ks[1], (E,), 0, N, dtype=jnp.int32), 'dst': jax.random.randint(ks[2], (E,), 0, N, dtype=jnp.int32), 'etype': jax.random.randint(ks[3], (E,), 0, T, dtype=jnp.int32), 'w1': jax.random.normal(ks[4], (T * D, D), dtype=jnp.float32) * scale, 'b1': jnp.zeros((T * D,), dtype=jnp.float32), 'g1': jnp.ones((D,), dtype=jnp.float32), 'be1': jnp.zeros((D,), dtype=jnp.float32), 'w2': jax.random.normal(ks[5], (T * D, D), dtype=jnp.float32) * scale, 'b2': jnp.zeros((T * D,), dtype=jnp.float32), 'g2': jnp.ones((D,), dtype=jnp.float32), 'be2': jnp.zeros((D,), dtype=jnp.float32)}
    _L0_gnn_all = _L0_gnn_setup()
    _L0_gnn_in = {k: v for k, v in _L0_gnn_all.items() if k in ('w1', 'b1', 'g1', 'be1', 'w2', 'b2', 'g2', 'be2')}
    del _L0_gnn_all

    def _L1_gnn_setup():
        import jax, jax.numpy as jnp
        import numpy as np
        LOG2 = 0.6931471805599453

        def ssp(x):
            return jax.nn.softplus(x) - LOG2
        N_ATOMS = 12500
        N_PAIRS = 200000
        F_ATOM = 128
        F_FILT = 128
        N_RBF = 32
        key = jax.random.key(seed)
        ks = jax.random.split(key, 12)
        s = lambda k, fan_in, shape: jax.random.normal(k, shape, dtype=jnp.float32) / np.sqrt(fan_in)
        return {'x': jax.random.normal(ks[0], (N_ATOMS, F_ATOM), dtype=jnp.float32), 'pairlist': jax.random.randint(ks[1], (2, N_PAIRS), 0, N_ATOMS), 'f_ij': jax.random.uniform(ks[2], (N_PAIRS, 1, N_RBF), dtype=jnp.float32), 'f_ij_cutoff': jax.random.uniform(ks[3], (N_PAIRS, 1), dtype=jnp.float32), 'W_in': s(ks[4], F_ATOM, (F_ATOM, F_FILT)), 'Wf1': s(ks[5], N_RBF, (N_RBF, F_FILT)), 'bf1': jnp.zeros((F_FILT,), dtype=jnp.float32), 'Wf2': s(ks[6], F_FILT, (F_FILT, F_FILT)), 'bf2': jnp.zeros((F_FILT,), dtype=jnp.float32), 'Wo1': s(ks[7], F_FILT, (F_FILT, F_ATOM)), 'bo1': jnp.zeros((F_ATOM,), dtype=jnp.float32), 'Wo2': s(ks[8], F_ATOM, (F_ATOM, F_ATOM)), 'bo2': jnp.zeros((F_ATOM,), dtype=jnp.float32)}
    _L1_gnn_all = _L1_gnn_setup()
    _L1_gnn_in = {k: v for k, v in _L1_gnn_all.items() if k in ('W_in', 'Wf1', 'bf1', 'Wf2', 'bf2', 'Wo1', 'bo1', 'Wo2', 'bo2')}
    del _L1_gnn_all
    return {'x': x, 'src': src, 'dst': dst, 'edge_attr3_1x32': edge_attr3_1x32, 'edge_type_5': edge_type_5, 'edge_weight1': edge_weight1, 'L0_gnn_w1': _L0_gnn_in['w1'], 'L0_gnn_b1': _L0_gnn_in['b1'], 'L0_gnn_g1': _L0_gnn_in['g1'], 'L0_gnn_be1': _L0_gnn_in['be1'], 'L0_gnn_w2': _L0_gnn_in['w2'], 'L0_gnn_b2': _L0_gnn_in['b2'], 'L0_gnn_g2': _L0_gnn_in['g2'], 'L0_gnn_be2': _L0_gnn_in['be2'], 'L1_gnn_W_in': _L1_gnn_in['W_in'], 'L1_gnn_Wf1': _L1_gnn_in['Wf1'], 'L1_gnn_bf1': _L1_gnn_in['bf1'], 'L1_gnn_Wf2': _L1_gnn_in['Wf2'], 'L1_gnn_bf2': _L1_gnn_in['bf2'], 'L1_gnn_Wo1': _L1_gnn_in['Wo1'], 'L1_gnn_bo1': _L1_gnn_in['bo1'], 'L1_gnn_Wo2': _L1_gnn_in['Wo2'], 'L1_gnn_bo2': _L1_gnn_in['bo2']}

def reference(x, src, dst, edge_attr3_1x32, edge_type_5, edge_weight1, L0_gnn_w1, L0_gnn_b1, L0_gnn_g1, L0_gnn_be1, L0_gnn_w2, L0_gnn_b2, L0_gnn_g2, L0_gnn_be2, L1_gnn_W_in, L1_gnn_Wf1, L1_gnn_bf1, L1_gnn_Wf2, L1_gnn_bf2, L1_gnn_Wo1, L1_gnn_bo1, L1_gnn_Wo2, L1_gnn_bo2):
    import jax
    import jax.numpy as jnp

    def _L0_gnn_ref(features, src, dst, etype, w1, b1, g1, be1, w2, b2, g2, be2):
        import jax, jax.numpy as jnp
        import numpy as np
        N, E, D, T = (12500, 200000, 128, 5)
        EPS = 1e-05

        def _bn(x, gamma, beta):
            mu = jnp.mean(x, axis=0)
            var = jnp.mean((x - mu) ** 2, axis=0)
            return gamma * (x - mu) * jax.lax.rsqrt(var + EPS) + beta

        def _round(x, w, b, gamma, beta, src, dst, etype):
            h = jax.nn.relu(_bn(x, gamma, beta))
            h = jnp.einsum('nd,od->no', h, w) + b
            h3 = h.reshape(N, T, D)
            msg = h3[src, etype]
            return jax.ops.segment_sum(msg, dst, num_segments=N)
        h_new = _round(features, w1, b1, g1, be1, src, dst, etype)
        h_new = _round(h_new, w2, b2, g2, be2, src, dst, etype)
        return h_new + features

    def _L1_gnn_ref(x, pairlist, f_ij, f_ij_cutoff, W_in, Wf1, bf1, Wf2, bf2, Wo1, bo1, Wo2, bo2):
        import jax, jax.numpy as jnp
        import numpy as np
        LOG2 = 0.6931471805599453

        def ssp(x):
            return jax.nn.softplus(x) - LOG2
        N_ATOMS = 12500
        N_PAIRS = 200000
        F_ATOM = 128
        F_FILT = 128
        N_RBF = 32
        idx_i, idx_j = (pairlist[0], pairlist[1])
        h = x @ W_in
        W_ij = ssp(f_ij[:, 0, :] @ Wf1 + bf1) @ Wf2 + bf2
        W_ij = W_ij * f_ij_cutoff
        x_ij = h[idx_j] * W_ij
        out = jax.ops.segment_sum(x_ij, idx_i, num_segments=x.shape[0])
        return ssp(out @ Wo1 + bo1) @ Wo2 + bo2
    edge_index = jnp.stack([src, dst])
    x = _layernorm(x + _L0_gnn_ref(x, src, dst, edge_type_5, L0_gnn_w1, L0_gnn_b1, L0_gnn_g1, L0_gnn_be1, L0_gnn_w2, L0_gnn_b2, L0_gnn_g2, L0_gnn_be2), axis=-1)
    x = _layernorm(x + _L1_gnn_ref(x, edge_index, edge_attr3_1x32, edge_weight1, L1_gnn_W_in, L1_gnn_Wf1, L1_gnn_bf1, L1_gnn_Wf2, L1_gnn_bf2, L1_gnn_Wo1, L1_gnn_bo1, L1_gnn_Wo2, L1_gnn_bo2), axis=-1)
    return x

_drawn_inputs = setup_inputs


def setup_inputs(seed=0):
    import zlib

    import numpy as np

    out = dict(_drawn_inputs(seed))
    spreads = {'L0_gnn_b1': (0.0, 0.1),
     'L0_gnn_g1': (1.0, 0.2),
     'L0_gnn_be1': (0.0, 0.1),
     'L0_gnn_b2': (0.0, 0.1),
     'L0_gnn_g2': (1.0, 0.2),
     'L0_gnn_be2': (0.0, 0.1),
     'L1_gnn_bf1': (0.0, 0.1),
     'L1_gnn_bf2': (0.0, 0.1),
     'L1_gnn_bo1': (0.0, 0.1),
     'L1_gnn_bo2': (0.0, 0.1)}
    factors = {}
    for name, (base, spread) in spreads.items():
        noise = np.random.default_rng([zlib.crc32(name.encode()), seed]).standard_normal(out[name].shape)
        drawn = base * np.exp(spread * noise) if base else spread * noise
        out[name] = jnp.asarray(drawn.astype(out[name].dtype))
    for name, factor in factors.items():
        out[name] = (out[name] * factor).astype(out[name].dtype)
    return out
```

```python
import numpy as np

import concourse.bass as bass
from concourse import mybir
from contextlib import ExitStack

N, E, D, T, RBF = 12500, 200000, 128, 5, 32
EPS = 1e-5
LOG2 = 0.6931471805599453
P = 128
WINDOW = 128
GROUP_TILES = 4
GROUP_EDGES = GROUP_TILES * P
HALF_TILES = 2 * GROUP_TILES
ITER_TILES = 2 * HALF_TILES
ITERS = -(-E // (ITER_TILES * P))
TILES = ITERS * ITER_TILES
GROUPS = TILES // GROUP_TILES
COLS_HALF = HALF_TILES * P
COLS = TILES + ITER_TILES
HALVES = 2 * ITERS + 2
BLOCKS = -(-N // P)
NPAD = BLOCKS * P
WIDE = 512
COPIES = HALF_TILES
CHUNKS = 2 * -(-NPAD // (2 * WIDE))
NBUF = CHUNKS * WIDE
ACC_ROWS = NBUF + 2 * WIDE
SUM_STEPS = COPIES.bit_length() - 1
ZERO_COLS = ACC_ROWS // 8
WIDE_STEPS = -(-N // WIDE)
BODY = 14
TRANS_ITERS = BLOCKS // BODY
SLOTS = 7
BN_CHUNK = 500
TD = T * D
RANGE_PARTS = GROUPS // GROUP_TILES
EXP_LN_SET = 6
assert BLOCKS % BODY == 0 and N % BN_CHUNK == 0 and GROUPS % 4 == 0 and BODY % SLOTS == 0


def gnn_program(nc, dram, out):
    f32, bf16, i32 = mybir.dt.float32, mybir.dt.bfloat16, mybir.dt.int32
    ALU, ACT, AX = mybir.AluOpType, mybir.ActivationFunctionType, mybir.AxisListType
    ds = bass.ds

    ctx = ExitStack()
    with ctx:
        def sb(name, shape, dt=f32):
            return ctx.enter_context(nc.sbuf_tensor(name, shape, dt))

        def pb(name, shape):
            return ctx.enter_context(nc.psum_tensor(name, shape, f32))

        def sem(name):
            return ctx.enter_context(nc.semaphore(name))

        table = [nc.dram_tensor(f"messages_{i}", (NPAD, TD), f32).ap() for i in range(2)]
        htable = nc.dram_tensor("h_in", (NPAD, D), f32).ap()
        acc_rows = [nc.dram_tensor(f"acc_{c}", (ACC_ROWS, D), f32).ap() for c in range(COPIES)]
        base_dram = nc.dram_tensor("group_base", (RANGE_PARTS, 4), i32).ap()
        span_dram = nc.dram_tensor("group_span", (RANGE_PARTS, 4), i32).ap()

        buf_x = sb("buf_x", [P, NBUF])
        buf_a = sb("buf_a", [P, NBUF])
        src_idx = sb("src_idx", [P, COLS], i32)
        msg_idx = sb("msg_idx", [P, COLS], i32)
        dst_local = sb("dst_local", [P, COLS])
        cutoff = sb("cutoff", [P, COLS])
        base_row = sb("base_row", [1, GROUPS + 4], i32)
        base_bc = sb("base_bc", [P, GROUPS], i32)
        span_bc = sb("span_bc", [P, GROUPS], i32)
        flag_f = sb("flag_f", [P, 1])
        flag_i = sb("flag_i", [P, 1], i32)
        idx_stage = sb("idx_stage", [P, 2, HALF_TILES], i32)
        gathered = sb("gathered", [P, 2, HALF_TILES, D])
        onehot = sb("onehot", [P, 2, HALF_TILES, WINDOW])
        work = sb("work", [P, 10 * WIDE])
        x_onehot = sb("x_onehot", [P, GROUP_TILES, WIDE])
        x_rem = sb("x_rem", [P, GROUP_TILES])
        h_stage = sb("h_stage", [P, 2, P])
        t_stage = sb("t_stage", [P, 2, P])
        iota_f = sb("iota_f", [P, WIDE])
        part_i = sb("part_i", [P, 1], i32)
        part_f = sb("part_f", [P, 1])
        ident = sb("ident", [P, P])
        w_types = [sb(f"w_types_{i}", [P, TD]) for i in range(2)]
        b_types = [sb(f"b_types_{i}", [P, TD]) for i in range(2)]
        gamma = [sb(f"gamma_{i}", [P, 1]) for i in range(2)]
        beta = [sb(f"beta_{i}", [P, 1]) for i in range(2)]
        w_in = sb("w_in", [P, D])
        wf1 = sb("wf1", [RBF + 1, D])
        wf2 = sb("wf2", [P, D])
        bf2 = sb("bf2", [1, D])
        bf2_f = sb("bf2_f", [1, 3, D])
        bf2_parts = sb("bf2_parts", [1, 3, D], bf16)
        bf2_rows = sb("bf2_rows", [3, D], bf16)
        ones_rows = sb("ones_rows", [3, P], bf16)
        wo1 = sb("wo1", [P, D])
        bo1 = sb("bo1", [P, 1])
        wo2 = sb("wo2", [P, D])
        bo2_bc = sb("bo2_bc", [P, D])
        first_w = sb("first_w", [P, 2])
        trash_row = sb("trash_row", [P, 1])
        bn_raw = sb("bn_raw", [P, N // BN_CHUNK, 6])
        bn_mv = sb("bn_mv", [P, 2])
        bn_scale = sb("bn_scale", [P, 1])
        bn_shift = sb("bn_shift", [P, 1])
        bn_tmp = sb("bn_tmp", [P, 2])
        eps_col = sb("eps_col", [P, 1])
        half_col = sb("half_col", [P, 1])
        ln_raw = sb("ln_raw", [P, CHUNKS * 4, 6])
        ln_mean = sb("ln_mean", [P, CHUNKS * 4])
        ln_rstd = sb("ln_rstd", [P, CHUNKS * 4])
        ln_tmp = sb("ln_tmp", [P, 2, CHUNKS * 4])

        out_rows = work[:, 0:SLOTS * TD].rearrange("p (q n) -> p q n", q=SLOTS)
        stage5 = work[:, :].rearrange("p (a j n) -> p a j n", a=5, j=2)
        abs_z, relu_z, log_z, soft, msg = (stage5[:, a] for a in range(5))
        x_rows = work[:, 0:SLOTS * D].rearrange("p (q n) -> p q n", q=SLOTS)
        h_rows = work[:, 1024:1024 + SLOTS * D].rearrange("p (q n) -> p q n", q=SLOTS)
        edge_slots = [buf_a[:, i * 2 * COLS_HALF:(i + 1) * 2 * COLS_HALF].rearrange("p (h n) -> p h n", h=2) for i in range(3)]
        src_bc, dst_bc = edge_slots[0].bitcast(i32), edge_slots[1].bitcast(i32)
        same_src = edge_slots[2].rearrange("p h (t n) -> p h t n", t=HALF_TILES)
        h_edge = buf_a[:, 6144:7168].rearrange("p (j n) -> p j n", j=2)
        h_win = buf_a[:, 7168:7680].rearrange("p (h j n) -> p h j n", h=2, j=2)
        x_dst = buf_a[:, 7680:8192]
        x_h = buf_a[:, 8192:8192 + P]
        uniq_idx = buf_a[:, 8320:8320 + COLS].bitcast(i32)
        win_node = buf_a[:, 9984:9984 + GROUPS + 4]
        cut_stage = buf_a[:, 10400:10400 + 2 * HALF_TILES].rearrange("p (h t) -> p h t", h=2)
        to_trash = buf_a[:, 10432:10432 + HALF_TILES]
        f_sb = buf_a[0:RBF + 1, 10496:10496 + 4 * GROUP_EDGES].rearrange("p (h j n) -> p h j n", h=2, j=2)
        out_t = buf_a[:, 10496:10496 + 2 * WIDE].rearrange("p (s n) -> p s n", s=2)
        spread = onehot[:, :, :, :].rearrange("p h t n -> p h (t n)")
        combined = gathered[:, :, :, :].rearrange("p h t n -> p h (t n)")
        copy_rows = buf_a[:, 0:2 * COPIES * WIDE].rearrange("p (s c n) -> p s c n", s=2, c=COPIES)
        zeros = work[:, 0:ZERO_COLS]
        dst_groups = buf_a[0:RANGE_PARTS, 0:4 * GROUP_EDGES].bitcast(i32).rearrange("p (g n) -> p g n", g=4)
        dst_tiles = buf_a[:, 2048:2048 + COLS].bitcast(i32)
        type_tiles = buf_a[:, 4096:4096 + COLS].bitcast(i32)
        range_f = buf_a[0:RANGE_PARTS, 6144:6152].rearrange("p (a g) -> p a g", a=2)
        iota_i = buf_a[:, 6400:6400 + WIDE].bitcast(i32)
        range_i = buf_a[0:RANGE_PARTS, 6152:6160].bitcast(i32).rearrange("p (a g) -> p a g", a=2)

        ps_a = [pb(f"ps_a{i}", [P, 2 * WIDE]) for i in range(2)]
        ps_b = [pb(f"ps_b{i}", [P, WIDE]) for i in range(4)]
        ps_z = [ps_a[0][:, j * WIDE:(j + 1) * WIDE] for j in range(2)]
        ps_w = [ps_a[1][:, j * WIDE:(j + 1) * WIDE] for j in range(2)]
        ps_agg = [ps_b[j][:, 0:WINDOW] for j in range(2)]
        ps_extra = ps_b[2]
        ps_first = ps_b[3][:, 0:HALF_TILES]
        ps_h, ps_c = ps_b[0:2], ps_b[2:4]

        s_range_in, s_edges_in, s_x_in, s_const_in = sem("range_in"), sem("edges_in"), sem("x_in"), sem("const_in")
        s_iota, s_setup = sem("iota_made"), sem("setup_step")
        s_range_out, s_range_back = sem("range_stored"), sem("range_back")
        s_parts_in, s_bias_split = sem("bias_rows_in"), sem("bias_split")
        s_bn, s_bn_sd = [sem(f"bn_step_{i}") for i in range(2)], [sem(f"bn_sd_{i}") for i in range(2)]
        s_h_ready = [sem(f"h_ready_{i}") for i in range(2)]
        s_mm_done = [sem(f"transform_done_{i}") for i in range(2)]
        s_row_ready = [sem(f"rows_ready_{i}") for i in range(2)]
        s_row_out = [[sem(f"rows_out_{i}_{q}") for q in range(SLOTS)] for i in range(2)]
        s_clear = [sem(f"acc_cleared_{i}") for i in range(3)]
        s_turn = [sem(f"gather_turn_{i}") for i in range(3)]
        s_idx = [sem(f"idx_ready_{i}") for i in range(3)]
        s_gather = [[[sem(f"gathered_{i}_{h}_{j}") for j in range(2)] for h in range(2)] for i in range(3)]
        s_onehot = [sem(f"onehot_ready_{i}") for i in range(3)]
        s_agg = [sem(f"agg_ready_{i}") for i in range(3)]
        s_acc = [sem(f"acc_done_{i}") for i in range(3)]
        s_xoh = [sem(f"extra_onehot_{i}") for i in range(3)]
        s_xagg = [sem(f"extra_agg_{i}") for i in range(3)]
        s_xr_in = [sem(f"x_rows_in_{q}") for q in range(SLOTS)]
        s_cp, s_tr, s_y, s_yst = sem("block_copied"), sem("block_turned"), sem("y_done"), sem("y_stats")
        s_ln, s_ln_sd = [sem(f"ln_step_{i}") for i in range(2)], [sem(f"ln_sd_{i}") for i in range(2)]
        s_x1, s_x1t, s_x1c, s_x1b = sem("x1_done"), sem("x1_turned"), sem("x1_copied"), sem("x1_kept")
        s_hmm, s_hrow = sem("h_done"), sem("h_rows_ready")
        s_hout = [sem(f"h_rows_out_{q}") for q in range(SLOTS)]
        s_f_in = [sem(f"filter_in_{h}") for h in range(2)]
        s_z, s_act, s_soft, s_w, s_msg = (sem(n) for n in (
            "z_ready", "act_step", "soft_done", "filter_ready", "msg_done"))
        s_cut, s_xadd = sem("cutoff_staged"), sem("extra_added")
        s_src_in, s_dup, s_first, s_uniq = [sem(f"src_in_{h}") for h in range(2)], sem("dup_ready"), sem("first_ready"), sem("uniq_step")
        s_edge_in, s_win_in = [sem(f"edge_rows_in_{h}") for h in range(2)], [sem(f"h_window_in_{h}") for h in range(2)]
        s_spread, s_same, s_hexp, s_hcopy = sem("spread_ready"), sem("same_ready"), sem("h_edges_ready"), sem("h_edges_copied")
        s_comb, s_comb_out = sem("combined_ready"), sem("combined_copied")
        s_scat = [[sem(f"scattered_{h}_{j}") for j in range(2)] for h in range(2)]
        s_go = sem("scatter_turn")
        s_xh_in = sem("extra_h_in")
        s_zero, s_zeroed = sem("zeros_made"), sem("copies_zeroed")
        s_cp_in, s_cp_sum, s_cp_t, s_cp_out = [sem(f"copies_in_{i}") for i in range(2)], sem("copies_summed"), sem("sums_turned"), sem("sums_copied")
        s_fz, s_fact, s_fsoft, s_fo, s_fy, s_fst = (sem(n) for n in (
            "out_z_ready", "out_act_step", "out_soft_done", "out_ready", "out_y_done", "out_y_stats"))
        s_fin, s_fin_out = sem("final_ready"), [sem(f"final_out_{s}") for s in range(2)]

        block = ctx.enter_context(nc.Block())

        SLOT2 = 2

        @block.sync
        def _(sp):
            sp.dma_start(dst_groups, dram["dst_groups"].rearrange("p (g n) -> p g n", g=4)).then_inc(s_range_in, 16)
            sp.dma_start(dst_tiles, dram["dst"]).then_inc(s_edges_in, 16)
            sp.dma_start(type_tiles, dram["etype"]).then_inc(s_edges_in, 16)
            sp.dma_start(src_idx[:, :], dram["src"]).then_inc(s_edges_in, 16)
            sp.dma_start(cutoff[:, :], dram["cutoff"]).then_inc(s_edges_in, 16)
            sp.dma_start(buf_x[:, 0:NPAD], dram["xT"]).then_inc(s_x_in, 16)
            for t, name in ((gamma[0], "g1"), (beta[0], "be1"), (w_types[0], "w1T"), (gamma[1], "g2"),
                            (beta[1], "be2"), (w_types[1], "w2T"), (w_in, "W_in"), (wf2, "Wf2"),
                            (bf2, "bf2"), (wo1, "Wo1"), (bo1, "bo1"), (wo2, "Wo2"), (first_w, "first_w")):
                sp.dma_start(t[:, :], dram[name]).then_inc(s_const_in, 16)
            sp.dma_start(wf1[0:RBF, :], dram["Wf1"]).then_inc(s_const_in, 16)
            sp.dma_start(wf1[RBF:RBF + 1, :], dram["bf1"]).then_inc(s_const_in, 16)
            for t, name, n in ((b_types[0], "b1", TD), (b_types[1], "b2", TD), (bo2_bc, "bo2", D)):
                sp.dma_start(t[:, :], dram[name].broadcast_to([P, n])).then_inc(s_const_in, 16)
            sp.wait_ge(s_setup, 4)
            sp.dma_start(base_dram, range_i[:, 0, :]).then_inc(s_range_out, 16)
            sp.dma_start(span_dram, range_i[:, 1, :]).then_inc(s_range_out, 16)
            sp.wait_ge(s_range_out, 32)
            base_flat = base_dram.rearrange("(o p) g -> o (p g)", o=1)
            span_flat = span_dram.rearrange("(o p) g -> o (p g)", o=1)
            sp.dma_start(base_row[0:1, 0:GROUPS], base_flat).then_inc(s_range_back, 16)
            sp.dma_start(base_bc[:, :], base_flat.broadcast_to([P, GROUPS])).then_inc(s_range_back, 16)
            sp.dma_start(span_bc[:, :], span_flat.broadcast_to([P, GROUPS])).then_inc(s_range_back, 16)
            sp.wait_ge(s_bias_split, 5)
            for i in range(3):
                sp.dma_start(bf2_rows[i:i + 1, :], bf2_parts[0:1, i, :]).then_inc(s_parts_in, 16)

            for rnd in range(2):
                with sp.Fori(0, TRANS_ITERS) as r:
                    for j in range(BODY):
                        sp.wait_ge(s_row_ready[rnd], r * BODY + (j + 1 + SLOT2))
                        sp.dma_start(table[rnd][ds((r * BODY + j) * P, P), :],
                                     out_rows[:, j % SLOTS, :]).then_inc(s_row_out[rnd][j % SLOTS], 16)

                if rnd == 0:
                    sp.wait_ge(s_zero, 1)
                    for acc in acc_rows:
                        flat = acc.rearrange("(p x) n -> p (x n)", p=P)
                        with sp.Fori(0, ACC_ROWS // ZERO_COLS) as q:
                            sp.dma_start(flat[:, ds(q * ZERO_COLS, ZERO_COLS)], zeros).then_inc(s_zeroed, 16)
                else:
                    sp.wait_ge(s_h_ready[1], BLOCKS)
                    sp.wait_ge(s_mm_done[1], BLOCKS + SLOT2)
                    for h in range(2):
                        sp.dma_start(src_bc[:, h, :], dram["src_row"][0:1, h * COLS_HALF:(h + 1) * COLS_HALF]
                                     .broadcast_to([P, COLS_HALF])).then_inc(s_src_in[h], 16)
                    with sp.Fori(0, ITERS) as r:
                        for h in range(2):
                            sp.wait_ge(s_dup, r * 2 + (h + 1))
                            sp.dma_start(src_bc[:, h, :],
                                         dram["src_row"][0:1, ds((r * 2 + (2 + h)) * COLS_HALF, COLS_HALF)]
                                         .broadcast_to([P, COLS_HALF])).then_inc(s_src_in[h], 16)
                    for h in range(2):
                        sp.wait_ge(s_src_in[h], 16 * (ITERS + 1))

            for q in range(SLOTS):
                sp.wait_ge(s_row_out[1][q], 16 * (BLOCKS // SLOTS + 1))
            with sp.Fori(0, TRANS_ITERS) as r:
                for j in range(BODY):
                    sp.wait_ge(s_y, r * BODY + (j + 1))
                    sp.dma_start(x_rows[:, j % SLOTS, :],
                                 dram["x"][ds((r * BODY + j) * P, P), :]).then_inc(s_xr_in[j % SLOTS], 16)
            with sp.Fori(0, TRANS_ITERS) as r:
                for j in range(BODY):
                    sp.wait_ge(s_hrow, r * BODY + (j + 1 + SLOT2))
                    sp.dma_start(htable[ds((r * BODY + j) * P, P), :],
                                 h_rows[:, j % SLOTS, :]).then_inc(s_hout[j % SLOTS], 16)

            def load_attributes(h, half):
                sp.dma_start(f_sb[0:RBF, h, :, :], dram["attr"][ds(half * (2 * RBF), 2 * RBF), :]
                             .rearrange("(j r) n -> r j n", j=2)).then_inc(s_f_in[h], 16)

            def load_ends(h, half):
                for t, name in ((dst_bc, "dst_row"), (src_bc, "src_row")):
                    sp.dma_start(t[:, h, :], dram[name][0:1, ds(half * COLS_HALF, COLS_HALF)].broadcast_to([P, COLS_HALF])
                                 ).then_inc(s_edge_in[h], 16)

            def load_windows(h, bases):
                for j in range(2):
                    sp.dma_start(h_win[:, h, j, :], htable[ds(bases[j], WINDOW), :]).then_inc(s_win_in[h], 16)

            def load_bases(r):
                return nc.values_load_multi_w_load_instructions(
                    base_row[0:1, ds(r * 4, 4)], engines=[mybir.EngineType.SP], min_val=0, max_val=N - WINDOW,
                    skip_runtime_bounds_check_because="computed as a minimum with N - WINDOW")[1]

            for q in range(SLOTS):
                sp.wait_ge(s_hout[q], 16 * (BLOCKS // SLOTS + 1))
            bases = load_bases(0)
            flag = nc.sync.value_load(flag_i[0:1, 0:1], min_val=0, max_val=1)
            for h in range(2):
                load_attributes(h, h)
                load_ends(h, h)
                load_windows(h, bases[2 * h:2 * h + 2])
            with sp.Fori(0, ITERS) as r:
                bases = load_bases(r + 1)
                for h in range(2):
                    with sp.If(flag > 0):
                        with sp.Fori(0, 2) as j:
                            with sp.Fori(0, BLOCKS) as b:
                                step = ((r * 2 + h) * 2 + j) * BLOCKS + b
                                sp.wait_ge(s_xagg[2], step + 1)
                                sp.dma_start(x_h, htable[ds(b * P, P), :]).then_inc(s_xh_in, 16)
                    k = r * 2 + h
                    sp.wait_ge(s_z, k * 2 + 2)
                    load_attributes(h, k + 2)
                    sp.wait_ge(s_same, k + 1)
                    load_ends(h, k + 2)
                    sp.wait_ge(s_hexp, k * 2 + 2)
                    load_windows(h, bases[2 * h:2 * h + 2])
            for h in range(2):
                sp.wait_ge(s_f_in[h], 16 * (ITERS + 1))
                sp.wait_ge(s_edge_in[h], 32 * (ITERS + 1))
                sp.wait_ge(s_win_in[h], 32 * (ITERS + 1))

            def load_copies(s, m):
                for c in range(COPIES):
                    sp.dma_start(copy_rows[:, s, c, :].rearrange("p (b n) -> p b n", b=4),
                                 acc_rows[c][ds(m * WIDE, WIDE), :].rearrange("(b p) n -> p b n", p=P)
                                 ).then_inc(s_cp_in[s], 16)

            for h in range(2):
                for j in range(2):
                    sp.wait_ge(s_scat[h][j], 64 * ITERS)
            load_copies(0, 0)
            load_copies(1, 1)
            with sp.Fori(0, CHUNKS // 2) as r:
                for s in range(2):
                    sp.wait_ge(s_cp_t, r * 2 + (s + 1))
                    load_copies(s, r * 2 + (2 + s))
            with sp.Fori(0, CHUNKS // 2) as r:
                for s in range(2):
                    sp.wait_ge(s_fin, r * 2 + (s + 1))
                    sp.dma_start(out[ds((r * 2 + s) * WIDE, WIDE), :].rearrange("(b p) n -> p b n", p=P),
                                 msg[:, s, :].rearrange("p (b n) -> p b n", b=4)).then_inc(s_fin_out[s], 16)
            for s in range(2):
                sp.wait_ge(s_cp_in[s], 16 * COPIES * (CHUNKS // 2 + 1))
            for s in range(2):
                sp.wait_ge(s_fin_out[s], 16 * (CHUNKS // 2 + 1))

        @block.gpsimd
        def _(pool):
            nc.gpsimd.iota(iota_i, [[1, WIDE]], base=0, channel_multiplier=0).then_inc(s_iota, 1)
            nc.gpsimd.iota(part_i[:, :], [[0, 1]], base=0, channel_multiplier=1).then_inc(s_iota, 1)

            def gather_pass(p, source, last_wait):
                for s, v in last_wait:
                    pool.wait_ge(s, v)
                with pool.Fori(0, ITERS) as r:
                    for h in range(2):
                        pool.wait_ge(s_idx[p], r * 2 + (h + 1))
                        pool.sem_inc(s_turn[p], 1)
                        for t in range(HALF_TILES):
                            nc.gpsimd.indirect_dma_start(
                                gathered[:, h, t, :], None, source,
                                bass.IndirectOffsetOnAxis(ap=idx_stage[:, h, t:t + 1], axis=0),
                            ).then_inc(s_gather[p][h][t // GROUP_TILES], 16)

            pool.wait_ge(s_setup, 17)
            nc.gpsimd.memset(buf_a[:, :], 0.0).then_inc(s_clear[0], 1)
            for rnd in range(2):
                if rnd == 1:
                    pool.wait_ge(s_h_ready[0], BLOCKS)
                    nc.gpsimd.memset(buf_x[:, :], 0.0).then_inc(s_clear[1], 1)
                gather_pass(rnd, table[rnd].rearrange("n (t d) -> (n t) d", t=T),
                            [(s_row_out[rnd][q], 16 * (BLOCKS // SLOTS + 1)) for q in range(SLOTS)])
            pool.wait_ge(s_zeroed, 16 * COPIES * (ACC_ROWS // ZERO_COLS))
            def scatter_sums(r, first):
                for h in range(2):
                    for j in range(2):
                        pool.wait_ge(s_idx[2], r * 2 + (h + 1))
                        pool.wait_ge(s_comb_out, r * 4 + (2 * h + j + 1 + SLOT2))
                        if h == 1 or not first:
                            pool.wait_ge(s_scat[1 - h][j], r * 64 + 64 * h)
                        pool.sem_inc(s_go, 1)
                        for t in range(j * GROUP_TILES, (j + 1) * GROUP_TILES):
                            nc.gpsimd.indirect_dma_start(
                                acc_rows[t], bass.IndirectOffsetOnAxis(ap=idx_stage[:, h, t:t + 1], axis=0),
                                gathered[:, h, t, :], None, compute_op=ALU.add,
                            ).then_inc(s_scat[h][j], 16)

            scatter_sums(0, True)
            with pool.Fori(1, ITERS) as r:
                scatter_sums(r, False)

        @block.scalar
        def _(act):
            for rnd in range(2):
                feat = buf_x if rnd == 0 else buf_a
                act.wait_ge(s_bn[rnd], 26)
                nc.scalar.activation(bn_tmp[:, 0:1], bn_mv[:, 1:2], ACT.Sqrt, bias=eps_col[:, 0:1]).then_inc(s_bn_sd[rnd], 1)
                act.wait_ge(s_bn[rnd], 30)
                with act.Fori(0, TRANS_ITERS) as r:
                    for j in range(BODY):
                        act.wait_ge(s_mm_done[rnd], r * BODY + (j + 1))
                        nc.scalar.activation(h_stage[:, j % 2, :], feat[:, ds((r * BODY + j) * P, P)], ACT.Relu,
                                             bias=bn_shift[:, 0:1], scale=bn_scale[:, 0:1]).then_inc(s_h_ready[rnd], 1)

            act.wait_ge(s_acc[1], GROUPS + SLOT2)
            with act.Fori(0, TRANS_ITERS) as r:
                for j in range(BODY):
                    act.wait_ge(s_tr, r * BODY + (j + 1))
                    nc.scalar.activation(h_stage[:, j % 2, :], buf_x[:, ds((r * BODY + j) * P, P)],
                                         ACT.Copy).then_inc(s_cp, 1)
            act.wait_ge(s_ln[0], 6)
            nc.scalar.activation(ln_tmp[:, 0, 0:BLOCKS], ln_tmp[:, 1, 0:BLOCKS], ACT.Sqrt,
                                 bias=eps_col[:, 0:1]).then_inc(s_ln_sd[0], 1)
            with act.Fori(0, TRANS_ITERS) as r:
                for j in range(BODY):
                    act.wait_ge(s_x1t, r * BODY + (j + 1 + SLOT2))
                    act.wait_ge(s_hmm, r * BODY + (j + 1))
                    nc.scalar.activation(t_stage[:, j % 2, :], ps_b[2 + j % 2][:, 0:P], ACT.Copy).then_inc(s_x1c, 1)

            def softplus_half(k):
                for j in range(2):
                    act.wait_ge(s_z, k * 2 + (j + 1))
                    act.wait_ge(s_act, k * 6 + 1)
                    nc.scalar.activation(abs_z[:, j, :], ps_z[j], ACT.Abs).then_inc(s_act, 1)
                for j in range(2):
                    act.wait_ge(s_act, k * 6 + (2 + j))
                    nc.scalar.activation(abs_z[:, j, :], abs_z[:, j, :], ACT.Exp, scale=-1.0).then_inc(s_act, 1)
                for j in range(2):
                    act.wait_ge(s_act, k * 6 + (4 + j))
                    act.wait_ge(s_soft, k * 2 + SLOT2)
                    nc.scalar.activation(log_z[:, j, :], abs_z[:, j, :], ACT.Ln, bias=half_col[:, 0:1],
                                         scale=0.5).then_inc(s_act, 1)

            for q in range(SLOTS):
                act.wait_ge(s_hout[q], 16 * (BLOCKS // SLOTS + 1))
            def convolution_step(r, first):
                for h in range(2):
                    k = r * 2 + h
                    for j in range(2):
                        act.wait_ge(s_hexp, k * 2 + (j + 1))
                        act.wait_ge(s_msg, k * 2 + (j + 1))
                        nc.scalar.activation(h_edge[:, j, :], ps_h[j][:, :], ACT.Copy).then_inc(s_hcopy, 1)
                    softplus_half(k + 1)
                    for j in range(2):
                        act.wait_ge(s_comb, k * 2 + (j + 1 + SLOT2))
                        if not first:
                            act.wait_ge(s_scat[h][j], r * 64)
                        nc.scalar.activation(combined[:, h, j * WIDE:(j + 1) * WIDE], ps_c[j][:, :],
                                             ACT.Copy).then_inc(s_comb_out, 1)

            nc.scalar.add_instruction(mybir.InstLoadActFuncSet(
                name=nc.get_next_instruction_name(), engine=mybir.EngineType.Activation, act_func_set_id=EXP_LN_SET))
            softplus_half(0)
            convolution_step(0, True)
            with act.Fori(1, ITERS) as r:
                convolution_step(r, False)

            def copy_turned(m, s):
                act.wait_ge(s_cp_t, m + 1)
                act.wait_ge(s_fz, m + 1)
                nc.scalar.activation(out_t[:, s, :], ps_b[s][:, :], ACT.Copy).then_inc(s_cp_out, 1)

            copy_turned(0, 0)
            with act.Fori(0, CHUNKS // 2) as r:
                for s in range(2):
                    m = r * 2 + s
                    act.wait_ge(s_fz, m + (1 + SLOT2))
                    act.wait_ge(s_fact, m * 4 + 1)
                    nc.scalar.activation(abs_z[:, s, :], ps_z[s], ACT.Abs, bias=bo1[:, 0:1]).then_inc(s_fact, 1)
                    act.wait_ge(s_fsoft, m + 1)
                    nc.scalar.activation(relu_z[:, s, :], ps_z[s], ACT.Relu, bias=bo1[:, 0:1]).then_inc(s_fact, 1)
                    act.wait_ge(s_fact, m * 4 + 2)
                    nc.scalar.activation(abs_z[:, s, :], abs_z[:, s, :], ACT.Exp, scale=-1.0).then_inc(s_fact, 1)
                    act.wait_ge(s_fact, m * 4 + 4)
                    nc.scalar.activation(log_z[:, s, :], abs_z[:, s, :], ACT.Ln, bias=1.0).then_inc(s_fact, 1)
                    copy_turned(m + 1, 1 - s)
            act.wait_ge(s_ln[1], 6)
            nc.scalar.activation(ln_tmp[:, 0, :], ln_tmp[:, 1, :], ACT.Sqrt, bias=eps_col[:, 0:1]).then_inc(s_ln_sd[1], 1)

        @block.vector
        def _(dve):
            chain_sem, chain_at = None, 0

            def begin_chain(s, at=0):
                nonlocal chain_sem, chain_at
                chain_sem, chain_at = s, at

            def link(ins):
                nonlocal chain_at
                chain_at += 1
                ins.then_inc(chain_sem, 1)
                dve.wait_ge(chain_sem, chain_at)

            begin_chain(s_setup)
            dve.wait_ge(s_range_in, 16)
            link(nc.vector.tensor_reduce(range_f[:, 0, :], dst_groups, AX.X, ALU.min))
            link(nc.vector.tensor_reduce(range_f[:, 1, :], dst_groups, AX.X, ALU.max))
            link(nc.vector.tensor_scalar(range_i[:, 0, :], range_f[:, 0, :], float(N - WINDOW), None, ALU.min))
            link(nc.vector.tensor_tensor(range_i[:, 1, :], range_f[:, 1, :], range_i[:, 0, :], ALU.subtract))
            dve.wait_ge(s_edges_in, 64)
            link(nc.vector.scalar_tensor_tensor(out=msg_idx[:, :], in0=src_idx[:, :], scalar=float(T), in1=type_tiles,
                                                op0=ALU.mult, op1=ALU.add))
            dve.wait_ge(s_range_back, 48)
            link(nc.vector.tensor_tensor(dst_local[:, 0:TILES].rearrange("p (g t) -> p g t", t=GROUP_TILES),
                                         dst_tiles[:, 0:TILES].rearrange("p (g t) -> p g t", t=GROUP_TILES),
                                         base_bc[:, :].unsqueeze(2).broadcast_to([P, GROUPS, GROUP_TILES]),
                                         ALU.subtract))
            full, rest = divmod(E, P)
            if rest:
                link(nc.vector.memset(dst_local[rest:P, full:full + 1], -1.0))
            link(nc.vector.memset(dst_local[:, -(-E // P):COLS], -1.0))
            link(nc.vector.tensor_reduce(flag_f[:, :], span_bc[:, :], AX.X, ALU.max))
            link(nc.vector.tensor_scalar(flag_i[:, :], flag_f[:, :], float(WINDOW), None, ALU.is_ge))
            dve.wait_ge(s_iota, 2)
            link(nc.vector.tensor_copy(iota_f[:, :], iota_i))
            link(nc.vector.tensor_copy(part_f[:, :], part_i[:, :]))
            link(nc.vector.tensor_scalar(ident[:, :], iota_f[:, 0:P], part_f[:, 0:1], None, ALU.is_equal))
            link(nc.vector.memset(eps_col[:, :], EPS))
            link(nc.vector.memset(half_col[:, :], 0.5))
            link(nc.vector.memset(ones_rows[:, :], 1.0))
            link(nc.vector.tensor_scalar(trash_row[:, :], part_f[:, :], float(NPAD), None, ALU.add))
            link(nc.vector.memset(base_row[0:1, GROUPS:GROUPS + 4], 0))
            dve.wait_ge(s_const_in, 18 * 16)
            begin_chain(s_bias_split)
            link(nc.vector.tensor_copy(bf2_parts[0:1, 0, :], bf2[:, :]))
            link(nc.vector.tensor_tensor(bf2_f[0:1, 1, :], bf2[:, :], bf2_parts[0:1, 0, :], ALU.subtract))
            link(nc.vector.tensor_copy(bf2_parts[0:1, 1, :], bf2_f[0:1, 1, :]))
            link(nc.vector.tensor_tensor(bf2_f[0:1, 2, :], bf2_f[0:1, 1, :], bf2_parts[0:1, 1, :], ALU.subtract))
            link(nc.vector.tensor_copy(bf2_parts[0:1, 2, :], bf2_f[0:1, 2, :]))
            flag = nc.vector.value_load(flag_i[0:1, 0:1], min_val=0, max_val=1)

            def batch_norm(rnd, feat):
                begin_chain(s_bn[rnd])
                for c in range(N // BN_CHUNK):
                    nc.vector.bn_stats(bn_raw[:, c, :], feat[:, c * BN_CHUNK:(c + 1) * BN_CHUNK]).then_inc(s_bn[rnd], 1)
                begin_chain(s_bn[rnd], N // BN_CHUNK)
                dve.wait_ge(s_bn[rnd], N // BN_CHUNK)
                link(nc.vector.bn_aggr(bn_mv[:, :], bn_raw[:, :, :].rearrange("p c s -> p (c s)")))
                dve.wait_ge(s_bn_sd[rnd], 1)
                link(nc.vector.reciprocal(bn_tmp[:, 1:2], bn_tmp[:, 0:1]))
                link(nc.vector.tensor_tensor(bn_scale[:, :], gamma[rnd][:, :], bn_tmp[:, 1:2], ALU.mult))
                link(nc.vector.tensor_tensor(bn_tmp[:, 1:2], bn_scale[:, :], bn_mv[:, 0:1], ALU.mult))
                link(nc.vector.tensor_tensor(bn_shift[:, :], beta[rnd][:, :], bn_tmp[:, 1:2], ALU.subtract))

            def message_rows(rnd):
                with dve.Fori(0, TRANS_ITERS) as r:
                    for j in range(BODY):
                        dve.wait_ge(s_mm_done[rnd], r * BODY + (j + 1 + SLOT2))
                        dve.wait_ge(s_row_out[rnd][j % SLOTS], r * (16 * BODY // SLOTS) + 16 * (j // SLOTS + 1))
                        nc.vector.tensor_tensor(out_rows[:, j % SLOTS, :], ps_a[j % 2][:, 0:TD], b_types[rnd][:, :],
                                                ALU.add).then_inc(s_row_ready[rnd], 1)

            def stage_indices(p, it, h):
                rows = msg_idx if p < 2 else uniq_idx
                nc.vector.tensor_copy(idx_stage[:, h, :],
                                      rows[:, ds(it * ITER_TILES + h * HALF_TILES, HALF_TILES)]
                                      ).then_inc(s_idx[p], 1)

            def build_onehot(p, it, h):
                shape = [P, HALF_TILES, WINDOW]
                nc.vector.tensor_tensor(
                    onehot[:, h, :, :], iota_f[:, 0:WINDOW].unsqueeze(1).broadcast_to(shape),
                    dst_local[:, ds(it * ITER_TILES + h * HALF_TILES, HALF_TILES)].unsqueeze(2).broadcast_to(shape),
                    ALU.is_equal).then_inc(s_onehot[p], 1)

            def same_source(it, h, signal):
                shape = [P, HALF_TILES, P]
                nc.vector.tensor_tensor(
                    same_src[:, h, :, :], src_bc[:, h, :].rearrange("p (t n) -> p t n", t=HALF_TILES),
                    src_idx[:, ds(it * ITER_TILES + h * HALF_TILES, HALF_TILES)].unsqueeze(2).broadcast_to(shape),
                    ALU.is_equal).then_inc(signal, 1)

            def output_rows(r, h):
                k = r * 2 + h
                src = src_idx[:, ds(r * ITER_TILES + h * HALF_TILES, HALF_TILES)]
                nc.vector.tensor_scalar(to_trash, src, -1.0, trash_row[:, 0:1], ALU.mult, ALU.add).then_inc(s_uniq, 1)
                dve.wait_ge(s_first, k + 1)
                dve.wait_ge(s_uniq, k * 3 + 2)
                nc.vector.scalar_tensor_tensor(out=to_trash, in0=ps_first, scalar=first_w[:, 1:2], in1=to_trash,
                                               op0=ALU.is_ge, op1=ALU.mult).then_inc(s_uniq, 1)
                dve.wait_ge(s_uniq, k * 3 + 3)
                nc.vector.tensor_tensor(uniq_idx[:, ds(r * ITER_TILES + h * HALF_TILES, HALF_TILES)], src, to_trash,
                                        ALU.add).then_inc(s_uniq, 1)
                dve.wait_ge(s_uniq, k * 3 + 4)

            def accumulate(p, acc, r, h, bases):
                for j in range(2):
                    g = r * 4 + (2 * h + j)
                    dve.wait_ge(s_agg[p], g + 1)
                    dve.wait_ge(s_acc[p], g + SLOT2)
                    at = acc[:, ds(bases[2 * h + j], WINDOW)]
                    nc.vector.tensor_tensor(at, at, ps_agg[j], ALU.add).then_inc(s_acc[p], 1)

            def beyond_window(p, acc, r, h):
                with dve.If(flag > 0):
                    for j in range(2):
                        g = r * 4 + (2 * h + j)
                        cols = dst_local[:, ds(g * GROUP_TILES, GROUP_TILES)]
                        nc.vector.drain()
                        nc.vector.tensor_tensor(x_rem[:, :], cols,
                                                base_bc[:, ds(g, 1)].broadcast_to([P, GROUP_TILES]), ALU.add)
                        nc.vector.drain()
                        nc.vector.tensor_scalar(x_rem[:, :], x_rem[:, :], 1.0, None, ALU.add)
                        nc.vector.drain()
                        nc.vector.scalar_tensor_tensor(out=x_rem[:, :], in0=cols, scalar=float(WINDOW),
                                                       in1=x_rem[:, :], op0=ALU.is_ge, op1=ALU.mult)
                        nc.vector.drain()
                        nc.vector.tensor_scalar(x_rem[:, :], x_rem[:, :], -1.0, None, ALU.add)
                        with dve.Fori(0, WIDE_STEPS) as b:
                            step = g * WIDE_STEPS + b
                            nc.vector.drain()
                            for t in range(GROUP_TILES):
                                last = nc.vector.tensor_scalar(x_onehot[:, t, :], iota_f[:, :], x_rem[:, t:t + 1],
                                                               None, ALU.is_equal)
                            last.then_inc(s_xoh[p], 1)
                            nc.vector.drain()
                            nc.vector.tensor_scalar(x_rem[:, :], x_rem[:, :], float(-WIDE), None, ALU.add)
                            dve.wait_ge(s_xagg[p], step + 1)
                            at = acc[:, ds(b * WIDE, WIDE)]
                            nc.vector.tensor_tensor(at, at, ps_extra[:, :], ALU.add)
                        nc.vector.drain()

            def load_bases(r):
                return nc.values_load_multi_w_load_instructions(
                    base_row[0:1, ds(r * 4, 4)], engines=[mybir.EngineType.DVE], min_val=0, max_val=N - WINDOW,
                    skip_runtime_bounds_check_because="computed as a minimum with N - WINDOW")[1]

            def round_pass(p, acc):
                dve.wait_ge(s_clear[p], 1)
                for h in range(2):
                    stage_indices(p, 0, h)
                build_onehot(p, 0, 0)
                with dve.Fori(0, ITERS) as r:
                    bases = load_bases(r)
                    for h in range(2):
                        build_onehot(p, r + h, 1 - h)
                        if p == 1:
                            dve.wait_ge(s_src_in[h], r * 16 + 16)
                            same_source(r, h, s_dup)
                        accumulate(p, acc, r, h, bases)
                        beyond_window(p, acc, r, h)
                        if p == 1:
                            output_rows(r, h)
                        stage_indices(p, r + 1, h)

            dve.wait_ge(s_x_in, 16)
            batch_norm(0, buf_x)
            message_rows(0)
            for q in range(SLOTS):
                dve.wait_ge(s_row_out[0][q], 16 * (BLOCKS // SLOTS + 1))
            nc.vector.memset(zeros, 0.0).then_inc(s_zero, 1)
            round_pass(0, buf_a)
            dve.wait_ge(s_acc[0], GROUPS + SLOT2)
            dve.wait_ge(s_zeroed, 16 * COPIES * (ACC_ROWS // ZERO_COLS))
            batch_norm(1, buf_a)
            message_rows(1)
            round_pass(1, buf_x)

            def layer_norm_scale(which, blocks):
                begin_chain(s_ln[which])
                me, mo = ln_raw[:, 0:blocks, 1], ln_raw[:, 0:blocks, 4]
                qe, qo = ln_raw[:, 0:blocks, 2], ln_raw[:, 0:blocks, 5]
                a, v = ln_tmp[:, 0, 0:blocks], ln_tmp[:, 1, 0:blocks]
                mean, rstd = ln_mean[:, 0:blocks], ln_rstd[:, 0:blocks]
                link(nc.vector.tensor_tensor(a, me, mo, ALU.subtract))
                link(nc.vector.tensor_tensor(mean, me, mo, ALU.add))
                link(nc.vector.tensor_tensor(v, qe, qo, ALU.add))
                link(nc.vector.scalar_tensor_tensor(out=a, in0=a, scalar=D / 4.0, in1=a, op0=ALU.mult, op1=ALU.mult))
                link(nc.vector.tensor_tensor(v, v, a, ALU.add))
                link(nc.vector.tensor_scalar(v, v, 1.0 / D, None, ALU.mult))
                dve.wait_ge(s_ln_sd[which], 1)
                link(nc.vector.reciprocal(rstd, a))
                link(nc.vector.tensor_scalar(mean, mean, 0.5, None, ALU.mult))

            with dve.Fori(0, TRANS_ITERS) as r:
                for j in range(BODY):
                    n = r * BODY + j
                    dve.wait_ge(s_tr, n + (1 + SLOT2))
                    dve.wait_ge(s_xr_in[j % SLOTS], r * (16 * BODY // SLOTS) + 16 * (j // SLOTS + 1))
                    row = buf_x[:, ds(n * P, P)]
                    nc.vector.scalar_tensor_tensor(out=row, in0=x_rows[:, j % SLOTS, :], scalar=2.0,
                                                   in1=ps_b[j % 2][:, 0:P], op0=ALU.mult, op1=ALU.add
                                                   ).then_inc(s_y, 1)
                    dve.wait_ge(s_y, n + (1 + SLOTS))
                    nc.vector.bn_stats(ln_raw[:, ds(n, 1), :].rearrange("p o s -> p (o s)"), row).then_inc(s_yst, 1)
            dve.wait_ge(s_yst, BLOCKS)
            layer_norm_scale(0, BLOCKS)
            with dve.Fori(0, TRANS_ITERS) as r:
                for j in range(BODY):
                    n = r * BODY + j
                    row = buf_x[:, ds(n * P, P)]
                    dve.wait_ge(s_x1t, n + 1)
                    dve.wait_ge(s_x1b, n + 1)
                    nc.vector.tensor_scalar(h_stage[:, j % 2, :], row, ln_mean[:, ds(n, 1)], ln_rstd[:, ds(n, 1)],
                                            ALU.subtract, ALU.mult).then_inc(s_x1, 1)
                    dve.wait_ge(s_x1, n + 1)
                    nc.vector.tensor_tensor(row, h_stage[:, j % 2, :], bo2_bc[:, :], ALU.add).then_inc(s_x1b, 1)
                    dve.wait_ge(s_hmm, n + (1 + SLOT2))
                    dve.wait_ge(s_hout[j % SLOTS], r * (16 * BODY // SLOTS) + 16 * (j // SLOTS + 1))
                    nc.vector.tensor_copy(h_rows[:, j % SLOTS, :], ps_a[j % 2][:, 0:D]).then_inc(s_hrow, 1)

            def soft_half(k):
                for j in range(2):
                    dve.wait_ge(s_act, k * 6 + (6 + j))
                    nc.vector.scalar_tensor_tensor(out=soft[:, j, :], in0=ps_z[j], scalar=0.0,
                                                   in1=log_z[:, j, :], op0=ALU.max, op1=ALU.add).then_inc(s_soft, 1)

            def spread_half(it, h):
                dve.wait_ge(s_edge_in[h], it * 32 + 32)
                for j in range(2):
                    nc.vector.tensor_scalar(spread[:, h, j * WIDE:(j + 1) * WIDE], dst_bc[:, h, j * WIDE:(j + 1) * WIDE],
                                            win_node[:, ds(it * 4 + (2 * h + j), 1)], None, ALU.is_equal
                                            ).then_inc(s_spread, 1)

            def stage_cutoff(it, h):
                nc.vector.tensor_copy(cut_stage[:, h, :],
                                      cutoff[:, ds(it * ITER_TILES + h * HALF_TILES, HALF_TILES)]).then_inc(s_cut, 1)

            def spread_beyond(r, h):
                with dve.If(flag > 0):
                    with dve.Fori(0, 2) as j:
                        g = r * 4 + 2 * h + j
                        dst = dst_bc[:, h, ds(j * WIDE, WIDE)]
                        nc.vector.drain()
                        nc.vector.tensor_scalar(x_rem[:, 0:1], base_bc[:, ds(g, 1)], float(WINDOW), None, ALU.add)
                        nc.vector.tensor_scalar(x_onehot[:, 0, :], dst, 1.0, None, ALU.add)
                        nc.vector.drain()
                        nc.vector.scalar_tensor_tensor(out=x_dst, in0=dst, scalar=x_rem[:, 0:1], in1=x_onehot[:, 0, :],
                                                       op0=ALU.is_ge, op1=ALU.mult)
                        nc.vector.drain()
                        nc.vector.tensor_scalar(x_dst, x_dst, -1.0, None, ALU.add)
                        with dve.Fori(0, BLOCKS) as b:
                            step = g * BLOCKS + b
                            nc.vector.drain()
                            nc.vector.tensor_scalar(x_onehot[:, 0, :], x_dst, part_f[:, 0:1], None,
                                                    ALU.is_equal).then_inc(s_xoh[2], 1)
                            nc.vector.drain()
                            nc.vector.tensor_scalar(x_dst, x_dst, float(-P), None, ALU.add)
                            dve.wait_ge(s_xagg[2], step + 2)
                            at = h_edge[:, ds(j, 1), :].rearrange("p o n -> p (o n)")
                            nc.vector.tensor_tensor(at, at, ps_c[0][:, :], ALU.add).then_inc(s_xadd, 1)
                    nc.vector.drain()

            def convolution_step(r, first):
                for h in range(2):
                    k = r * 2 + h
                    spread_half(r + h, 1 - h)
                    dve.wait_ge(s_comb, k * 2 + SLOT2)
                    same_source(r + h, 1 - h, s_same)
                    dve.wait_ge(s_hcopy, k * 2 + (2 + SLOT2))
                    stage_cutoff(r + h, 1 - h)
                    spread_beyond(r, h)
                    dve.wait_ge(s_cut, k + 4)
                    for j in range(2):
                        dve.wait_ge(s_w, k * 2 + (j + 1))
                        for t in range(GROUP_TILES):
                            tile = slice(t * D, (t + 1) * D)
                            last = nc.vector.scalar_tensor_tensor(
                                out=msg[:, j, tile], in0=ps_w[j][:, tile],
                                scalar=cut_stage[:, h, j * GROUP_TILES + t:j * GROUP_TILES + t + 1],
                                in1=h_edge[:, j, tile], op0=ALU.mult, op1=ALU.mult)
                        last.then_inc(s_msg, 1)
                    if not first:
                        for j in range(2):
                            dve.wait_ge(s_scat[h][j], r * 64)
                    stage_indices(2, r, h)
                    soft_half(k + 1)

            nc.vector.memset(win_node[:, GROUPS:GROUPS + 4], -1.0).then_inc(s_cut, 1)
            nc.vector.tensor_scalar(win_node[:, 0:GROUPS], base_bc[:, :], part_f[:, 0:1], None, ALU.add).then_inc(s_cut, 1)
            nc.vector.memset(f_sb[RBF:RBF + 1, :, :, :], 1.0).then_inc(s_cut, 1)
            stage_cutoff(0, 0)
            dve.wait_ge(s_cut, 4)
            spread_half(0, 0)
            same_source(0, 0, s_same)
            soft_half(0)
            convolution_step(0, True)
            with dve.Fori(1, ITERS) as r:
                convolution_step(r, False)

            def sum_copies(m, s):
                half = COPIES
                step = 0
                while half > 1:
                    half //= 2
                    step += 1
                    if step > 1:
                        dve.wait_ge(s_cp_sum, m * SUM_STEPS + (step - 1))
                    nc.vector.tensor_tensor(copy_rows[:, s, 0:half, :], copy_rows[:, s, 0:half, :],
                                            copy_rows[:, s, half:2 * half, :], ALU.add).then_inc(s_cp_sum, 1)

            dve.wait_ge(s_cp_in[0], 16 * COPIES)
            sum_copies(0, 0)
            with dve.Fori(0, CHUNKS // 2) as r:
                for s in range(2):
                    m = r * 2 + s
                    dve.wait_ge(s_cp_in[1 - s], (r + s) * (16 * COPIES) + 16 * COPIES)
                    sum_copies(m + 1, 1 - s)
                    dve.wait_ge(s_fact, m * 4 + 5)
                    nc.vector.scalar_tensor_tensor(out=soft[:, s, :], in0=log_z[:, s, :], scalar=-LOG2,
                                                   in1=relu_z[:, s, :], op0=ALU.add, op1=ALU.add).then_inc(s_fsoft, 1)
                    dve.wait_ge(s_fo, m + 1)
                    rows = buf_x[:, ds(m * WIDE, WIDE)]
                    nc.vector.tensor_tensor(rows, rows, ps_w[s], ALU.add).then_inc(s_fy, 1)
                    dve.wait_ge(s_fy, m + 1)
                    for b in range(4):
                        nc.vector.bn_stats(ln_raw[:, ds(m * 4 + b, 1), :].rearrange("p o s -> p (o s)"),
                                           buf_x[:, ds(m * WIDE + b * P, P)]).then_inc(s_fst, 1)
            dve.wait_ge(s_fst, 4 * CHUNKS)
            layer_norm_scale(1, 4 * CHUNKS)
            with dve.Fori(0, CHUNKS // 2) as r:
                for s in range(2):
                    m = r * 2 + s
                    dve.wait_ge(s_fin_out[s], r * 16 + 16)
                    for b in range(4):
                        last = nc.vector.tensor_scalar(msg[:, s, b * P:(b + 1) * P], buf_x[:, ds(m * WIDE + b * P, P)],
                                                       ln_mean[:, ds(m * 4 + b, 1)], ln_rstd[:, ds(m * 4 + b, 1)],
                                                       ALU.subtract, ALU.mult)
                    last.then_inc(s_fin, 1)

        @block.tensor
        def _(pe):
            for rnd in range(2):
                pe.sem_inc(s_mm_done[rnd], SLOT2)
                pe.sem_inc(s_row_ready[rnd], SLOT2)
                for q in range(SLOTS):
                    pe.sem_inc(s_row_out[rnd][q], 16)
            for p in range(2):
                pe.sem_inc(s_acc[p], SLOT2)
            for q in range(SLOTS):
                pe.sem_inc(s_hout[q], 16)
            pe.sem_inc(s_y, SLOTS)
            for s in (s_tr, s_x1t, s_hmm, s_hrow, s_soft, s_fsoft, s_msg, s_hcopy, s_comb_out, s_comb, s_fz):
                pe.sem_inc(s, SLOT2)
            for s in (s_x1b, s_act, s_fact):
                pe.sem_inc(s, 1)
            for s in s_fin_out:
                pe.sem_inc(s, 16)
            for s in (s_xagg[2], s_xadd, s_uniq):
                pe.sem_inc(s, 1)
            pe.sem_inc(s_cp_out, SLOT2)
            pe.wait_ge(s_const_in, 18 * 16)
            pe.wait_ge(s_setup, 17)
            pe.wait_ge(s_parts_in, 48)

            def load_flag():
                return nc.tensor.value_load(flag_i[0:1, 0:1], min_val=0, max_val=1)

            flag = load_flag()

            def transform(rnd):
                with pe.Fori(0, TRANS_ITERS) as r:
                    for j in range(BODY):
                        n = r * BODY + j
                        pe.wait_ge(s_h_ready[rnd], n + 1)
                        pe.wait_ge(s_row_ready[rnd], n + 1)
                        nc.tensor.matmul(ps_a[j % 2][:, 0:WIDE], h_stage[:, j % 2, :], w_types[rnd][:, 0:WIDE],
                                         start=True, stop=True)
                        nc.tensor.matmul(ps_a[j % 2][:, WIDE:TD], h_stage[:, j % 2, :], w_types[rnd][:, WIDE:TD],
                                         start=True, stop=True).then_inc(s_mm_done[rnd], 1)

            def aggregate(p, r, h):
                for j in range(2):
                    g = r * 4 + (2 * h + j)
                    pe.wait_ge(s_gather[p][h][j], r * (16 * GROUP_TILES) + 16 * GROUP_TILES)
                    pe.wait_ge(s_onehot[p], r * 2 + (h + 1))
                    pe.wait_ge(s_acc[p], g + 1)
                    for t in range(GROUP_TILES):
                        last = nc.tensor.matmul(ps_agg[j], gathered[:, h, j * GROUP_TILES + t, :], onehot[:, h, j * GROUP_TILES + t, :],
                                                start=(t == 0), stop=(t == GROUP_TILES - 1))
                    last.then_inc(s_agg[p], 1)
                with pe.If(flag > 0):
                    for j in range(2):
                        g = r * 4 + (2 * h + j)
                        with pe.Fori(0, WIDE_STEPS) as b:
                            pe.wait_ge(s_xoh[p], g * WIDE_STEPS + b + 1)
                            for t in range(GROUP_TILES):
                                last = nc.tensor.matmul(ps_extra[:, :], gathered[:, h, j * GROUP_TILES + t, :], x_onehot[:, t, :],
                                                        start=(t == 0), stop=(t == GROUP_TILES - 1))
                            last.then_inc(s_xagg[p], 1)

            def first_of_source(k, h):
                pe.wait_ge(s_dup, k + 1)
                pe.wait_ge(s_uniq, k * 3 + 1)
                for t in range(HALF_TILES):
                    last = nc.tensor.matmul(ps_first[:, t:t + 1], same_src[:, h, t, :], first_w[:, 0:1], start=True,
                                            stop=True)
                last.then_inc(s_first, 1)

            for rnd in range(2):
                transform(rnd)
                with pe.Fori(0, ITERS) as r:
                    for h in range(2):
                        aggregate(rnd, r, h)
                        if rnd == 1:
                            first_of_source(r * 2 + h, h)

            with pe.Fori(0, TRANS_ITERS) as r:
                for j in range(BODY):
                    n = r * BODY + j
                    pe.wait_ge(s_cp, n + 1)
                    pe.wait_ge(s_y, n + (SLOTS - 1))
                    nc.tensor.transpose(ps_b[j % 2][:, 0:P], h_stage[:, j % 2, :], ident[:, :]).then_inc(s_tr, 1)
            with pe.Fori(0, TRANS_ITERS) as r:
                for j in range(BODY):
                    n = r * BODY + j
                    pe.wait_ge(s_x1, n + 1)
                    nc.tensor.transpose(ps_b[2 + j % 2][:, 0:P], h_stage[:, j % 2, :], ident[:, :]).then_inc(s_x1t, 1)
                    pe.wait_ge(s_x1c, n + 1)
                    pe.wait_ge(s_hrow, n + 1)
                    nc.tensor.matmul(ps_a[j % 2][:, 0:D], t_stage[:, j % 2, :], w_in[:, :], start=True,
                                     stop=True).then_inc(s_hmm, 1)

            def filter_in(k, h, f_count):
                for j in range(2):
                    pe.wait_ge(s_f_in[h], f_count)
                    pe.wait_ge(s_soft, k * 2 + (j - 1 + SLOT2))
                    nc.tensor.matmul(ps_z[j], wf1[:, :], f_sb[:, h, j, :], start=True, stop=True).then_inc(s_z, 1)

            pe.wait_ge(s_cut, 3)
            filter_in(0, 0, 16)
            with pe.Fori(0, ITERS) as r:
                for h in range(2):
                    k = r * 2 + h
                    for j in range(2):
                        pe.wait_ge(s_win_in[h], r * 32 + 32)
                        pe.wait_ge(s_spread, k * 2 + (j + 1))
                        pe.wait_ge(s_hcopy, k * 2 + (j + 1))
                        for t in range(GROUP_TILES):
                            tile = slice(t * P, (t + 1) * P)
                            last = nc.tensor.matmul(ps_h[j][:, tile], spread[:, h, j * WIDE + t * P:j * WIDE + (t + 1) * P],
                                                    h_win[:, h, j, :], start=True, stop=True)
                        last.then_inc(s_hexp, 1)
                    with pe.If(flag > 0):
                        with pe.Fori(0, 2) as j:
                            with pe.Fori(0, BLOCKS) as b:
                                step = (k * 2 + j) * BLOCKS + b
                                pe.wait_ge(s_comb_out, k * 2 + SLOT2)
                                pe.wait_ge(s_xh_in, step * 16 + 16)
                                pe.wait_ge(s_xoh[2], step + 1)
                                pe.wait_ge(s_xadd, step + 1)
                                for t in range(GROUP_TILES):
                                    tile = slice(t * P, (t + 1) * P)
                                    last = nc.tensor.matmul(ps_c[0][:, tile], x_onehot[:, 0, tile], x_h, start=True,
                                                            stop=True)
                                last.then_inc(s_xagg[2], 1)
                    filter_in(k + 1, 1 - h, (r + h) * 16 + 16)
                    for j in range(2):
                        pe.wait_ge(s_soft, k * 2 + (j + 1 + SLOT2))
                        nc.tensor.matmul(ps_w[j], ones_rows[:, :],
                                         bf2_rows[:, :].unsqueeze(1).broadcast_to([3, GROUP_TILES, D]),
                                         start=True, stop=False)
                        for t in range(GROUP_TILES):
                            last = nc.tensor.matmul(ps_w[j][:, t * D:(t + 1) * D], soft[:, j, t * P:(t + 1) * P],
                                                    wf2[:, :], start=False, stop=(t == GROUP_TILES - 1))
                        last.then_inc(s_w, 1)
                    for j in range(2):
                        pe.wait_ge(s_msg, k * 2 + (j + 1 + SLOT2))
                        pe.wait_ge(s_same, k + 1)
                        pe.wait_ge(s_comb_out, k * 2 + (j + 1))
                        for t in range(GROUP_TILES):
                            last = nc.tensor.matmul(ps_c[j][:, t * D:(t + 1) * D], same_src[:, h, j * GROUP_TILES + t, :],
                                                    msg[:, j, t * D:(t + 1) * D], start=True, stop=True)
                        last.then_inc(s_comb, 1)

            def turn_sums(m, s):
                pe.wait_ge(s_cp_sum, m * SUM_STEPS + SUM_STEPS)
                pe.wait_ge(s_cp_out, m + 1)
                for b in range(4):
                    last = nc.tensor.transpose(ps_b[s][:, b * P:(b + 1) * P], copy_rows[:, s, 0, b * P:(b + 1) * P],
                                               ident[:, :])
                last.then_inc(s_cp_t, 1)

            turn_sums(0, 0)
            with pe.Fori(0, CHUNKS // 2) as r:
                for s in range(2):
                    m = r * 2 + s
                    pe.wait_ge(s_cp_out, m + (1 + SLOT2))
                    nc.tensor.matmul(ps_z[s], wo1[:, :], out_t[:, s, :], start=True, stop=True).then_inc(s_fz, 1)
                    turn_sums(m + 1, 1 - s)
                    pe.wait_ge(s_fsoft, m + (1 + SLOT2))
                    for t in range(4):
                        last = nc.tensor.matmul(ps_w[s][:, t * D:(t + 1) * D], soft[:, s, t * P:(t + 1) * P], wo2[:, :],
                                                start=True, stop=True)
                    last.then_inc(s_fo, 1)


def kernel(**inputs):
    import concourse.bacc as bacc
    from concourse.bass_utils import run_bass_kernel_spmd

    def tiles(name, padding=0):
        a = np.asarray(inputs[name]).reshape(E)
        return np.ascontiguousarray(np.pad(a, (0, COLS * P - E), constant_values=padding).reshape(COLS, P).T)

    def row(a, **padding):
        return np.pad(a, (0, HALVES * COLS_HALF - E), **padding).reshape(1, HALVES * COLS_HALF)

    x = np.pad(np.asarray(inputs["x"]), ((0, NPAD - N), (0, 0)))
    dst = np.asarray(inputs["dst"])
    attr = np.pad(np.asarray(inputs["edge_attr3_1x32"]).reshape(E, RBF), ((0, HALVES * 2 * GROUP_EDGES - E), (0, 0)))
    arrays = {
        "x": x,
        "xT": np.ascontiguousarray(x.T),
        "src": tiles("src", NPAD - 1), "dst": tiles("dst"), "etype": tiles("edge_type_5"), "cutoff": tiles("edge_weight1"),
        "dst_groups": np.pad(dst, (0, GROUPS * GROUP_EDGES - E), mode="edge").reshape(RANGE_PARTS, 4 * GROUP_EDGES),
        "dst_row": row(dst, mode="edge"),
        "src_row": row(np.asarray(inputs["src"]), constant_values=NPAD - 1),
        "first_w": np.array([[3.0 ** (P // 2 - p), 2 * 3.0 ** (P // 2 - p)] for p in range(P)], np.float32),
        "attr": np.ascontiguousarray(attr.reshape(HALVES, 2, GROUP_EDGES, RBF).transpose(0, 1, 3, 2)
                                     ).reshape(HALVES * 2 * RBF, GROUP_EDGES),
    }
    for i in (1, 2):
        arrays[f"w{i}T"] = np.ascontiguousarray(np.asarray(inputs[f"L0_gnn_w{i}"]).T)
        arrays[f"b{i}"] = np.asarray(inputs[f"L0_gnn_b{i}"]).reshape(1, TD)
        arrays[f"g{i}"] = np.asarray(inputs[f"L0_gnn_g{i}"]).reshape(D, 1)
        arrays[f"be{i}"] = np.asarray(inputs[f"L0_gnn_be{i}"]).reshape(D, 1)
    for name in ("W_in", "Wf1", "Wf2", "Wo1", "Wo2"):
        arrays[name] = np.asarray(inputs[f"L1_gnn_{name}"])
    for name, shape in (("bf1", (1, D)), ("bo1", (D, 1)), ("bf2", (1, D)), ("bo2", (1, D))):
        arrays[name] = np.asarray(inputs[f"L1_gnn_{name}"]).reshape(shape)

    nc = bacc.Bacc("TRN2", target_bir_lowering=False, num_devices=1)
    dram = {n: nc.dram_tensor(f"in_{n}", a.shape, mybir.dt.from_np(a.dtype), kind="ExternalInput").ap()
            for n, a in arrays.items()}
    out = nc.dram_tensor("out", (NBUF, D), mybir.dt.float32, kind="ExternalOutput").ap()
    gnn_program(nc, dram, out)
    ran = run_bass_kernel_spmd(nc, [{f"in_{n}": a for n, a in arrays.items()}], core_ids=[0])
    return ran.results[0]["out"][:N]
```

```python
import numpy as np

import concourse.bass as bass
from concourse import mybir
from contextlib import ExitStack

N, E, D, T, RBF = 12500, 200000, 128, 5, 32
EPS = 1e-5
LOG2 = 0.6931471805599453
P = 128
WINDOW = 128
GROUP_TILES = 4
GROUP_EDGES = GROUP_TILES * P
HALF_TILES = 2 * GROUP_TILES
ITER_TILES = 2 * HALF_TILES
ITERS = -(-E // (ITER_TILES * P))
TILES = ITERS * ITER_TILES
GROUPS = TILES // GROUP_TILES
COLS_HALF = HALF_TILES * P
COLS = TILES + ITER_TILES
HALVES = 2 * ITERS + 2
BLOCKS = -(-N // P)
NPAD = BLOCKS * P
WIDE = 512
COPIES = HALF_TILES
CHUNKS = 2 * -(-NPAD // (2 * WIDE))
NBUF = CHUNKS * WIDE
ACC_ROWS = NBUF + 2 * WIDE
SUM_STEPS = COPIES.bit_length() - 2
ZERO_STEPS = 14
ZERO_COLS = ACC_ROWS // ZERO_STEPS
LOOP6 = CHUNKS // 6
WIDE_STEPS = -(-N // WIDE)
BODY = 14
TRANS_ITERS = BLOCKS // BODY
SLOTS = 7
BN_CHUNK = 500
TD = T * D
RANGE_PARTS = GROUPS // GROUP_TILES
EXP_LN_SET = 6
X_PARTS = 5
X_COLS = N // X_PARTS
assert BLOCKS % BODY == 0 and X_COLS * X_PARTS == N and X_COLS % BN_CHUNK == 0 and GROUPS % 4 == 0 and BODY % SLOTS == 0


def gnn_program(nc, dram, out):
    f32, bf16, i32 = mybir.dt.float32, mybir.dt.bfloat16, mybir.dt.int32
    ALU, ACT, AX = mybir.AluOpType, mybir.ActivationFunctionType, mybir.AxisListType
    ds = bass.ds

    ctx = ExitStack()
    with ctx:
        def sb(name, shape, dt=f32):
            return ctx.enter_context(nc.sbuf_tensor(name, shape, dt))

        def pb(name, shape):
            return ctx.enter_context(nc.psum_tensor(name, shape, f32))

        def sem(name):
            return ctx.enter_context(nc.semaphore(name))

        table = [nc.dram_tensor(f"messages_{i}", (NPAD, TD), f32).ap() for i in range(2)]
        htable = nc.dram_tensor("h_in", (NBUF, D), f32).ap()
        acc_rows = [nc.dram_tensor(f"acc_{c}", (ACC_ROWS, D), f32).ap() for c in range(COPIES)]
        base_dram = nc.dram_tensor("group_base", (RANGE_PARTS, 4), i32).ap()
        span_dram = nc.dram_tensor("group_span", (RANGE_PARTS, 4), i32).ap()

        buf_x = sb("buf_x", [P, NBUF])
        buf_a = sb("buf_a", [P, NBUF])
        src_idx = sb("src_idx", [P, COLS], i32)
        msg_idx = sb("msg_idx", [P, COLS], i32)
        dst_local = sb("dst_local", [P, COLS])
        cutoff = sb("cutoff", [P, COLS])
        base_row = sb("base_row", [1, GROUPS + 4], i32)
        base_bc = sb("base_bc", [P, GROUPS], i32)
        span_bc = sb("span_bc", [P, GROUPS], i32)
        flag_f = sb("flag_f", [P, 1])
        flag_i = sb("flag_i", [P, 1], i32)
        idx_stage = sb("idx_stage", [P, 2, HALF_TILES], i32)
        gathered = sb("gathered", [P, 2, HALF_TILES, D])
        onehot = sb("onehot", [P, 2, HALF_TILES, WINDOW])
        work = sb("work", [P, 10 * WIDE])
        x_onehot = sb("x_onehot", [P, GROUP_TILES, WIDE])
        x_rem = sb("x_rem", [P, GROUP_TILES])
        h_stage = sb("h_stage", [P, 2, P])
        ones_d = sb("ones_d", [P, P])
        iota_f = sb("iota_f", [P, WIDE])
        part_i = sb("part_i", [P, 1], i32)
        part_f = sb("part_f", [P, 1])
        ident = sb("ident", [P, P])
        w_types = [sb(f"w_types_{i}", [P, TD]) for i in range(2)]
        b_types = [sb(f"b_types_{i}", [P, TD]) for i in range(2)]
        gamma = [sb(f"gamma_{i}", [P, 1]) for i in range(2)]
        beta = [sb(f"beta_{i}", [P, 1]) for i in range(2)]
        w_in = sb("w_in", [P, D])
        wf1 = sb("wf1", [RBF + 1, D])
        wf2 = sb("wf2", [P, D])
        bf2 = sb("bf2", [1, D])
        bf2_f = sb("bf2_f", [1, 3, D])
        bf2_parts = sb("bf2_parts", [1, 3, D], bf16)
        bf2_rows = sb("bf2_rows", [3, D], bf16)
        ones_rows = sb("ones_rows", [3, P], bf16)
        wo1 = sb("wo1", [P, D])
        bo1 = sb("bo1", [P, 1])
        wo2 = sb("wo2", [P, D])
        bo2 = sb("bo2", [P, 1])
        first_w = sb("first_w", [P, 2])
        trash_row = sb("trash_row", [P, 1])
        bn_raw = sb("bn_raw", [P, N // BN_CHUNK, 6])
        bn_mv = sb("bn_mv", [P, 2])
        bn_scale = sb("bn_scale", [P, 1])
        bn_shift = sb("bn_shift", [P, 1])
        bn_tmp = sb("bn_tmp", [P, 2])
        eps_col = sb("eps_col", [P, 1])
        half_col = sb("half_col", [P, 1])
        ln_raw = sb("ln_raw", [P, CHUNKS * 4, 6])
        ln_mean = sb("ln_mean", [P, CHUNKS * 4])
        ln_rstd = sb("ln_rstd", [P, CHUNKS * 4])
        ln_shift = sb("ln_shift", [P, CHUNKS * 4])
        ln_tmp = sb("ln_tmp", [P, 2, CHUNKS * 4])

        out_rows = work[:, 0:SLOTS * TD].rearrange("p (q n) -> p q n", q=SLOTS)
        stage5 = work[:, :].rearrange("p (a j n) -> p a j n", a=5, j=2)
        abs_z, relu_z, log_z, soft, msg = (stage5[:, a] for a in range(5))
        x_in = work[:, 0:4 * WIDE].rearrange("p (q n) -> p q n", q=4)
        squares, sd, x1 = (work[:, (4 + 2 * i) * WIDE:(6 + 2 * i) * WIDE].rearrange("p (s n) -> p s n", s=2) for i in range(3))
        h_rows = buf_a[:, 8 * WIDE:10 * WIDE].rearrange("p (s n) -> p s n", s=2)
        final_rows = work[:, 6 * WIDE:10 * WIDE].rearrange("p (q n) -> p q n", q=4)
        edge_slots = [buf_a[:, i * 2 * COLS_HALF:(i + 1) * 2 * COLS_HALF].rearrange("p (h n) -> p h n", h=2) for i in range(3)]
        src_bc, dst_bc = edge_slots[0].bitcast(i32), edge_slots[1].bitcast(i32)
        same_src = edge_slots[2].rearrange("p h (t n) -> p h t n", t=HALF_TILES)
        h_edge = buf_a[:, 6144:7168].rearrange("p (j n) -> p j n", j=2)
        h_win = buf_a[:, 7168:7680].rearrange("p (h j n) -> p h j n", h=2, j=2)
        x_dst = buf_a[:, 7680:8192]
        x_h = buf_a[:, 8192:8192 + P]
        uniq_idx = buf_a[:, 8320:8320 + COLS].bitcast(i32)
        win_node = buf_a[:, 9984:9984 + GROUPS + 4]
        cut_stage = buf_a[:, 10400:10400 + 2 * HALF_TILES].rearrange("p (h t) -> p h t", h=2)
        to_trash = buf_a[:, 10432:10432 + HALF_TILES]
        f_sb = buf_a[0:RBF + 1, 10496:10496 + 4 * GROUP_EDGES].rearrange("p (h j n) -> p h j n", h=2, j=2)
        spread = onehot[:, :, :, :].rearrange("p h t n -> p h (t n)")
        combined = gathered[:, :, :, :].rearrange("p h t n -> p h (t n)")
        copy_rows = buf_a[:, 0:3 * COPIES * WIDE].rearrange("p (q c n) -> p q c n", q=3, c=COPIES)
        out_t, x_stage = (spread[:, i, :].rearrange("p (s n) -> p s n", s=2) for i in range(2))
        zeros = work[:, 0:ZERO_COLS]
        dst_groups = buf_a[0:RANGE_PARTS, 0:4 * GROUP_EDGES].bitcast(i32).rearrange("p (g n) -> p g n", g=4)
        dst_tiles = onehot[:, :, :, :].rearrange("p h t n -> p (h t n)")[:, 0:COLS].bitcast(i32)
        type_tiles = gathered[:, :, :, :].rearrange("p h t n -> p (h t n)")[:, 0:COLS].bitcast(i32)
        iota_i = x_onehot[:, 0, :].bitcast(i32)
        range_f = x_onehot[0:RANGE_PARTS, 1, 0:8].rearrange("p (a g) -> p a g", a=2)
        range_i = x_onehot[0:RANGE_PARTS, 1, 8:16].bitcast(i32).rearrange("p (a g) -> p a g", a=2)

        ps_a = [pb(f"ps_a{i}", [P, 2 * WIDE]) for i in range(2)]
        ps_b = [pb(f"ps_b{i}", [P, WIDE]) for i in range(4)]
        ps_z = [ps_a[0][:, j * WIDE:(j + 1) * WIDE] for j in range(2)]
        ps_w = [ps_a[1][:, j * WIDE:(j + 1) * WIDE] for j in range(2)]
        ps_agg = [ps_b[j][:, 0:WINDOW] for j in range(2)]
        ps_extra = ps_b[2]
        ps_first = ps_b[3][:, 0:HALF_TILES]
        ps_h, ps_c = ps_b[0:2], ps_b[2:4]
        ps_mean, ps_var, ps_rows = ps_z, ps_w, ps_b[0:2]

        s_range_in, s_edges_in, s_const_in = sem("range_in"), sem("edges_in"), sem("const_in")
        s_x_in = [sem(f"x_in_{i}") for i in range(X_PARTS)]
        s_iota, s_setup = sem("iota_made"), sem("setup_step")
        s_range_out, s_range_back = sem("range_stored"), sem("range_back")
        s_parts_in, s_bias_split = sem("bias_rows_in"), sem("bias_split")
        s_bn, s_bn_sd = [sem(f"bn_step_{i}") for i in range(2)], [sem(f"bn_sd_{i}") for i in range(2)]
        s_h_ready = [sem(f"h_ready_{i}") for i in range(2)]
        s_mm_done = [sem(f"transform_done_{i}") for i in range(2)]
        s_row_ready = [sem(f"rows_ready_{i}") for i in range(2)]
        s_row_out = [[sem(f"rows_out_{i}_{q}") for q in range(SLOTS)] for i in range(2)]
        s_clear = [sem(f"acc_cleared_{i}") for i in range(3)]
        s_turn = [sem(f"gather_turn_{i}") for i in range(3)]
        s_idx = [sem(f"idx_ready_{i}") for i in range(3)]
        s_gather = [[[sem(f"gathered_{i}_{h}_{j}") for j in range(2)] for h in range(2)] for i in range(3)]
        s_onehot = [sem(f"onehot_ready_{i}") for i in range(3)]
        s_agg = [sem(f"agg_ready_{i}") for i in range(3)]
        s_acc = [sem(f"acc_done_{i}") for i in range(3)]
        s_xoh = [sem(f"extra_onehot_{i}") for i in range(3)]
        s_xagg = [sem(f"extra_agg_{i}") for i in range(3)]
        s_xt_in = [sem(f"x_chunk_in_{q}") for q in range(4)]
        s_y, s_mean, s_yc, s_sq, s_var, s_sd, s_rsd = (sem(n) for n in (
            "y_done", "mean_ready", "centred", "squared", "variance_ready", "sd_done", "sd_inverted"))
        s_x1, s_x1b, s_hmm, s_hrow = sem("x1_done"), sem("x1_kept"), sem("h_done"), sem("h_rows_ready")
        s_hout = [sem(f"h_rows_out_{q}") for q in range(2)]
        s_turn_act = sem("scalar_turn")
        s_ln, s_ln_sd = sem("ln_step"), sem("ln_sd")
        s_f_in = [sem(f"filter_in_{h}") for h in range(2)]
        s_z, s_act, s_soft, s_w, s_msg = (sem(n) for n in (
            "z_ready", "act_step", "soft_done", "filter_ready", "msg_done"))
        s_cut, s_xadd = sem("cutoff_staged"), sem("extra_added")
        s_src_in, s_dup, s_first, s_uniq = [sem(f"src_in_{h}") for h in range(2)], sem("dup_ready"), sem("first_ready"), sem("uniq_step")
        s_edge_in, s_win_in = [sem(f"edge_rows_in_{h}") for h in range(2)], [sem(f"h_window_in_{h}") for h in range(2)]
        s_spread, s_same, s_hexp, s_hcopy = sem("spread_ready"), sem("same_ready"), sem("h_edges_ready"), sem("h_edges_copied")
        s_comb, s_comb_out = sem("combined_ready"), sem("combined_copied")
        s_scat = [[sem(f"scattered_{h}_{j}") for j in range(2)] for h in range(2)]
        s_go = sem("scatter_turn")
        s_xh_in = sem("extra_h_in")
        s_zero, s_zeroed = sem("zeros_made"), sem("copies_zeroed")
        s_cp_in, s_cp_sum, s_cp_t, s_cp_out = [sem(f"copies_in_{i}") for i in range(3)], sem("copies_summed"), sem("sums_turned"), sem("sums_copied")
        s_fz, s_fact, s_fsoft, s_fo, s_fy, s_fst = (sem(n) for n in (
            "out_z_ready", "out_act_step", "out_soft_done", "out_ready", "out_y_done", "out_y_stats"))
        s_fx = sem("x1_staged")
        s_fin, s_fin_out = [sem(f"final_ready_{i}") for i in range(2)], [sem(f"final_out_{q}") for q in range(4)]

        block = ctx.enter_context(nc.Block())

        SLOT2 = 2

        @block.sync
        def _(sp):
            sp.dma_start(dst_groups, dram["dst_groups"].rearrange("p (g n) -> p g n", g=4)).then_inc(s_range_in, 16)
            for i in range(X_PARTS):
                part = slice(i * X_COLS, (i + 1) * X_COLS if i < X_PARTS - 1 else NPAD)
                sp.dma_start(buf_x[:, part], dram["xT"][:, part]).then_inc(s_x_in[i], 16)
            for t, name in ((gamma[0], "g1"), (beta[0], "be1"), (w_types[0], "w1T"), (gamma[1], "g2"),
                            (beta[1], "be2"), (w_types[1], "w2T"), (w_in, "W_in"), (wf2, "Wf2"),
                            (bf2, "bf2"), (wo1, "Wo1"), (bo1, "bo1"), (wo2, "Wo2"), (first_w, "first_w"), (bo2, "bo2")):
                sp.dma_start(t[:, :], dram[name]).then_inc(s_const_in, 16)
            sp.dma_start(wf1[0:RBF, :], dram["Wf1"]).then_inc(s_const_in, 16)
            sp.dma_start(wf1[RBF:RBF + 1, :], dram["bf1"]).then_inc(s_const_in, 16)
            for t, name, n in ((b_types[0], "b1", TD), (b_types[1], "b2", TD)):
                sp.dma_start(t[:, :], dram[name].broadcast_to([P, n])).then_inc(s_const_in, 16)
            for t, name in ((type_tiles, "etype"), (src_idx[:, :], "src"), (dst_tiles, "dst"), (cutoff[:, :], "cutoff")):
                sp.dma_start(t, dram[name]).then_inc(s_edges_in, 16)
            sp.wait_ge(s_setup, 4)
            sp.dma_start(base_dram, range_i[:, 0, :]).then_inc(s_range_out, 16)
            sp.dma_start(span_dram, range_i[:, 1, :]).then_inc(s_range_out, 16)
            sp.wait_ge(s_range_out, 32)
            base_flat = base_dram.rearrange("(o p) g -> o (p g)", o=1)
            span_flat = span_dram.rearrange("(o p) g -> o (p g)", o=1)
            sp.dma_start(base_row[0:1, 0:GROUPS], base_flat).then_inc(s_range_back, 16)
            sp.dma_start(base_bc[:, :], base_flat.broadcast_to([P, GROUPS])).then_inc(s_range_back, 16)
            sp.dma_start(span_bc[:, :], span_flat.broadcast_to([P, GROUPS])).then_inc(s_range_back, 16)
            for rnd in range(2):
                with sp.Fori(0, TRANS_ITERS) as r:
                    for j in range(BODY):
                        sp.wait_ge(s_row_ready[rnd], r * BODY + (j + 1 + SLOT2))
                        sp.dma_start(table[rnd][ds((r * BODY + j) * P, P), :],
                                     out_rows[:, j % SLOTS, :]).then_inc(s_row_out[rnd][j % SLOTS], 16)

                if rnd == 0:
                    sp.wait_ge(s_bias_split, 5)
                    for i in range(3):
                        sp.dma_start(bf2_rows[i:i + 1, :], bf2_parts[0:1, i, :]).then_inc(s_parts_in, 16)
                    sp.wait_ge(s_zero, 1)
                    for c, acc in enumerate(acc_rows):
                        flat = acc.rearrange("(p x) n -> p (x n)", p=P)
                        with sp.Fori(0, ZERO_STEPS) as q:
                            sp.wait_ge(s_idx[0], q + (c * ZERO_STEPS + 1))
                            sp.dma_start(flat[:, ds(q * ZERO_COLS, ZERO_COLS)], zeros).then_inc(s_zeroed, 16)
                else:
                    sp.wait_ge(s_h_ready[1], BLOCKS)
                    sp.wait_ge(s_mm_done[1], BLOCKS + SLOT2)
                    for h in range(2):
                        sp.dma_start(src_bc[:, h, :], dram["src_row"][0:1, h * COLS_HALF:(h + 1) * COLS_HALF]
                                     .broadcast_to([P, COLS_HALF])).then_inc(s_src_in[h], 16)
                    with sp.Fori(0, ITERS) as r:
                        for h in range(2):
                            sp.wait_ge(s_dup, r * 2 + (h + 1))
                            sp.dma_start(src_bc[:, h, :],
                                         dram["src_row"][0:1, ds((r * 2 + (2 + h)) * COLS_HALF, COLS_HALF)]
                                         .broadcast_to([P, COLS_HALF])).then_inc(s_src_in[h], 16)
                    for h in range(2):
                        sp.wait_ge(s_src_in[h], 16 * (ITERS + 1))

            for q in range(SLOTS):
                sp.wait_ge(s_row_out[1][q], 16 * (BLOCKS // SLOTS + 1))

            def load_x(m, q):
                sp.dma_start(x_in[:, q, :], dram["xT"][:, ds(m * WIDE, WIDE)]).then_inc(s_xt_in[q], 16)

            def store_h(m, s):
                sp.wait_ge(s_hrow, m + (1 + SLOT2))
                sp.dma_start(htable[ds(m * WIDE, WIDE), :].rearrange("(b p) n -> p b n", p=P),
                             h_rows[:, s, :].rearrange("p (b n) -> p b n", b=4)).then_inc(s_hout[s], 16)

            for m in range(6):
                if m >= 4:
                    sp.wait_ge(s_y, m - 3)
                load_x(m, m % 4)
            full = (CHUNKS - 6) // 4
            with sp.Fori(0, full) as r:
                for j in range(4):
                    m = r * 4 + j
                    sp.wait_ge(s_y, m + 3)
                    load_x(m + 6, (j + 2) % 4)
                    store_h(m, j % 2)
            for m in range(4 * full, CHUNKS):
                store_h(m, m % 2)

            def load_attributes(h, half):
                sp.dma_start(f_sb[0:RBF, h, :, :], dram["attr"][ds(half * (2 * RBF), 2 * RBF), :]
                             .rearrange("(j r) n -> r j n", j=2)).then_inc(s_f_in[h], 16)

            def load_ends(h, half):
                for t, name in ((dst_bc, "dst_row"), (src_bc, "src_row")):
                    sp.dma_start(t[:, h, :], dram[name][0:1, ds(half * COLS_HALF, COLS_HALF)].broadcast_to([P, COLS_HALF])
                                 ).then_inc(s_edge_in[h], 16)

            def load_windows(h, bases):
                for j in range(2):
                    sp.dma_start(h_win[:, h, j, :], htable[ds(bases[j], WINDOW), :]).then_inc(s_win_in[h], 16)

            def load_bases(r):
                return nc.values_load_multi_w_load_instructions(
                    base_row[0:1, ds(r * 4, 4)], engines=[mybir.EngineType.SP], min_val=0, max_val=N - WINDOW,
                    skip_runtime_bounds_check_because="computed as a minimum with N - WINDOW")[1]

            for s in s_hout:
                sp.wait_ge(s, 16 * (CHUNKS // 2 + 1))
            bases = load_bases(0)
            flag = nc.sync.value_load(flag_i[0:1, 0:1], min_val=0, max_val=1)
            for h in range(2):
                load_attributes(h, h)
                load_ends(h, h)
                load_windows(h, bases[2 * h:2 * h + 2])
            with sp.Fori(0, ITERS) as r:
                bases = load_bases(r + 1)
                for h in range(2):
                    with sp.If(flag > 0):
                        with sp.Fori(0, 2) as j:
                            with sp.Fori(0, BLOCKS) as b:
                                step = ((r * 2 + h) * 2 + j) * BLOCKS + b
                                sp.wait_ge(s_xagg[2], step + 1)
                                sp.dma_start(x_h, htable[ds(b * P, P), :]).then_inc(s_xh_in, 16)
                    k = r * 2 + h
                    sp.wait_ge(s_z, k * 2 + 2)
                    load_attributes(h, k + 2)
                    sp.wait_ge(s_same, k + 1)
                    load_ends(h, k + 2)
                    sp.wait_ge(s_hexp, k * 2 + 2)
                    load_windows(h, bases[2 * h:2 * h + 2])
            for h in range(2):
                sp.wait_ge(s_f_in[h], 16 * (ITERS + 1))
                sp.wait_ge(s_edge_in[h], 32 * (ITERS + 1))
                sp.wait_ge(s_win_in[h], 32 * (ITERS + 1))

            def load_copies(m, q):
                for c in range(COPIES):
                    sp.dma_start(copy_rows[:, q, c, :].rearrange("p (b n) -> p b n", b=4),
                                 acc_rows[c][ds(m * WIDE, WIDE), :].rearrange("(b p) n -> p b n", p=P)
                                 ).then_inc(s_cp_in[q], 16)

            def reload_copies(m, q):
                sp.wait_ge(s_cp_t, m + 1)
                load_copies(m + 3, q)

            for h in range(2):
                for j in range(2):
                    sp.wait_ge(s_scat[h][j], 64 * ITERS)
            for q in range(3):
                load_copies(q, q)
            full = (CHUNKS - 3) // 3
            with sp.Fori(0, full) as r:
                for q in range(3):
                    reload_copies(r * 3 + q, q)
            for m in range(3 * full, CHUNKS - 3):
                reload_copies(m, m % 3)

            def store_rows(m, q, count):
                sp.wait_ge(s_fin[q % 2], count)
                sp.dma_start(out[ds(m * WIDE, WIDE), :].rearrange("(b p) n -> p b n", p=P),
                             final_rows[:, q, :].rearrange("p (b n) -> p b n", b=4)).then_inc(s_fin_out[q], 16)

            with sp.Fori(0, CHUNKS // 4) as r:
                for q in range(4):
                    store_rows(r * 4 + q, q, r * 2 + (q // 2 + 1))
            for m in range(CHUNKS // 4 * 4, CHUNKS):
                store_rows(m, m % 4, m // 2 + 1)
            for q in range(3):
                sp.wait_ge(s_cp_in[q], 16 * COPIES * len(range(q, CHUNKS, 3)))
            for q in range(4):
                sp.wait_ge(s_fin_out[q], 16 * (len(range(q, CHUNKS, 4)) + 1))

        @block.gpsimd
        def _(pool):
            nc.gpsimd.iota(iota_i, [[1, WIDE]], base=0, channel_multiplier=0).then_inc(s_iota, 1)
            nc.gpsimd.iota(part_i[:, :], [[0, 1]], base=0, channel_multiplier=1).then_inc(s_iota, 1)

            def gather_pass(p, source, last_wait):
                for s, v in last_wait:
                    pool.wait_ge(s, v)
                with pool.Fori(0, ITERS) as r:
                    for h in range(2):
                        pool.wait_ge(s_idx[p], r * 2 + (h + 1))
                        pool.sem_inc(s_turn[p], 1)
                        for t in range(HALF_TILES):
                            nc.gpsimd.indirect_dma_start(
                                gathered[:, h, t, :], None, source,
                                bass.IndirectOffsetOnAxis(ap=idx_stage[:, h, t:t + 1], axis=0),
                            ).then_inc(s_gather[p][h][t // GROUP_TILES], 16)

            pool.wait_ge(s_setup, 2)
            nc.gpsimd.memset(buf_a[:, :], 0.0).then_inc(s_clear[0], 1)
            for rnd in range(2):
                if rnd == 1:
                    pool.wait_ge(s_h_ready[0], BLOCKS)
                    nc.gpsimd.memset(buf_x[:, :], 0.0).then_inc(s_clear[1], 1)
                gather_pass(rnd, table[rnd].rearrange("n (t d) -> (n t) d", t=T),
                            [(s_row_out[rnd][q], 16 * (BLOCKS // SLOTS + 1)) for q in range(SLOTS)])
            pool.wait_ge(s_zeroed, 16 * COPIES * ZERO_STEPS)
            def scatter_sums(r, first):
                for h in range(2):
                    for j in range(2):
                        pool.wait_ge(s_idx[2], r * 2 + (h + 1))
                        pool.wait_ge(s_comb_out, r * 4 + (2 * h + j + 1 + SLOT2))
                        if h == 1 or not first:
                            pool.wait_ge(s_scat[1 - h][j], r * 64 + 64 * h)
                        pool.sem_inc(s_go, 1)
                        for t in range(j * GROUP_TILES, (j + 1) * GROUP_TILES):
                            nc.gpsimd.indirect_dma_start(
                                acc_rows[t], bass.IndirectOffsetOnAxis(ap=idx_stage[:, h, t:t + 1], axis=0),
                                gathered[:, h, t, :], None, compute_op=ALU.add,
                            ).then_inc(s_scat[h][j], 16)

            scatter_sums(0, True)
            with pool.Fori(1, ITERS) as r:
                scatter_sums(r, False)

        @block.scalar
        def _(act):
            for rnd in range(2):
                feat = buf_x if rnd == 0 else buf_a
                act.wait_ge(s_bn[rnd], 26)
                nc.scalar.activation(bn_tmp[:, 0:1], bn_mv[:, 1:2], ACT.Sqrt, bias=eps_col[:, 0:1]).then_inc(s_bn_sd[rnd], 1)
                act.wait_ge(s_bn[rnd], 30)
                with act.Fori(0, TRANS_ITERS) as r:
                    for j in range(BODY):
                        act.wait_ge(s_mm_done[rnd], r * BODY + (j + 1))
                        nc.scalar.activation(h_stage[:, j % 2, :], feat[:, ds((r * BODY + j) * P, P)], ACT.Relu,
                                             bias=bn_shift[:, 0:1], scale=bn_scale[:, 0:1]).then_inc(s_h_ready[rnd], 1)

            def square(m, s):
                act.wait_ge(s_yc, m + (1 + SLOT2))
                act.wait_ge(s_var, m + 1)
                act.sem_inc(s_turn_act, 1)
                nc.scalar.activation(squares[:, s, :], buf_x[:, ds(m * WIDE, WIDE)], ACT.Square).then_inc(s_sq, 1)

            def deviation(m, s):
                act.wait_ge(s_var, m + (1 + SLOT2))
                act.wait_ge(s_x1, m + 1)
                nc.scalar.activation(sd[:, s, :], ps_var[s], ACT.Sqrt, bias=eps_col[:, 0:1]).then_inc(s_sd, 1)

            def keep_x1(m, s):
                act.wait_ge(s_x1, m + (1 + SLOT2))
                act.sem_inc(s_turn_act, 1)
                nc.scalar.activation(buf_x[:, ds(m * WIDE, WIDE)], x1[:, s, :], ACT.Identity,
                                     bias=bo2[:, 0:1]).then_inc(s_x1b, 1)

            def copy_h(m, s, stored):
                act.wait_ge(s_hmm, m + (1 + SLOT2))
                act.wait_ge(s_hout[s], stored)
                nc.scalar.activation(h_rows[:, s, :], ps_rows[s][:, :], ACT.Copy).then_inc(s_hrow, 1)

            square(0, 0)
            deviation(0, 0)
            with act.Fori(0, CHUNKS // 4) as r:
                for j in range(4):
                    m = r * 4 + j
                    square(m + 1, (j + 1) % 2)
                    deviation(m + 1, (j + 1) % 2)
                    keep_x1(m, j % 2)
                    copy_h(m, j % 2, r * 32 + 16 * (j // 2 + 1))
            for m in range(CHUNKS // 4 * 4, CHUNKS):
                if m + 1 < CHUNKS:
                    square(m + 1, (m + 1) % 2)
                    deviation(m + 1, (m + 1) % 2)
                keep_x1(m, m % 2)
                copy_h(m, m % 2, 16 * (m // 2 + 1))

            def softplus_half(k):
                for j in range(2):
                    act.wait_ge(s_z, k * 2 + (j + 1))
                    act.wait_ge(s_act, k * 6 + 1)
                    nc.scalar.activation(abs_z[:, j, :], ps_z[j], ACT.Abs).then_inc(s_act, 1)
                for j in range(2):
                    act.wait_ge(s_act, k * 6 + (2 + j))
                    nc.scalar.activation(abs_z[:, j, :], abs_z[:, j, :], ACT.Exp, scale=-1.0).then_inc(s_act, 1)
                for j in range(2):
                    act.wait_ge(s_act, k * 6 + (4 + j))
                    act.wait_ge(s_soft, k * 2 + SLOT2)
                    nc.scalar.activation(log_z[:, j, :], abs_z[:, j, :], ACT.Ln, bias=half_col[:, 0:1],
                                         scale=0.5).then_inc(s_act, 1)

            def convolution_step(r, first):
                for h in range(2):
                    k = r * 2 + h
                    for j in range(2):
                        act.wait_ge(s_hexp, k * 2 + (j + 1))
                        act.wait_ge(s_msg, k * 2 + (j + 1))
                        nc.scalar.activation(h_edge[:, j, :], ps_h[j][:, :], ACT.Copy).then_inc(s_hcopy, 1)
                    softplus_half(k + 1)
                    for j in range(2):
                        act.wait_ge(s_comb, k * 2 + (j + 1 + SLOT2))
                        if not first:
                            act.wait_ge(s_scat[h][j], r * 64)
                        nc.scalar.activation(combined[:, h, j * WIDE:(j + 1) * WIDE], ps_c[j][:, :],
                                             ACT.Copy).then_inc(s_comb_out, 1)

            nc.scalar.add_instruction(mybir.InstLoadActFuncSet(
                name=nc.get_next_instruction_name(), engine=mybir.EngineType.Activation, act_func_set_id=EXP_LN_SET))
            softplus_half(0)
            convolution_step(0, True)
            with act.Fori(1, ITERS) as r:
                convolution_step(r, False)

            def copy_turned(m, s):
                act.wait_ge(s_cp_t, m + 1)
                act.wait_ge(s_fz, m + 1)
                nc.scalar.activation(out_t[:, s, :], ps_b[s][:, :], ACT.Copy).then_inc(s_cp_out, 1)

            def out_softplus(m, s):
                act.wait_ge(s_fz, m + (1 + SLOT2))
                act.wait_ge(s_fact, m * 4 + 1)
                nc.scalar.activation(abs_z[:, s, :], ps_z[s], ACT.Abs, bias=bo1[:, 0:1]).then_inc(s_fact, 1)
                act.wait_ge(s_fsoft, m + 1)
                nc.scalar.activation(relu_z[:, s, :], ps_z[s], ACT.Relu, bias=bo1[:, 0:1]).then_inc(s_fact, 1)
                act.wait_ge(s_fact, m * 4 + 2)
                nc.scalar.activation(abs_z[:, s, :], abs_z[:, s, :], ACT.Exp, scale=-1.0).then_inc(s_fact, 1)
                act.wait_ge(s_fact, m * 4 + 4)
                nc.scalar.activation(log_z[:, s, :], abs_z[:, s, :], ACT.Ln, bias=half_col[:, 0:1],
                                     scale=0.5).then_inc(s_fact, 1)

            def stage_x1(m, s):
                act.wait_ge(s_fo, m + 1)
                act.sem_inc(s_turn_act, 1)
                nc.scalar.activation(x_stage[:, s, :], buf_x[:, ds(m * WIDE, WIDE)], ACT.Copy).then_inc(s_fx, 1)

            def copy_y(m, s):
                act.wait_ge(s_fo, m + (1 + SLOT2))
                act.sem_inc(s_turn_act, 1)
                nc.scalar.activation(buf_x[:, ds(m * WIDE, WIDE)], ps_w[s], ACT.Copy).then_inc(s_fy, 1)

            def output_step(m, j):
                s = j % 2
                if j + 1 < CHUNKS:
                    out_softplus(m + 1, 1 - s)
                    stage_x1(m + 1, 1 - s)
                copy_y(m, s)
                if j + 2 < CHUNKS:
                    copy_turned(m + 2, s)

            for m in range(2):
                copy_turned(m, m)
            out_softplus(0, 0)
            stage_x1(0, 0)
            with act.Fori(0, LOOP6) as r:
                for j in range(6):
                    output_step(r * 6 + j, j)
            for m in range(6 * LOOP6, CHUNKS):
                output_step(m, m)
            act.wait_ge(s_ln, 6)
            nc.scalar.activation(ln_tmp[:, 0, :], ln_tmp[:, 1, :], ACT.Sqrt, bias=eps_col[:, 0:1]).then_inc(s_ln_sd, 1)

            def normalise(m, q, stored):
                act.wait_ge(s_fin_out[q], stored)
                act.sem_inc(s_turn_act, 1)
                for b in range(4):
                    last = nc.scalar.activation(final_rows[:, q, b * P:(b + 1) * P], buf_x[:, ds(m * WIDE + b * P, P)],
                                                ACT.Identity, bias=ln_shift[:, ds(m * 4 + b, 1)],
                                                scale=ln_rstd[:, ds(m * 4 + b, 1)])
                last.then_inc(s_fin[1], 1)

            act.wait_ge(s_ln, 9)
            with act.Fori(0, CHUNKS // 4) as r:
                for q in (1, 3):
                    normalise(r * 4 + q, q, r * 16 + 16)
            for m in range(CHUNKS // 4 * 4 + 1, CHUNKS, 2):
                normalise(m, m % 4, 16 * (m // 4 + 1))

        @block.vector
        def _(dve):
            chain_sem, chain_at = None, 0

            def begin_chain(s, at=0):
                nonlocal chain_sem, chain_at
                chain_sem, chain_at = s, at

            def link(ins):
                nonlocal chain_at
                chain_at += 1
                ins.then_inc(chain_sem, 1)
                dve.wait_ge(chain_sem, chain_at)

            begin_chain(s_setup)
            dve.wait_ge(s_range_in, 16)
            link(nc.vector.tensor_reduce(range_f[:, 0, :], dst_groups, AX.X, ALU.min))
            link(nc.vector.tensor_reduce(range_f[:, 1, :], dst_groups, AX.X, ALU.max))
            link(nc.vector.tensor_scalar(range_i[:, 0, :], range_f[:, 0, :], float(N - WINDOW), None, ALU.min))
            link(nc.vector.tensor_tensor(range_i[:, 1, :], range_f[:, 1, :], range_i[:, 0, :], ALU.subtract))
            link(nc.vector.memset(eps_col[:, :], EPS))

            def set_up():
                begin_chain(s_setup, 5)
                dve.wait_ge(s_edges_in, 64)
                link(nc.vector.scalar_tensor_tensor(out=msg_idx[:, :], in0=src_idx[:, :], scalar=float(T), in1=type_tiles,
                                                    op0=ALU.mult, op1=ALU.add))
                for h in range(2):
                    stage_indices(0, 0, h)
                dve.wait_ge(s_range_back, 48)
                link(nc.vector.tensor_tensor(dst_local[:, 0:TILES].rearrange("p (g t) -> p g t", t=GROUP_TILES),
                                             dst_tiles[:, 0:TILES].rearrange("p (g t) -> p g t", t=GROUP_TILES),
                                             base_bc[:, :].unsqueeze(2).broadcast_to([P, GROUPS, GROUP_TILES]),
                                             ALU.subtract))
                full, rest = divmod(E, P)
                if rest:
                    link(nc.vector.memset(dst_local[rest:P, full:full + 1], -1.0))
                link(nc.vector.memset(dst_local[:, -(-E // P):COLS], -1.0))
                link(nc.vector.tensor_reduce(flag_f[:, :], span_bc[:, :], AX.X, ALU.max))
                link(nc.vector.tensor_scalar(flag_i[:, :], flag_f[:, :], float(WINDOW), None, ALU.is_ge))
                dve.wait_ge(s_iota, 2)
                link(nc.vector.tensor_copy(iota_f[:, :], iota_i))
                link(nc.vector.tensor_copy(part_f[:, :], part_i[:, :]))
                link(nc.vector.tensor_scalar(ident[:, :], iota_f[:, 0:P], part_f[:, 0:1], None, ALU.is_equal))
                link(nc.vector.memset(half_col[:, :], 0.5))
                link(nc.vector.memset(ones_d[:, :], 1.0 / D))
                link(nc.vector.memset(ones_rows[:, :], 1.0))
                link(nc.vector.tensor_scalar(trash_row[:, :], part_f[:, :], float(NPAD), None, ALU.add))
                link(nc.vector.memset(base_row[0:1, GROUPS:GROUPS + 4], 0))
                begin_chain(s_bias_split)
                link(nc.vector.tensor_copy(bf2_parts[0:1, 0, :], bf2[:, :]))
                link(nc.vector.tensor_tensor(bf2_f[0:1, 1, :], bf2[:, :], bf2_parts[0:1, 0, :], ALU.subtract))
                link(nc.vector.tensor_copy(bf2_parts[0:1, 1, :], bf2_f[0:1, 1, :]))
                link(nc.vector.tensor_tensor(bf2_f[0:1, 2, :], bf2_f[0:1, 1, :], bf2_parts[0:1, 1, :], ALU.subtract))
                link(nc.vector.tensor_copy(bf2_parts[0:1, 2, :], bf2_f[0:1, 2, :]))
                return nc.vector.value_load(flag_i[0:1, 0:1], min_val=0, max_val=1)

            def batch_norm(rnd, feat):
                begin_chain(s_bn[rnd])
                for c in range(N // BN_CHUNK):
                    if rnd == 0 and c % (X_COLS // BN_CHUNK) == 0:
                        dve.wait_ge(s_x_in[c * BN_CHUNK // X_COLS], 16)
                    nc.vector.bn_stats(bn_raw[:, c, :], feat[:, c * BN_CHUNK:(c + 1) * BN_CHUNK]).then_inc(s_bn[rnd], 1)
                begin_chain(s_bn[rnd], N // BN_CHUNK)
                dve.wait_ge(s_bn[rnd], N // BN_CHUNK)
                link(nc.vector.bn_aggr(bn_mv[:, :], bn_raw[:, :, :].rearrange("p c s -> p (c s)")))
                dve.wait_ge(s_bn_sd[rnd], 1)
                dve.wait_ge(s_const_in, 18 * 16)
                link(nc.vector.reciprocal(bn_tmp[:, 1:2], bn_tmp[:, 0:1]))
                link(nc.vector.tensor_tensor(bn_scale[:, :], gamma[rnd][:, :], bn_tmp[:, 1:2], ALU.mult))
                link(nc.vector.tensor_tensor(bn_tmp[:, 1:2], bn_scale[:, :], bn_mv[:, 0:1], ALU.mult))
                link(nc.vector.tensor_tensor(bn_shift[:, :], beta[rnd][:, :], bn_tmp[:, 1:2], ALU.subtract))

            def message_rows(rnd):
                with dve.Fori(0, TRANS_ITERS) as r:
                    for j in range(BODY):
                        dve.wait_ge(s_mm_done[rnd], r * BODY + (j + 1 + SLOT2))
                        dve.wait_ge(s_row_out[rnd][j % SLOTS], r * (16 * BODY // SLOTS) + 16 * (j // SLOTS + 1))
                        nc.vector.tensor_tensor(out_rows[:, j % SLOTS, :], ps_a[j % 2][:, 0:TD], b_types[rnd][:, :],
                                                ALU.add).then_inc(s_row_ready[rnd], 1)

            def stage_indices(p, it, h):
                rows = msg_idx if p < 2 else uniq_idx
                nc.vector.tensor_copy(idx_stage[:, h, :],
                                      rows[:, ds(it * ITER_TILES + h * HALF_TILES, HALF_TILES)]
                                      ).then_inc(s_idx[p], 1)

            def build_onehot(p, it, h):
                shape = [P, HALF_TILES, WINDOW]
                nc.vector.tensor_tensor(
                    onehot[:, h, :, :], iota_f[:, 0:WINDOW].unsqueeze(1).broadcast_to(shape),
                    dst_local[:, ds(it * ITER_TILES + h * HALF_TILES, HALF_TILES)].unsqueeze(2).broadcast_to(shape),
                    ALU.is_equal).then_inc(s_onehot[p], 1)

            def same_source(it, h, signal):
                shape = [P, HALF_TILES, P]
                nc.vector.tensor_tensor(
                    same_src[:, h, :, :], src_bc[:, h, :].rearrange("p (t n) -> p t n", t=HALF_TILES),
                    src_idx[:, ds(it * ITER_TILES + h * HALF_TILES, HALF_TILES)].unsqueeze(2).broadcast_to(shape),
                    ALU.is_equal).then_inc(signal, 1)

            def output_rows(r, h):
                k = r * 2 + h
                src = src_idx[:, ds(r * ITER_TILES + h * HALF_TILES, HALF_TILES)]
                nc.vector.tensor_scalar(to_trash, src, -1.0, trash_row[:, 0:1], ALU.mult, ALU.add).then_inc(s_uniq, 1)
                dve.wait_ge(s_first, k + 1)
                dve.wait_ge(s_uniq, k * 3 + 2)
                nc.vector.scalar_tensor_tensor(out=to_trash, in0=ps_first, scalar=first_w[:, 1:2], in1=to_trash,
                                               op0=ALU.is_ge, op1=ALU.mult).then_inc(s_uniq, 1)
                dve.wait_ge(s_uniq, k * 3 + 3)
                nc.vector.tensor_tensor(uniq_idx[:, ds(r * ITER_TILES + h * HALF_TILES, HALF_TILES)], src, to_trash,
                                        ALU.add).then_inc(s_uniq, 1)
                dve.wait_ge(s_uniq, k * 3 + 4)

            def accumulate(p, acc, r, h, bases):
                for j in range(2):
                    g = r * 4 + (2 * h + j)
                    dve.wait_ge(s_agg[p], g + 1)
                    dve.wait_ge(s_acc[p], g + SLOT2)
                    at = acc[:, ds(bases[2 * h + j], WINDOW)]
                    nc.vector.tensor_tensor(at, at, ps_agg[j], ALU.add).then_inc(s_acc[p], 1)

            def beyond_window(p, acc, r, h):
                with dve.If(flag > 0):
                    for j in range(2):
                        g = r * 4 + (2 * h + j)
                        cols = dst_local[:, ds(g * GROUP_TILES, GROUP_TILES)]
                        nc.vector.drain()
                        nc.vector.tensor_tensor(x_rem[:, :], cols,
                                                base_bc[:, ds(g, 1)].broadcast_to([P, GROUP_TILES]), ALU.add)
                        nc.vector.drain()
                        nc.vector.tensor_scalar(x_rem[:, :], x_rem[:, :], 1.0, None, ALU.add)
                        nc.vector.drain()
                        nc.vector.scalar_tensor_tensor(out=x_rem[:, :], in0=cols, scalar=float(WINDOW),
                                                       in1=x_rem[:, :], op0=ALU.is_ge, op1=ALU.mult)
                        nc.vector.drain()
                        nc.vector.tensor_scalar(x_rem[:, :], x_rem[:, :], -1.0, None, ALU.add)
                        with dve.Fori(0, WIDE_STEPS) as b:
                            step = g * WIDE_STEPS + b
                            nc.vector.drain()
                            for t in range(GROUP_TILES):
                                last = nc.vector.tensor_scalar(x_onehot[:, t, :], iota_f[:, :], x_rem[:, t:t + 1],
                                                               None, ALU.is_equal)
                            last.then_inc(s_xoh[p], 1)
                            nc.vector.drain()
                            nc.vector.tensor_scalar(x_rem[:, :], x_rem[:, :], float(-WIDE), None, ALU.add)
                            dve.wait_ge(s_xagg[p], step + 1)
                            at = acc[:, ds(b * WIDE, WIDE)]
                            nc.vector.tensor_tensor(at, at, ps_extra[:, :], ALU.add)
                        nc.vector.drain()

            def load_bases(r):
                return nc.values_load_multi_w_load_instructions(
                    base_row[0:1, ds(r * 4, 4)], engines=[mybir.EngineType.DVE], min_val=0, max_val=N - WINDOW,
                    skip_runtime_bounds_check_because="computed as a minimum with N - WINDOW")[1]

            def round_pass(p, acc):
                dve.wait_ge(s_clear[p], 1)
                if p == 1:
                    for h in range(2):
                        stage_indices(p, 0, h)
                build_onehot(p, 0, 0)
                with dve.Fori(0, ITERS) as r:
                    bases = load_bases(r)
                    for h in range(2):
                        build_onehot(p, r + h, 1 - h)
                        if p == 1:
                            dve.wait_ge(s_src_in[h], r * 16 + 16)
                            same_source(r, h, s_dup)
                        accumulate(p, acc, r, h, bases)
                        beyond_window(p, acc, r, h)
                        if p == 1:
                            output_rows(r, h)
                        stage_indices(p, r + 1, h)

            batch_norm(0, buf_x)
            message_rows(0)
            flag = set_up()
            for q in range(SLOTS):
                dve.wait_ge(s_row_out[0][q], 16 * (BLOCKS // SLOTS + 1))
            nc.vector.memset(zeros, 0.0).then_inc(s_zero, 1)
            round_pass(0, buf_a)
            dve.wait_ge(s_acc[0], GROUPS + SLOT2)
            dve.wait_ge(s_zeroed, 16 * COPIES * ZERO_STEPS)
            batch_norm(1, buf_a)
            message_rows(1)
            round_pass(1, buf_x)

            def y_chunk(m, q, loaded):
                dve.wait_ge(s_xt_in[q], loaded)
                chunk = buf_x[:, ds(m * WIDE, WIDE)]
                nc.vector.scalar_tensor_tensor(out=chunk, in0=x_in[:, q, :], scalar=2.0, in1=chunk, op0=ALU.mult,
                                               op1=ALU.add).then_inc(s_y, 1)

            def centre(m, s):
                dve.wait_ge(s_mean, m + 1)
                chunk = buf_x[:, ds(m * WIDE, WIDE)]
                nc.vector.tensor_tensor(chunk, chunk, ps_mean[s], ALU.subtract).then_inc(s_yc, 1)

            def x1_chunk(m, s):
                dve.wait_ge(s_sd, m + (1 + SLOT2))
                nc.vector.reciprocal(sd[:, s, :], sd[:, s, :]).then_inc(s_rsd, 1)
                dve.wait_ge(s_rsd, m + 1)
                dve.wait_ge(s_hmm, m + 1)
                dve.wait_ge(s_x1b, m + 1)
                nc.vector.tensor_tensor(x1[:, s, :], buf_x[:, ds(m * WIDE, WIDE)], sd[:, s, :],
                                        ALU.mult).then_inc(s_x1, 1)

            dve.wait_ge(s_acc[1], GROUPS + SLOT2)
            y_chunk(0, 0, 16)
            y_chunk(1, 1, 16)
            centre(0, 0)
            with dve.Fori(0, CHUNKS // 4) as r:
                for j in range(4):
                    m = r * 4 + j
                    y_chunk(m + 2, (j + 2) % 4, r * 16 + 16 * ((j + 2) // 4 + 1))
                    centre(m + 1, (j + 1) % 2)
                    x1_chunk(m, j % 2)
            for m in range(CHUNKS // 4 * 4, CHUNKS):
                if m + 1 < CHUNKS:
                    centre(m + 1, (m + 1) % 2)
                x1_chunk(m, m % 2)

            def soft_half(k):
                for j in range(2):
                    dve.wait_ge(s_act, k * 6 + (6 + j))
                    nc.vector.scalar_tensor_tensor(out=soft[:, j, :], in0=ps_z[j], scalar=0.0,
                                                   in1=log_z[:, j, :], op0=ALU.max, op1=ALU.add).then_inc(s_soft, 1)

            def spread_half(it, h):
                dve.wait_ge(s_edge_in[h], it * 32 + 32)
                for j in range(2):
                    nc.vector.tensor_scalar(spread[:, h, j * WIDE:(j + 1) * WIDE], dst_bc[:, h, j * WIDE:(j + 1) * WIDE],
                                            win_node[:, ds(it * 4 + (2 * h + j), 1)], None, ALU.is_equal
                                            ).then_inc(s_spread, 1)

            def stage_cutoff(it, h):
                nc.vector.tensor_copy(cut_stage[:, h, :],
                                      cutoff[:, ds(it * ITER_TILES + h * HALF_TILES, HALF_TILES)]).then_inc(s_cut, 1)

            def spread_beyond(r, h):
                with dve.If(flag > 0):
                    with dve.Fori(0, 2) as j:
                        g = r * 4 + 2 * h + j
                        dst = dst_bc[:, h, ds(j * WIDE, WIDE)]
                        nc.vector.drain()
                        nc.vector.tensor_scalar(x_rem[:, 0:1], base_bc[:, ds(g, 1)], float(WINDOW), None, ALU.add)
                        nc.vector.tensor_scalar(x_onehot[:, 0, :], dst, 1.0, None, ALU.add)
                        nc.vector.drain()
                        nc.vector.scalar_tensor_tensor(out=x_dst, in0=dst, scalar=x_rem[:, 0:1], in1=x_onehot[:, 0, :],
                                                       op0=ALU.is_ge, op1=ALU.mult)
                        nc.vector.drain()
                        nc.vector.tensor_scalar(x_dst, x_dst, -1.0, None, ALU.add)
                        with dve.Fori(0, BLOCKS) as b:
                            step = g * BLOCKS + b
                            nc.vector.drain()
                            nc.vector.tensor_scalar(x_onehot[:, 0, :], x_dst, part_f[:, 0:1], None,
                                                    ALU.is_equal).then_inc(s_xoh[2], 1)
                            nc.vector.drain()
                            nc.vector.tensor_scalar(x_dst, x_dst, float(-P), None, ALU.add)
                            dve.wait_ge(s_xagg[2], step + 2)
                            at = h_edge[:, ds(j, 1), :].rearrange("p o n -> p (o n)")
                            nc.vector.tensor_tensor(at, at, ps_c[0][:, :], ALU.add).then_inc(s_xadd, 1)
                    nc.vector.drain()

            def convolution_step(r, first):
                for h in range(2):
                    k = r * 2 + h
                    spread_half(r + h, 1 - h)
                    dve.wait_ge(s_comb, k * 2 + SLOT2)
                    same_source(r + h, 1 - h, s_same)
                    dve.wait_ge(s_hcopy, k * 2 + (2 + SLOT2))
                    stage_cutoff(r + h, 1 - h)
                    spread_beyond(r, h)
                    dve.wait_ge(s_cut, k + 4)
                    for j in range(2):
                        dve.wait_ge(s_w, k * 2 + (j + 1))
                        for t in range(GROUP_TILES):
                            tile = slice(t * D, (t + 1) * D)
                            last = nc.vector.scalar_tensor_tensor(
                                out=msg[:, j, tile], in0=ps_w[j][:, tile],
                                scalar=cut_stage[:, h, j * GROUP_TILES + t:j * GROUP_TILES + t + 1],
                                in1=h_edge[:, j, tile], op0=ALU.mult, op1=ALU.mult)
                        last.then_inc(s_msg, 1)
                    if not first:
                        for j in range(2):
                            dve.wait_ge(s_scat[h][j], r * 64)
                    stage_indices(2, r, h)
                    soft_half(k + 1)

            nc.vector.memset(win_node[:, GROUPS:GROUPS + 4], -1.0).then_inc(s_cut, 1)
            nc.vector.tensor_scalar(win_node[:, 0:GROUPS], base_bc[:, :], part_f[:, 0:1], None, ALU.add).then_inc(s_cut, 1)
            nc.vector.memset(f_sb[RBF:RBF + 1, :, :, :], 1.0).then_inc(s_cut, 1)
            stage_cutoff(0, 0)
            dve.wait_ge(s_cut, 4)
            for s in s_hout:
                dve.wait_ge(s, 16 * (CHUNKS // 2 + 1))
            spread_half(0, 0)
            same_source(0, 0, s_same)
            soft_half(0)
            convolution_step(0, True)
            with dve.Fori(1, ITERS) as r:
                convolution_step(r, False)

            def sum_copies(m, q, loaded):
                dve.wait_ge(s_cp_in[q], loaded)
                half, step = COPIES, 0
                while half > 2:
                    half //= 2
                    step += 1
                    if step > 1:
                        dve.wait_ge(s_cp_sum, m * SUM_STEPS + (step - 1))
                    nc.vector.tensor_tensor(copy_rows[:, q, 0:half, :], copy_rows[:, q, 0:half, :],
                                            copy_rows[:, q, half:2 * half, :], ALU.add).then_inc(s_cp_sum, 1)

            def row_statistics(m):
                dve.wait_ge(s_fy, m + (1 + SLOT2))
                for b in range(4):
                    nc.vector.bn_stats(ln_raw[:, ds(m * 4 + b, 1), :].rearrange("p o s -> p (o s)"),
                                       buf_x[:, ds(m * WIDE + b * P, P)]).then_inc(s_fst, 1)

            def out_soft(m, s):
                dve.wait_ge(s_fact, m * 4 + 5)
                nc.vector.tensor_tensor(soft[:, s, :], log_z[:, s, :], relu_z[:, s, :], ALU.add).then_inc(s_fsoft, 1)

            def output_step(m, j, loaded):
                s = j % 2
                if j + 2 < CHUNKS:
                    sum_copies(m + 2, (j + 2) % 3, loaded)
                row_statistics(m)
                if j + 1 < CHUNKS:
                    out_soft(m + 1, 1 - s)

            LOADED = 16 * COPIES
            sum_copies(0, 0, LOADED)
            sum_copies(1, 1, LOADED)
            out_soft(0, 0)
            with dve.Fori(0, LOOP6) as r:
                for j in range(6):
                    output_step(r * 6 + j, j, r * (2 * LOADED) + LOADED * ((j + 2) // 3 + 1))
            for m in range(6 * LOOP6, CHUNKS):
                output_step(m, m, LOADED * ((m + 2) // 3 + 1))
            dve.wait_ge(s_fst, 4 * CHUNKS)
            begin_chain(s_ln)
            me, mo, qe, qo = (ln_raw[:, :, i] for i in (1, 4, 2, 5))
            a, v = ln_tmp[:, 0, :], ln_tmp[:, 1, :]
            link(nc.vector.tensor_tensor(a, me, mo, ALU.subtract))
            link(nc.vector.tensor_tensor(ln_mean[:, :], me, mo, ALU.add))
            link(nc.vector.tensor_tensor(v, qe, qo, ALU.add))
            link(nc.vector.scalar_tensor_tensor(out=a, in0=a, scalar=D / 4.0, in1=a, op0=ALU.mult, op1=ALU.mult))
            link(nc.vector.tensor_tensor(v, v, a, ALU.add))
            link(nc.vector.tensor_scalar(v, v, 1.0 / D, None, ALU.mult))
            dve.wait_ge(s_ln_sd, 1)
            link(nc.vector.reciprocal(ln_rstd[:, :], a))
            link(nc.vector.tensor_scalar(ln_mean[:, :], ln_mean[:, :], 0.5, None, ALU.mult))
            link(nc.vector.scalar_tensor_tensor(out=ln_shift[:, :], in0=ln_mean[:, :], scalar=-1.0, in1=ln_rstd[:, :],
                                                op0=ALU.mult, op1=ALU.mult))

            def normalise(m, q, stored):
                dve.wait_ge(s_fin_out[q], stored)
                for b in range(4):
                    last = nc.vector.tensor_scalar(final_rows[:, q, b * P:(b + 1) * P], buf_x[:, ds(m * WIDE + b * P, P)],
                                                   ln_mean[:, ds(m * 4 + b, 1)], ln_rstd[:, ds(m * 4 + b, 1)],
                                                   ALU.subtract, ALU.mult)
                last.then_inc(s_fin[0], 1)

            with dve.Fori(0, CHUNKS // 4) as r:
                for q in (0, 2):
                    normalise(r * 4 + q, q, r * 16 + 16)
            for m in range(CHUNKS // 4 * 4, CHUNKS, 2):
                normalise(m, m % 4, 16 * (m // 4 + 1))

        @block.tensor
        def _(pe):
            for rnd in range(2):
                pe.sem_inc(s_mm_done[rnd], SLOT2)
                pe.sem_inc(s_row_ready[rnd], SLOT2)
                for q in range(SLOTS):
                    pe.sem_inc(s_row_out[rnd][q], 16)
            for p in range(2):
                pe.sem_inc(s_acc[p], SLOT2)
            for s in s_hout + s_fin_out:
                pe.sem_inc(s, 16)
            for s in (s_yc, s_var, s_sd, s_x1, s_x1b, s_hmm, s_hrow, s_soft, s_fsoft, s_msg, s_hcopy, s_comb_out, s_comb,
                      s_fz, s_fo, s_fy, s_cp_out):
                pe.sem_inc(s, SLOT2)
            for s in (s_act, s_fact, s_xagg[2], s_xadd, s_uniq):
                pe.sem_inc(s, 1)
            pe.wait_ge(s_const_in, 18 * 16)

            def transform(rnd):
                with pe.Fori(0, TRANS_ITERS) as r:
                    for j in range(BODY):
                        n = r * BODY + j
                        pe.wait_ge(s_h_ready[rnd], n + 1)
                        pe.wait_ge(s_row_ready[rnd], n + 1)
                        nc.tensor.matmul(ps_a[j % 2][:, 0:WIDE], h_stage[:, j % 2, :], w_types[rnd][:, 0:WIDE],
                                         start=True, stop=True)
                        nc.tensor.matmul(ps_a[j % 2][:, WIDE:TD], h_stage[:, j % 2, :], w_types[rnd][:, WIDE:TD],
                                         start=True, stop=True).then_inc(s_mm_done[rnd], 1)

            def aggregate(p, r, h):
                for j in range(2):
                    g = r * 4 + (2 * h + j)
                    pe.wait_ge(s_gather[p][h][j], r * (16 * GROUP_TILES) + 16 * GROUP_TILES)
                    pe.wait_ge(s_onehot[p], r * 2 + (h + 1))
                    pe.wait_ge(s_acc[p], g + 1)
                    for t in range(GROUP_TILES):
                        last = nc.tensor.matmul(ps_agg[j], gathered[:, h, j * GROUP_TILES + t, :], onehot[:, h, j * GROUP_TILES + t, :],
                                                start=(t == 0), stop=(t == GROUP_TILES - 1))
                    last.then_inc(s_agg[p], 1)
                with pe.If(flag > 0):
                    for j in range(2):
                        g = r * 4 + (2 * h + j)
                        with pe.Fori(0, WIDE_STEPS) as b:
                            pe.wait_ge(s_xoh[p], g * WIDE_STEPS + b + 1)
                            for t in range(GROUP_TILES):
                                last = nc.tensor.matmul(ps_extra[:, :], gathered[:, h, j * GROUP_TILES + t, :], x_onehot[:, t, :],
                                                        start=(t == 0), stop=(t == GROUP_TILES - 1))
                            last.then_inc(s_xagg[p], 1)

            def first_of_source(k, h):
                pe.wait_ge(s_dup, k + 1)
                pe.wait_ge(s_uniq, k * 3 + 1)
                for t in range(HALF_TILES):
                    last = nc.tensor.matmul(ps_first[:, t:t + 1], same_src[:, h, t, :], first_w[:, 0:1], start=True,
                                            stop=True)
                last.then_inc(s_first, 1)

            for rnd in range(2):
                transform(rnd)
                if rnd == 0:
                    pe.wait_ge(s_setup, 18)
                    pe.wait_ge(s_parts_in, 48)
                    flag = nc.tensor.value_load(flag_i[0:1, 0:1], min_val=0, max_val=1)
                with pe.Fori(0, ITERS) as r:
                    for h in range(2):
                        aggregate(rnd, r, h)
                        if rnd == 1:
                            first_of_source(r * 2 + h, h)

            def mean(m, s):
                pe.wait_ge(s_y, m + 1)
                pe.wait_ge(s_yc, m + 1)
                nc.tensor.matmul(ps_mean[s], ones_d[:, :], buf_x[:, ds(m * WIDE, WIDE)], start=True,
                                 stop=True).then_inc(s_mean, 1)

            def variance(m, s):
                pe.wait_ge(s_sq, m + 1)
                pe.wait_ge(s_sd, m + 1)
                nc.tensor.matmul(ps_var[s], ones_d[:, :], squares[:, s, :], start=True, stop=True).then_inc(s_var, 1)

            def h_chunk(m, s):
                pe.wait_ge(s_x1, m + (1 + SLOT2))
                pe.wait_ge(s_hrow, m + 1)
                for t in range(4):
                    last = nc.tensor.matmul(ps_rows[s][:, t * P:(t + 1) * P], x1[:, s, t * P:(t + 1) * P], w_in[:, :],
                                            start=True, stop=True)
                last.then_inc(s_hmm, 1)

            mean(0, 0)
            mean(1, 1)
            variance(0, 0)
            with pe.Fori(0, CHUNKS // 4) as r:
                for j in range(4):
                    m = r * 4 + j
                    mean(m + 2, j % 2)
                    variance(m + 1, (j + 1) % 2)
                    h_chunk(m, j % 2)
            for m in range(CHUNKS // 4 * 4, CHUNKS):
                if m + 1 < CHUNKS:
                    variance(m + 1, (m + 1) % 2)
                h_chunk(m, m % 2)

            def filter_in(k, h, f_count):
                for j in range(2):
                    pe.wait_ge(s_f_in[h], f_count)
                    pe.wait_ge(s_soft, k * 2 + (j - 1 + SLOT2))
                    nc.tensor.matmul(ps_z[j], wf1[:, :], f_sb[:, h, j, :], start=True, stop=True).then_inc(s_z, 1)

            pe.wait_ge(s_cut, 3)
            filter_in(0, 0, 16)
            with pe.Fori(0, ITERS) as r:
                for h in range(2):
                    k = r * 2 + h
                    for j in range(2):
                        pe.wait_ge(s_win_in[h], r * 32 + 32)
                        pe.wait_ge(s_spread, k * 2 + (j + 1))
                        pe.wait_ge(s_hcopy, k * 2 + (j + 1))
                        for t in range(GROUP_TILES):
                            tile = slice(t * P, (t + 1) * P)
                            last = nc.tensor.matmul(ps_h[j][:, tile], spread[:, h, j * WIDE + t * P:j * WIDE + (t + 1) * P],
                                                    h_win[:, h, j, :], start=True, stop=True)
                        last.then_inc(s_hexp, 1)
                    with pe.If(flag > 0):
                        with pe.Fori(0, 2) as j:
                            with pe.Fori(0, BLOCKS) as b:
                                step = (k * 2 + j) * BLOCKS + b
                                pe.wait_ge(s_comb_out, k * 2 + SLOT2)
                                pe.wait_ge(s_xh_in, step * 16 + 16)
                                pe.wait_ge(s_xoh[2], step + 1)
                                pe.wait_ge(s_xadd, step + 1)
                                for t in range(GROUP_TILES):
                                    tile = slice(t * P, (t + 1) * P)
                                    last = nc.tensor.matmul(ps_c[0][:, tile], x_onehot[:, 0, tile], x_h, start=True,
                                                            stop=True)
                                last.then_inc(s_xagg[2], 1)
                    filter_in(k + 1, 1 - h, (r + h) * 16 + 16)
                    for j in range(2):
                        pe.wait_ge(s_soft, k * 2 + (j + 1 + SLOT2))
                        nc.tensor.matmul(ps_w[j], ones_rows[:, :],
                                         bf2_rows[:, :].unsqueeze(1).broadcast_to([3, GROUP_TILES, D]),
                                         start=True, stop=False)
                        for t in range(GROUP_TILES):
                            last = nc.tensor.matmul(ps_w[j][:, t * D:(t + 1) * D], soft[:, j, t * P:(t + 1) * P],
                                                    wf2[:, :], start=False, stop=(t == GROUP_TILES - 1))
                        last.then_inc(s_w, 1)
                    for j in range(2):
                        pe.wait_ge(s_msg, k * 2 + (j + 1 + SLOT2))
                        pe.wait_ge(s_same, k + 1)
                        pe.wait_ge(s_comb_out, k * 2 + (j + 1))
                        for t in range(GROUP_TILES):
                            last = nc.tensor.matmul(ps_c[j][:, t * D:(t + 1) * D], same_src[:, h, j * GROUP_TILES + t, :],
                                                    msg[:, j, t * D:(t + 1) * D], start=True, stop=True)
                        last.then_inc(s_comb, 1)

            def turn_sums(m, q, s):
                pe.wait_ge(s_cp_sum, m * SUM_STEPS + SUM_STEPS)
                pe.wait_ge(s_cp_out, m + 1)
                for b in range(4):
                    for c in range(2):
                        last = nc.tensor.matmul(ps_b[s][:, b * P:(b + 1) * P], copy_rows[:, q, c, b * P:(b + 1) * P],
                                                ident[:, :], start=(c == 0), stop=(c == 1))
                last.then_inc(s_cp_t, 1)

            def out_z(m, s):
                pe.wait_ge(s_cp_out, m + (1 + SLOT2))
                nc.tensor.matmul(ps_z[s], wo1[:, :], out_t[:, s, :], start=True, stop=True).then_inc(s_fz, 1)

            def out_rows_sum(m, s):
                pe.wait_ge(s_fsoft, m + (1 + SLOT2))
                pe.wait_ge(s_fx, m + 1)
                pe.wait_ge(s_fy, m + 1)
                for t in range(4):
                    tile = slice(t * P, (t + 1) * P)
                    nc.tensor.matmul(ps_w[s][:, tile], soft[:, s, tile], wo2[:, :], start=True, stop=False)
                    last = nc.tensor.matmul(ps_w[s][:, tile], x_stage[:, s, tile], ident[:, :], start=False, stop=True)
                last.then_inc(s_fo, 1)

            def output_step(m, j):
                s = j % 2
                if j + 1 < CHUNKS:
                    out_z(m + 1, 1 - s)
                out_rows_sum(m, s)
                if j + 2 < CHUNKS:
                    turn_sums(m + 2, (j + 2) % 3, s)

            turn_sums(0, 0, 0)
            turn_sums(1, 1, 1)
            out_z(0, 0)
            with pe.Fori(0, LOOP6) as r:
                for j in range(6):
                    output_step(r * 6 + j, j)
            for m in range(6 * LOOP6, CHUNKS):
                output_step(m, m)


def kernel(**inputs):
    import concourse.bacc as bacc
    from concourse.bass_utils import run_bass_kernel_spmd

    def tiles(name, padding=0):
        a = np.asarray(inputs[name]).reshape(E)
        return np.ascontiguousarray(np.pad(a, (0, COLS * P - E), constant_values=padding).reshape(COLS, P).T)

    def row(a, **padding):
        return np.pad(a, (0, HALVES * COLS_HALF - E), **padding).reshape(1, HALVES * COLS_HALF)

    x = np.pad(np.asarray(inputs["x"]), ((0, NBUF - N), (0, 0)))
    dst = np.asarray(inputs["dst"])
    attr = np.pad(np.asarray(inputs["edge_attr3_1x32"]).reshape(E, RBF), ((0, HALVES * 2 * GROUP_EDGES - E), (0, 0)))
    arrays = {
        "xT": np.ascontiguousarray(x.T),
        "src": tiles("src", NPAD - 1), "dst": tiles("dst"), "etype": tiles("edge_type_5"), "cutoff": tiles("edge_weight1"),
        "dst_groups": np.pad(dst, (0, GROUPS * GROUP_EDGES - E), mode="edge").reshape(RANGE_PARTS, 4 * GROUP_EDGES),
        "dst_row": row(dst, mode="edge"),
        "src_row": row(np.asarray(inputs["src"]), constant_values=NPAD - 1),
        "first_w": np.array([[3.0 ** (P // 2 - p), 2 * 3.0 ** (P // 2 - p)] for p in range(P)], np.float32),
        "attr": np.ascontiguousarray(attr.reshape(HALVES, 2, GROUP_EDGES, RBF).transpose(0, 1, 3, 2)
                                     ).reshape(HALVES * 2 * RBF, GROUP_EDGES),
    }
    for i in (1, 2):
        arrays[f"w{i}T"] = np.ascontiguousarray(np.asarray(inputs[f"L0_gnn_w{i}"]).T)
        arrays[f"b{i}"] = np.asarray(inputs[f"L0_gnn_b{i}"]).reshape(1, TD)
        arrays[f"g{i}"] = np.asarray(inputs[f"L0_gnn_g{i}"]).reshape(D, 1)
        arrays[f"be{i}"] = np.asarray(inputs[f"L0_gnn_be{i}"]).reshape(D, 1)
    for name in ("W_in", "Wf1", "Wf2", "Wo1", "Wo2"):
        arrays[name] = np.asarray(inputs[f"L1_gnn_{name}"])
    for name, shape in (("bf1", (1, D)), ("bo1", (D, 1)), ("bf2", (1, D)), ("bo2", (D, 1))):
        arrays[name] = np.asarray(inputs[f"L1_gnn_{name}"]).reshape(shape)

    nc = bacc.Bacc("TRN2", target_bir_lowering=False, num_devices=1)
    dram = {n: nc.dram_tensor(f"in_{n}", a.shape, mybir.dt.from_np(a.dtype), kind="ExternalInput").ap()
            for n, a in arrays.items()}
    out = nc.dram_tensor("out", (NBUF, D), mybir.dt.float32, kind="ExternalOutput").ap()
    gnn_program(nc, dram, out)
    ran = run_bass_kernel_spmd(nc, [{f"in_{n}": a for n, a in arrays.items()}], core_ids=[0])
    return ran.results[0]["out"][:N]
```

```python
import numpy as np

import concourse.bass as bass
from concourse import mybir
from contextlib import ExitStack

N, E, D, T, RBF = 12500, 200000, 128, 5, 32
EPS = 1e-5
LOG2 = 0.6931471805599453
P = 128
WINDOW = 128
GROUP_TILES = 4
GROUP_EDGES = GROUP_TILES * P
HALF_TILES = 2 * GROUP_TILES
ITER_TILES = 2 * HALF_TILES
ITERS = -(-E // (ITER_TILES * P))
TILES = ITERS * ITER_TILES
GROUPS = TILES // GROUP_TILES
COLS_HALF = HALF_TILES * P
COLS = TILES + ITER_TILES
HALVES = 2 * ITERS + 2
BLOCKS = -(-N // P)
NPAD = BLOCKS * P
WIDE = 512
COPIES = HALF_TILES
CHUNKS = 2 * -(-NPAD // (2 * WIDE))
NBUF = CHUNKS * WIDE
ACC_ROWS = NBUF + 2 * WIDE
SUM_STEPS = COPIES.bit_length() - 2
ZERO_STEPS = 14
ZERO_COLS = ACC_ROWS // ZERO_STEPS
LOOP6 = CHUNKS // 6
WIDE_STEPS = -(-N // WIDE)
BODY = 14
TRANS_ITERS = BLOCKS // BODY
SLOTS = 7
BN_CHUNK = 500
TD = T * D
RANGE_PARTS = GROUPS // GROUP_TILES
EXP_LN_SET = 6
X_PARTS = 5
X_COLS = N // X_PARTS
assert BLOCKS % BODY == 0 and X_COLS * X_PARTS == N and X_COLS % BN_CHUNK == 0 and GROUPS % 4 == 0 and BODY % SLOTS == 0


def gnn_program(nc, dram, out):
    f32, bf16, i32, i16 = mybir.dt.float32, mybir.dt.bfloat16, mybir.dt.int32, mybir.dt.int16
    ALU, ACT, AX = mybir.AluOpType, mybir.ActivationFunctionType, mybir.AxisListType
    ds = bass.ds

    ctx = ExitStack()
    with ctx:
        def sb(name, shape, dt=f32):
            return ctx.enter_context(nc.sbuf_tensor(name, shape, dt))

        def pb(name, shape):
            return ctx.enter_context(nc.psum_tensor(name, shape, f32))

        def sem(name):
            return ctx.enter_context(nc.semaphore(name))

        table = [nc.dram_tensor(f"messages_{i}", (NPAD, TD), f32).ap() for i in range(2)]
        htable = nc.dram_tensor("h_in", (NBUF, D), f32).ap()
        acc_rows = [nc.dram_tensor(f"acc_{c}", (ACC_ROWS, D), f32).ap() for c in range(COPIES)]
        src_rows, dst_rows = (nc.dram_tensor(n, (RANGE_PARTS + 1, 4 * GROUP_EDGES), i16).ap() for n in ("src_rows", "dst_rows"))
        base_dram = nc.dram_tensor("group_base", (RANGE_PARTS, 4), i32).ap()
        span_dram = nc.dram_tensor("group_span", (RANGE_PARTS, 4), i32).ap()

        buf_x = sb("buf_x", [P, NBUF])
        buf_a = sb("buf_a", [P, NBUF])
        src_idx = sb("src_idx", [P, COLS], i32)
        msg_idx = sb("msg_idx", [P, COLS], i32)
        dst_local = sb("dst_local", [P, COLS])
        cutoff = sb("cutoff", [P, COLS])
        base_row = sb("base_row", [1, GROUPS + 4], i32)
        base_bc = sb("base_bc", [P, GROUPS], i32)
        span_bc = sb("span_bc", [P, GROUPS], i32)
        flag_f = sb("flag_f", [P, 1])
        flag_i = sb("flag_i", [P, 1], i32)
        idx_stage = sb("idx_stage", [P, 2, HALF_TILES], i32)
        gathered = sb("gathered", [P, 2, HALF_TILES, D])
        onehot = sb("onehot", [P, 2, HALF_TILES, WINDOW])
        work = sb("work", [P, 10 * WIDE])
        x_onehot = sb("x_onehot", [P, GROUP_TILES, WIDE])
        x_rem = sb("x_rem", [P, GROUP_TILES])
        h_stage = sb("h_stage", [P, 2, P])
        ones_d = sb("ones_d", [P, P])
        iota_f = sb("iota_f", [P, WIDE])
        part_i = sb("part_i", [P, 1], i32)
        part_f = sb("part_f", [P, 1])
        w_types = [sb(f"w_types_{i}", [P, TD]) for i in range(2)]
        b_types = [sb(f"b_types_{i}", [P, TD]) for i in range(2)]
        gamma = [sb(f"gamma_{i}", [P, 1]) for i in range(2)]
        beta = [sb(f"beta_{i}", [P, 1]) for i in range(2)]
        w_in = sb("w_in", [P, D])
        ident = sb("ident", [P, P])
        wf1 = sb("wf1", [RBF + 1, D])
        wf2 = sb("wf2", [P, D])
        biases = sb("biases", [1, 2, D])
        bias_rest = sb("bias_rest", [1, 2, 2, D])
        bias_parts = sb("bias_parts", [1, 3, 2, D], bf16)
        bias_rows = sb("bias_rows", [3, 2, D], bf16)
        ones_rows = sb("ones_rows", [3, P], bf16)
        wo1 = sb("wo1", [P, D])
        bo1 = sb("bo1", [P, 1])
        wo2 = sb("wo2", [P, D])
        first_w = sb("first_w", [P, 2])
        trash_row = sb("trash_row", [P, 1])
        bn_raw = sb("bn_raw", [P, N // BN_CHUNK, 6])
        bn_mv = sb("bn_mv", [P, 2])
        bn_scale = sb("bn_scale", [P, 1])
        bn_shift = sb("bn_shift", [P, 1])
        bn_tmp = sb("bn_tmp", [P, 2])
        eps_col = sb("eps_col", [P, 1])
        half_col = sb("half_col", [P, 1])
        ln_raw = sb("ln_raw", [P, CHUNKS * 4, 6])
        ln_mean = sb("ln_mean", [P, CHUNKS * 4])
        ln_rstd = sb("ln_rstd", [P, CHUNKS * 4])
        ln_shift = sb("ln_shift", [P, CHUNKS * 4])
        ln_tmp = sb("ln_tmp", [P, 2, CHUNKS * 4])

        out_rows = work[:, 0:SLOTS * TD].rearrange("p (q n) -> p q n", q=SLOTS)
        stage5 = work[:, :].rearrange("p (a j n) -> p a j n", a=5, j=2)
        abs_z, relu_z, log_z, soft, msg = (stage5[:, a] for a in range(5))
        x_in = work[:, 0:4 * WIDE].rearrange("p (q n) -> p q n", q=4)
        squares, centred = (work[:, (4 + 2 * i) * WIDE:(6 + 2 * i) * WIDE].rearrange("p (s n) -> p s n", s=2) for i in range(2))
        sd, rstd = (work[:, 8 * WIDE + 8 * i:8 * WIDE + 8 * (i + 1)].rearrange("p (s b) -> p s b", s=2) for i in range(2))
        h_rows = buf_a[:, 8 * WIDE:10 * WIDE].rearrange("p (s n) -> p s n", s=2)
        final_rows = work[:, 6 * WIDE:10 * WIDE].rearrange("p (q n) -> p q n", q=4)
        src_bc, dst_bc = (buf_a[:, i * COLS_HALF:(i + 1) * COLS_HALF].bitcast(i16).rearrange("p (h n) -> p h n", h=2)
                          for i in range(2))
        same_src = buf_a[:, 4096:4096 + 2 * COLS_HALF].rearrange("p (h t n) -> p h t n", h=2, t=HALF_TILES)
        h_edge = buf_a[:, 6144:7168].rearrange("p (j n) -> p j n", j=2)
        h_win = buf_a[:, 7168:7680].rearrange("p (h j n) -> p h j n", h=2, j=2)
        x_dst = buf_a[:, 7680:8192]
        x_h = buf_a[:, 8192:8192 + P]
        uniq_idx = buf_a[:, 8320:8320 + COLS].bitcast(i32)
        cut_stage = buf_a[:, 10400:10400 + 2 * HALF_TILES].rearrange("p (h t) -> p h t", h=2)
        to_trash = buf_a[:, 10432:10432 + HALF_TILES]
        f_sb = buf_a[0:RBF + 1, 10496:10496 + 4 * GROUP_EDGES].rearrange("p (h j n) -> p h j n", h=2, j=2)
        spread = onehot[:, :, :, :].rearrange("p h t n -> p h (t n)")
        combined = gathered[:, :, :, :].rearrange("p h t n -> p h (t n)")
        copy_rows = buf_a[:, 0:3 * COPIES * WIDE].rearrange("p (q c n) -> p q c n", q=3, c=COPIES)
        out_t = spread[:, 0, :].rearrange("p (s n) -> p s n", s=2)
        zeros = work[:, 0:ZERO_COLS]
        dst_groups = buf_a[0:RANGE_PARTS, 0:4 * GROUP_EDGES].bitcast(i32).rearrange("p (g n) -> p g n", g=4)
        src_groups = buf_a[0:RANGE_PARTS, 4 * GROUP_EDGES:8 * GROUP_EDGES].bitcast(i32)
        dst_short, src_short = (buf_a[0:RANGE_PARTS, i * GROUP_EDGES:(i + 2) * GROUP_EDGES].bitcast(i16) for i in (8, 10))
        dst_tiles = onehot[:, :, :, :].rearrange("p h t n -> p (h t n)")[:, 0:COLS].bitcast(i32)
        type_tiles = gathered[:, :, :, :].rearrange("p h t n -> p (h t n)")[:, 0:COLS].bitcast(i32)
        iota_i = x_onehot[:, 0, :].bitcast(i32)
        range_f = x_onehot[0:RANGE_PARTS, 1, 0:8].rearrange("p (a g) -> p a g", a=2)
        range_i = x_onehot[0:RANGE_PARTS, 1, 8:16].bitcast(i32).rearrange("p (a g) -> p a g", a=2)

        ps_a = [pb(f"ps_a{i}", [P, 2 * WIDE]) for i in range(2)]
        ps_b = [pb(f"ps_b{i}", [P, WIDE]) for i in range(4)]
        ps_z = [ps_a[0][:, j * WIDE:(j + 1) * WIDE] for j in range(2)]
        ps_w = [ps_a[1][:, j * WIDE:(j + 1) * WIDE] for j in range(2)]
        ps_agg = [ps_b[j][:, 0:WINDOW] for j in range(2)]
        ps_extra = ps_b[2]
        ps_first = ps_b[3][:, 0:HALF_TILES]
        ps_h, ps_c = ps_b[0:2], ps_b[2:4]
        ps_mean, ps_hrows, ps_xrows, ps_var = ps_z, ps_w, ps_b[0:2], [b[:, 0:4] for b in ps_b[2:4]]

        s_range_in, s_edges_in, s_const_in = sem("range_in"), sem("edges_in"), sem("const_in")
        s_x_in = [sem(f"x_in_{i}") for i in range(X_PARTS)]
        s_iota, s_setup = sem("iota_made"), sem("setup_step")
        s_groups_in, s_short, s_short_out = sem("source_groups_in"), sem("rows_shortened"), sem("short_rows_out")
        s_range_out, s_range_back = sem("range_stored"), sem("range_back")
        s_parts_in, s_bias_split = sem("bias_rows_in"), sem("bias_split")
        s_bn, s_bn_sd = [sem(f"bn_step_{i}") for i in range(2)], [sem(f"bn_sd_{i}") for i in range(2)]
        s_h_ready = [sem(f"h_ready_{i}") for i in range(2)]
        s_mm_done = [sem(f"transform_done_{i}") for i in range(2)]
        s_row_ready = [sem(f"rows_ready_{i}") for i in range(2)]
        s_row_out = [[sem(f"rows_out_{i}_{q}") for q in range(SLOTS)] for i in range(2)]
        s_clear = [sem(f"acc_cleared_{i}") for i in range(3)]
        s_turn = [sem(f"gather_turn_{i}") for i in range(3)]
        s_idx = [sem(f"idx_ready_{i}") for i in range(3)]
        s_gather = [[[sem(f"gathered_{i}_{h}_{j}") for j in range(2)] for h in range(2)] for i in range(3)]
        s_onehot = [sem(f"onehot_ready_{i}") for i in range(3)]
        s_agg = [sem(f"agg_ready_{i}") for i in range(3)]
        s_acc = [sem(f"acc_done_{i}") for i in range(3)]
        s_xoh = [sem(f"extra_onehot_{i}") for i in range(3)]
        s_xagg = [sem(f"extra_agg_{i}") for i in range(3)]
        s_xt_in = [sem(f"x_chunk_in_{q}") for q in range(4)]
        s_y, s_mean, s_yc, s_sq, s_var, s_sd, s_rsd = (sem(n) for n in (
            "y_done", "mean_ready", "centred", "squared", "variance_ready", "sd_done", "sd_inverted"))
        s_rows, s_x1, s_hrow = sem("rows_turned"), sem("x1_done"), sem("h_rows_ready")
        s_hout = [sem(f"h_rows_out_{q}") for q in range(2)]
        s_turn_act = sem("scalar_turn")
        s_ln, s_ln_sd = sem("ln_step"), sem("ln_sd")
        s_f_in = [sem(f"filter_in_{h}") for h in range(2)]
        s_z, s_act, s_soft, s_w, s_msg = (sem(n) for n in (
            "z_ready", "act_step", "soft_done", "filter_ready", "msg_done"))
        s_cut, s_xadd = sem("cutoff_staged"), sem("extra_added")
        s_src_in, s_dup, s_first, s_uniq = [sem(f"src_in_{h}") for h in range(2)], sem("dup_ready"), sem("first_ready"), sem("uniq_step")
        s_edge_in, s_win_in = [sem(f"edge_rows_in_{h}") for h in range(2)], [sem(f"h_window_in_{h}") for h in range(2)]
        s_spread, s_same, s_hexp, s_hcopy = sem("spread_ready"), sem("same_ready"), sem("h_edges_ready"), sem("h_edges_copied")
        s_comb, s_comb_out = sem("combined_ready"), sem("combined_copied")
        s_scat = [[sem(f"scattered_{h}_{j}") for j in range(2)] for h in range(2)]
        s_go = sem("scatter_turn")
        s_xh_in = sem("extra_h_in")
        s_zero, s_zeroed = sem("zeros_made"), sem("copies_zeroed")
        s_cp_in, s_cp_sum, s_cp_t, s_cp_out = [sem(f"copies_in_{i}") for i in range(3)], sem("copies_summed"), sem("sums_turned"), sem("sums_copied")
        s_fz, s_fact, s_fsoft, s_fo, s_fy, s_fst = (sem(n) for n in (
            "out_z_ready", "out_act_step", "out_soft_done", "out_ready", "out_y_done", "out_y_stats"))
        s_fin, s_fin_out = [sem(f"final_ready_{i}") for i in range(2)], [sem(f"final_out_{q}") for q in range(4)]

        block = ctx.enter_context(nc.Block())

        SLOT2 = 2

        @block.sync
        def _(sp):
            sp.dma_start(dst_groups, dram["dst_groups"].rearrange("p (g n) -> p g n", g=4)).then_inc(s_range_in, 16)
            for i in range(X_PARTS):
                part = slice(i * X_COLS, (i + 1) * X_COLS if i < X_PARTS - 1 else NPAD)
                sp.dma_start(buf_x[:, part], dram["xT"][:, part]).then_inc(s_x_in[i], 16)
            for t, name in ((gamma[0], "g1"), (beta[0], "be1"), (w_types[0], "w1T"), (gamma[1], "g2"),
                            (beta[1], "be2"), (w_types[1], "w2T"), (w_in, "W_in"), (wf2, "Wf2"),
                            (biases[:, 0], "bf2"), (biases[:, 1], "bo2"), (wo1, "Wo1"), (bo1, "bo1"), (wo2, "Wo2"), (first_w, "first_w")):
                sp.dma_start(t[:, :], dram[name]).then_inc(s_const_in, 16)
            sp.dma_start(wf1[0:RBF, :], dram["Wf1"]).then_inc(s_const_in, 16)
            sp.dma_start(wf1[RBF:RBF + 1, :], dram["bf1"]).then_inc(s_const_in, 16)
            for t, name, n in ((b_types[0], "b1", TD), (b_types[1], "b2", TD)):
                sp.dma_start(t[:, :], dram[name].broadcast_to([P, n])).then_inc(s_const_in, 16)
            sp.dma_start(src_groups, dram["src_groups"]).then_inc(s_groups_in, 16)
            for t, name in ((type_tiles, "etype"), (src_idx[:, :], "src"), (dst_tiles, "dst"), (cutoff[:, :], "cutoff")):
                sp.dma_start(t, dram[name]).then_inc(s_edges_in, 16)
            src_flat, dst_flat = (rows.rearrange("(o p) n -> o (p n)", o=1) for rows in (src_rows, dst_rows))

            for rnd in range(2):
                with sp.Fori(0, TRANS_ITERS) as r:
                    for j in range(BODY):
                        sp.wait_ge(s_row_ready[rnd], r * BODY + (j + 1 + SLOT2))
                        sp.dma_start(table[rnd][ds((r * BODY + j) * P, P), :],
                                     out_rows[:, j % SLOTS, :]).then_inc(s_row_out[rnd][j % SLOTS], 16)

                if rnd == 0:
                    sp.wait_ge(s_bias_split, 5)
                    for i in range(3):
                        sp.dma_start(bias_rows[i:i + 1, :, :], bias_parts[0:1, i, :, :]).then_inc(s_parts_in, 16)
                    sp.wait_ge(s_zero, 1)
                    for c, acc in enumerate(acc_rows):
                        flat = acc.rearrange("(p x) n -> p (x n)", p=P)
                        with sp.Fori(0, ZERO_STEPS) as q:
                            sp.wait_ge(s_idx[0], q + (c * ZERO_STEPS + 1))
                            sp.dma_start(flat[:, ds(q * ZERO_COLS, ZERO_COLS)], zeros).then_inc(s_zeroed, 16)
                else:
                    sp.wait_ge(s_short_out, 64)
                    sp.wait_ge(s_h_ready[1], BLOCKS)
                    sp.wait_ge(s_mm_done[1], BLOCKS + SLOT2)
                    for h in range(2):
                        sp.dma_start(src_bc[:, h, :], src_flat[0:1, h * COLS_HALF:(h + 1) * COLS_HALF]
                                     .broadcast_to([P, COLS_HALF])).then_inc(s_src_in[h], 16)
                    with sp.Fori(0, ITERS) as r:
                        for h in range(2):
                            sp.wait_ge(s_dup, r * 2 + (h + 1))
                            sp.dma_start(src_bc[:, h, :],
                                         src_flat[0:1, ds((r * 2 + (2 + h)) * COLS_HALF, COLS_HALF)]
                                         .broadcast_to([P, COLS_HALF])).then_inc(s_src_in[h], 16)
                    for h in range(2):
                        sp.wait_ge(s_src_in[h], 16 * (ITERS + 1))

            for q in range(SLOTS):
                sp.wait_ge(s_row_out[1][q], 16 * (BLOCKS // SLOTS + 1))

            def load_x(m, q):
                sp.dma_start(x_in[:, q, :], dram["xT"][:, ds(m * WIDE, WIDE)]).then_inc(s_xt_in[q], 16)

            def store_h(m, s):
                sp.wait_ge(s_hrow, m + (1 + SLOT2))
                sp.dma_start(htable[ds(m * WIDE, WIDE), :].rearrange("(b p) n -> p b n", p=P),
                             h_rows[:, s, :].rearrange("p (b n) -> p b n", b=4)).then_inc(s_hout[s], 16)

            for m in range(6):
                if m >= 4:
                    sp.wait_ge(s_y, m - 3)
                load_x(m, m % 4)
            full = (CHUNKS - 6) // 4
            with sp.Fori(0, full) as r:
                for j in range(4):
                    m = r * 4 + j
                    sp.wait_ge(s_y, m + 3)
                    load_x(m + 6, (j + 2) % 4)
                    store_h(m, j % 2)
            for m in range(4 * full, CHUNKS):
                store_h(m, m % 2)

            def load_attributes(h, half):
                sp.dma_start(f_sb[0:RBF, h, :, :], dram["attr"][ds(half * (2 * RBF), 2 * RBF), :]
                             .rearrange("(j r) n -> r j n", j=2)).then_inc(s_f_in[h], 16)

            def load_ends(h, half):
                for t, rows in ((dst_bc, dst_flat), (src_bc, src_flat)):
                    sp.dma_start(t[:, h, :], rows[0:1, ds(half * COLS_HALF, COLS_HALF)].broadcast_to([P, COLS_HALF])
                                 ).then_inc(s_edge_in[h], 16)

            def load_windows(h, bases):
                for j in range(2):
                    sp.dma_start(h_win[:, h, j, :], htable[ds(bases[j], WINDOW), :]).then_inc(s_win_in[h], 16)

            def load_bases(r):
                return nc.values_load_multi_w_load_instructions(
                    base_row[0:1, ds(r * 4, 4)], engines=[mybir.EngineType.SP], min_val=0, max_val=N - WINDOW,
                    skip_runtime_bounds_check_because="computed as a minimum with N - WINDOW")[1]

            for s in s_hout:
                sp.wait_ge(s, 16 * (CHUNKS // 2 + 1))
            bases = load_bases(0)
            flag = nc.sync.value_load(flag_i[0:1, 0:1], min_val=0, max_val=1)
            for h in range(2):
                load_attributes(h, h)
                load_ends(h, h)
                load_windows(h, bases[2 * h:2 * h + 2])
            with sp.Fori(0, ITERS) as r:
                bases = load_bases(r + 1)
                for h in range(2):
                    with sp.If(flag > 0):
                        with sp.Fori(0, 2) as j:
                            with sp.Fori(0, BLOCKS) as b:
                                step = ((r * 2 + h) * 2 + j) * BLOCKS + b
                                sp.wait_ge(s_xagg[2], step + 1)
                                sp.dma_start(x_h, htable[ds(b * P, P), :]).then_inc(s_xh_in, 16)
                    k = r * 2 + h
                    sp.wait_ge(s_z, k * 2 + 2)
                    load_attributes(h, k + 2)
                    sp.wait_ge(s_same, k + 1)
                    load_ends(h, k + 2)
                    sp.wait_ge(s_hexp, k * 2 + 2)
                    load_windows(h, bases[2 * h:2 * h + 2])
            for h in range(2):
                sp.wait_ge(s_f_in[h], 16 * (ITERS + 1))
                sp.wait_ge(s_edge_in[h], 32 * (ITERS + 1))
                sp.wait_ge(s_win_in[h], 32 * (ITERS + 1))

            def load_copies(m, q):
                for c in range(COPIES):
                    sp.dma_start(copy_rows[:, q, c, :].rearrange("p (b n) -> p b n", b=4),
                                 acc_rows[c][ds(m * WIDE, WIDE), :].rearrange("(b p) n -> p b n", p=P)
                                 ).then_inc(s_cp_in[q], 16)

            def reload_copies(m, q):
                sp.wait_ge(s_cp_t, m + 1)
                load_copies(m + 3, q)

            for h in range(2):
                for j in range(2):
                    sp.wait_ge(s_scat[h][j], 64 * ITERS)
            for q in range(3):
                load_copies(q, q)
            full = (CHUNKS - 3) // 3
            with sp.Fori(0, full) as r:
                for q in range(3):
                    reload_copies(r * 3 + q, q)
            for m in range(3 * full, CHUNKS - 3):
                reload_copies(m, m % 3)

            def store_rows(m, q, count):
                sp.wait_ge(s_fin[q % 2], count)
                sp.dma_start(out[ds(m * WIDE, WIDE), :].rearrange("(b p) n -> p b n", p=P),
                             final_rows[:, q, :].rearrange("p (b n) -> p b n", b=4)).then_inc(s_fin_out[q], 16)

            with sp.Fori(0, CHUNKS // 4) as r:
                for q in range(4):
                    store_rows(r * 4 + q, q, r * 2 + (q // 2 + 1))
            for m in range(CHUNKS // 4 * 4, CHUNKS):
                store_rows(m, m % 4, m // 2 + 1)
            for q in range(3):
                sp.wait_ge(s_cp_in[q], 16 * COPIES * len(range(q, CHUNKS, 3)))
            for q in range(4):
                sp.wait_ge(s_fin_out[q], 16 * (len(range(q, CHUNKS, 4)) + 1))

        @block.gpsimd
        def _(pool):
            nc.gpsimd.iota(iota_i, [[1, WIDE]], base=0, channel_multiplier=0).then_inc(s_iota, 1)
            nc.gpsimd.iota(part_i[:, :], [[0, 1]], base=0, channel_multiplier=1).then_inc(s_iota, 1)

            def gather_pass(p, source, last_wait):
                for s, v in last_wait:
                    pool.wait_ge(s, v)
                with pool.Fori(0, ITERS) as r:
                    for h in range(2):
                        pool.wait_ge(s_idx[p], r * 2 + (h + 1))
                        pool.sem_inc(s_turn[p], 1)
                        for t in range(HALF_TILES):
                            nc.gpsimd.indirect_dma_start(
                                gathered[:, h, t, :], None, source,
                                bass.IndirectOffsetOnAxis(ap=idx_stage[:, h, t:t + 1], axis=0),
                            ).then_inc(s_gather[p][h][t // GROUP_TILES], 16)

            pool.wait_ge(s_setup, 4)
            nc.gpsimd.dma_start(base_dram, range_i[:, 0, :]).then_inc(s_range_out, 16)
            nc.gpsimd.dma_start(span_dram, range_i[:, 1, :]).then_inc(s_range_out, 16)
            nc.gpsimd.tensor_tensor(dst_groups, dst_groups,
                                    range_i[:, 0, :].unsqueeze(2).broadcast_to([RANGE_PARTS, 4, GROUP_EDGES]),
                                    ALU.subtract).then_inc(s_short, 1)
            pool.wait_ge(s_short, 1)
            nc.gpsimd.tensor_copy(dst_short.rearrange("p (g n) -> p g n", g=4), dst_groups).then_inc(s_short, 1)
            pool.wait_ge(s_range_out, 32)
            base_flat = base_dram.rearrange("(o p) g -> o (p g)", o=1)
            span_flat = span_dram.rearrange("(o p) g -> o (p g)", o=1)
            nc.gpsimd.dma_start(base_row[0:1, 0:GROUPS], base_flat).then_inc(s_range_back, 16)
            nc.gpsimd.dma_start(base_bc[:, :], base_flat.broadcast_to([P, GROUPS])).then_inc(s_range_back, 16)
            nc.gpsimd.dma_start(span_bc[:, :], span_flat.broadcast_to([P, GROUPS])).then_inc(s_range_back, 16)
            pool.wait_ge(s_groups_in, 16)
            nc.gpsimd.tensor_copy(src_short, src_groups).then_inc(s_short, 1)
            pool.wait_ge(s_short, 3)
            for rows, short in ((dst_rows, dst_short), (src_rows, src_short)):
                nc.gpsimd.dma_start(rows[0:RANGE_PARTS, :], short).then_inc(s_short_out, 16)
                nc.gpsimd.dma_start(rows[RANGE_PARTS:RANGE_PARTS + 1, :], short[0:1, :]).then_inc(s_short_out, 16)
            pool.wait_ge(s_short_out, 64)
            nc.gpsimd.memset(buf_a[:, :], 0.0).then_inc(s_clear[0], 1)
            for rnd in range(2):
                if rnd == 1:
                    pool.wait_ge(s_h_ready[0], BLOCKS)
                    nc.gpsimd.memset(buf_x[:, :], 0.0).then_inc(s_clear[1], 1)
                gather_pass(rnd, table[rnd].rearrange("n (t d) -> (n t) d", t=T),
                            [(s_row_out[rnd][q], 16 * (BLOCKS // SLOTS + 1)) for q in range(SLOTS)])
            pool.wait_ge(s_zeroed, 16 * COPIES * ZERO_STEPS)
            def scatter_sums(r, first):
                for h in range(2):
                    for j in range(2):
                        pool.wait_ge(s_idx[2], r * 2 + (h + 1))
                        pool.wait_ge(s_comb_out, r * 4 + (2 * h + j + 1 + SLOT2))
                        if h == 1 or not first:
                            pool.wait_ge(s_scat[1 - h][j], r * 64 + 64 * h)
                        pool.sem_inc(s_go, 1)
                        for t in range(j * GROUP_TILES, (j + 1) * GROUP_TILES):
                            nc.gpsimd.indirect_dma_start(
                                acc_rows[t], bass.IndirectOffsetOnAxis(ap=idx_stage[:, h, t:t + 1], axis=0),
                                gathered[:, h, t, :], None, compute_op=ALU.add,
                            ).then_inc(s_scat[h][j], 16)

            scatter_sums(0, True)
            with pool.Fori(1, ITERS) as r:
                scatter_sums(r, False)

        @block.scalar
        def _(act):
            for rnd in range(2):
                feat = buf_x if rnd == 0 else buf_a
                act.wait_ge(s_bn[rnd], N // BN_CHUNK + 1)
                nc.scalar.activation(bn_tmp[:, 0:1], bn_mv[:, 1:2], ACT.Sqrt, bias=eps_col[:, 0:1]).then_inc(s_bn_sd[rnd], 1)
                act.wait_ge(s_bn[rnd], N // BN_CHUNK + 5)
                with act.Fori(0, TRANS_ITERS) as r:
                    for j in range(BODY):
                        act.wait_ge(s_mm_done[rnd], r * BODY + (j + 1))
                        nc.scalar.activation(h_stage[:, j % 2, :], feat[:, ds((r * BODY + j) * P, P)], ACT.Relu,
                                             bias=bn_shift[:, 0:1], scale=bn_scale[:, 0:1]).then_inc(s_h_ready[rnd], 1)

            def square(m, s):
                act.wait_ge(s_yc, m + (1 + SLOT2))
                act.wait_ge(s_var, m + 1)
                nc.scalar.activation(squares[:, s, :], centred[:, s, :], ACT.Square).then_inc(s_sq, 1)

            def deviation(m, s):
                act.wait_ge(s_var, m + (1 + SLOT2))
                act.wait_ge(s_rsd, m + 1)
                nc.scalar.activation(sd[:, s, :], ps_var[s], ACT.Sqrt, bias=eps_col[:, 0:1]).then_inc(s_sd, 1)

            with act.Fori(0, CHUNKS // 2) as r:
                for s in range(2):
                    square(r * 2 + s, s)
                    deviation(r * 2 + s, s)

            def softplus_half(k):
                for j in range(2):
                    act.wait_ge(s_z, k * 2 + (j + 1))
                    act.wait_ge(s_act, k * 6 + 1)
                    nc.scalar.activation(abs_z[:, j, :], ps_z[j], ACT.Abs).then_inc(s_act, 1)
                for j in range(2):
                    act.wait_ge(s_act, k * 6 + (2 + j))
                    nc.scalar.activation(abs_z[:, j, :], abs_z[:, j, :], ACT.Exp, scale=-1.0).then_inc(s_act, 1)
                for j in range(2):
                    act.wait_ge(s_act, k * 6 + (4 + j))
                    act.wait_ge(s_soft, k * 2 + SLOT2)
                    nc.scalar.activation(log_z[:, j, :], abs_z[:, j, :], ACT.Ln, bias=half_col[:, 0:1],
                                         scale=0.5).then_inc(s_act, 1)

            def convolution_step(r, first):
                for h in range(2):
                    k = r * 2 + h
                    for j in range(2):
                        act.wait_ge(s_hexp, k * 2 + (j + 1))
                        act.wait_ge(s_msg, k * 2 + (j + 1))
                        nc.scalar.activation(h_edge[:, j, :], ps_h[j][:, :], ACT.Copy).then_inc(s_hcopy, 1)
                    softplus_half(k + 1)
                    for j in range(2):
                        act.wait_ge(s_comb, k * 2 + (j + 1 + SLOT2))
                        if not first:
                            act.wait_ge(s_scat[h][j], r * 64)
                        nc.scalar.activation(combined[:, h, j * WIDE:(j + 1) * WIDE], ps_c[j][:, :],
                                             ACT.Copy).then_inc(s_comb_out, 1)

            nc.scalar.add_instruction(mybir.InstLoadActFuncSet(
                name=nc.get_next_instruction_name(), engine=mybir.EngineType.Activation, act_func_set_id=EXP_LN_SET))
            softplus_half(0)
            convolution_step(0, True)
            with act.Fori(1, ITERS) as r:
                convolution_step(r, False)

            def copy_turned(m, s):
                act.wait_ge(s_cp_t, m + 1)
                act.wait_ge(s_fz, m + 1)
                nc.scalar.activation(out_t[:, s, :], ps_b[s][:, :], ACT.Copy).then_inc(s_cp_out, 1)

            def out_softplus(m, s):
                act.wait_ge(s_fz, m + (1 + SLOT2))
                act.wait_ge(s_fact, m * 4 + 1)
                nc.scalar.activation(abs_z[:, s, :], ps_z[s], ACT.Abs, bias=bo1[:, 0:1]).then_inc(s_fact, 1)
                act.wait_ge(s_fsoft, m + 1)
                nc.scalar.activation(relu_z[:, s, :], ps_z[s], ACT.Relu, bias=bo1[:, 0:1]).then_inc(s_fact, 1)
                act.wait_ge(s_fact, m * 4 + 2)
                nc.scalar.activation(abs_z[:, s, :], abs_z[:, s, :], ACT.Exp, scale=-1.0).then_inc(s_fact, 1)
                act.wait_ge(s_fact, m * 4 + 4)
                nc.scalar.activation(log_z[:, s, :], abs_z[:, s, :], ACT.Ln, bias=half_col[:, 0:1],
                                     scale=0.5).then_inc(s_fact, 1)

            def copy_y(m, s):
                act.wait_ge(s_fo, m + (1 + SLOT2))
                act.sem_inc(s_turn_act, 1)
                nc.scalar.activation(buf_x[:, ds(m * WIDE, WIDE)], ps_w[s], ACT.Copy).then_inc(s_fy, 1)

            def output_step(m, j):
                s = j % 2
                if j + 1 < CHUNKS:
                    out_softplus(m + 1, 1 - s)
                copy_y(m, s)
                if j + 2 < CHUNKS:
                    copy_turned(m + 2, s)

            for m in range(2):
                copy_turned(m, m)
            out_softplus(0, 0)
            with act.Fori(0, LOOP6) as r:
                for j in range(6):
                    output_step(r * 6 + j, j)
            for m in range(6 * LOOP6, CHUNKS):
                output_step(m, m)
            act.wait_ge(s_ln, 6)
            nc.scalar.activation(ln_tmp[:, 0, :], ln_tmp[:, 1, :], ACT.Sqrt, bias=eps_col[:, 0:1]).then_inc(s_ln_sd, 1)

            def normalise(m, q, stored):
                act.wait_ge(s_fin_out[q], stored)
                act.sem_inc(s_turn_act, 1)
                for b in range(4):
                    last = nc.scalar.activation(final_rows[:, q, b * P:(b + 1) * P], buf_x[:, ds(m * WIDE + b * P, P)],
                                                ACT.Identity, bias=ln_shift[:, ds(m * 4 + b, 1)],
                                                scale=ln_rstd[:, ds(m * 4 + b, 1)])
                last.then_inc(s_fin[1], 1)

            act.wait_ge(s_ln, 9)
            with act.Fori(0, CHUNKS // 4) as r:
                for q in (1, 3):
                    normalise(r * 4 + q, q, r * 16 + 16)
            for m in range(CHUNKS // 4 * 4 + 1, CHUNKS, 2):
                normalise(m, m % 4, 16 * (m // 4 + 1))

        @block.vector
        def _(dve):
            chain_sem, chain_at = None, 0

            def begin_chain(s, at=0):
                nonlocal chain_sem, chain_at
                chain_sem, chain_at = s, at

            def link(ins):
                nonlocal chain_at
                chain_at += 1
                ins.then_inc(chain_sem, 1)
                dve.wait_ge(chain_sem, chain_at)

            begin_chain(s_setup)
            dve.wait_ge(s_range_in, 16)
            link(nc.vector.tensor_reduce(range_f[:, 0, :], dst_groups, AX.X, ALU.min))
            link(nc.vector.tensor_reduce(range_f[:, 1, :], dst_groups, AX.X, ALU.max))
            link(nc.vector.tensor_scalar(range_i[:, 0, :], range_f[:, 0, :], float(N - WINDOW), None, ALU.min))
            link(nc.vector.tensor_tensor(range_i[:, 1, :], range_f[:, 1, :], range_i[:, 0, :], ALU.subtract))
            link(nc.vector.memset(eps_col[:, :], EPS))

            def set_up():
                begin_chain(s_setup, 5)
                dve.wait_ge(s_edges_in, 64)
                link(nc.vector.scalar_tensor_tensor(out=msg_idx[:, :], in0=src_idx[:, :], scalar=float(T), in1=type_tiles,
                                                    op0=ALU.mult, op1=ALU.add))
                for h in range(2):
                    stage_indices(0, 0, h)
                dve.wait_ge(s_range_back, 48)
                link(nc.vector.tensor_tensor(dst_local[:, 0:TILES].rearrange("p (g t) -> p g t", t=GROUP_TILES),
                                             dst_tiles[:, 0:TILES].rearrange("p (g t) -> p g t", t=GROUP_TILES),
                                             base_bc[:, :].unsqueeze(2).broadcast_to([P, GROUPS, GROUP_TILES]),
                                             ALU.subtract))
                full, rest = divmod(E, P)
                if rest:
                    link(nc.vector.memset(dst_local[rest:P, full:full + 1], -1.0))
                link(nc.vector.memset(dst_local[:, -(-E // P):COLS], -1.0))
                link(nc.vector.tensor_reduce(flag_f[:, :], span_bc[:, :], AX.X, ALU.max))
                link(nc.vector.tensor_scalar(flag_i[:, :], flag_f[:, :], float(WINDOW), None, ALU.is_ge))
                dve.wait_ge(s_iota, 2)
                link(nc.vector.tensor_copy(iota_f[:, :], iota_i))
                link(nc.vector.tensor_copy(part_f[:, :], part_i[:, :]))
                link(nc.vector.tensor_scalar(ident[:, :], iota_f[:, 0:P], part_f[:, 0:1], None, ALU.is_equal))
                link(nc.vector.memset(half_col[:, :], 0.5))
                link(nc.vector.memset(ones_d[:, :], 1.0 / D))
                link(nc.vector.memset(ones_rows[:, :], 1.0))
                link(nc.vector.tensor_scalar(trash_row[:, :], part_f[:, :], float(NPAD), None, ALU.add))
                link(nc.vector.memset(base_row[0:1, GROUPS:GROUPS + 4], 0))
                begin_chain(s_bias_split)
                rest = biases[:, :, :]
                for i in range(3):
                    link(nc.vector.tensor_copy(bias_parts[0:1, i, :, :], rest))
                    if i < 2:
                        link(nc.vector.tensor_tensor(bias_rest[0:1, i, :, :], rest, bias_parts[0:1, i, :, :], ALU.subtract))
                        rest = bias_rest[0:1, i, :, :]
                return nc.vector.value_load(flag_i[0:1, 0:1], min_val=0, max_val=1)

            def batch_norm(rnd, feat):
                begin_chain(s_bn[rnd])
                for c in range(N // BN_CHUNK):
                    if rnd == 0 and c % (X_COLS // BN_CHUNK) == 0:
                        dve.wait_ge(s_x_in[c * BN_CHUNK // X_COLS], 16)
                    nc.vector.bn_stats(bn_raw[:, c, :], feat[:, c * BN_CHUNK:(c + 1) * BN_CHUNK]).then_inc(s_bn[rnd], 1)
                begin_chain(s_bn[rnd], N // BN_CHUNK)
                dve.wait_ge(s_bn[rnd], N // BN_CHUNK)
                link(nc.vector.bn_aggr(bn_mv[:, :], bn_raw[:, :, :].rearrange("p c s -> p (c s)")))
                dve.wait_ge(s_bn_sd[rnd], 1)
                dve.wait_ge(s_const_in, 18 * 16)
                link(nc.vector.reciprocal(bn_tmp[:, 1:2], bn_tmp[:, 0:1]))
                link(nc.vector.tensor_tensor(bn_scale[:, :], gamma[rnd][:, :], bn_tmp[:, 1:2], ALU.mult))
                link(nc.vector.tensor_tensor(bn_tmp[:, 1:2], bn_scale[:, :], bn_mv[:, 0:1], ALU.mult))
                link(nc.vector.tensor_tensor(bn_shift[:, :], beta[rnd][:, :], bn_tmp[:, 1:2], ALU.subtract))

            def message_rows(rnd):
                with dve.Fori(0, TRANS_ITERS) as r:
                    for j in range(BODY):
                        dve.wait_ge(s_mm_done[rnd], r * BODY + (j + 1 + SLOT2))
                        dve.wait_ge(s_row_out[rnd][j % SLOTS], r * (16 * BODY // SLOTS) + 16 * (j // SLOTS + 1))
                        nc.vector.tensor_tensor(out_rows[:, j % SLOTS, :], ps_a[j % 2][:, 0:TD], b_types[rnd][:, :],
                                                ALU.add).then_inc(s_row_ready[rnd], 1)

            def stage_indices(p, it, h):
                rows = msg_idx if p < 2 else uniq_idx
                nc.vector.tensor_copy(idx_stage[:, h, :],
                                      rows[:, ds(it * ITER_TILES + h * HALF_TILES, HALF_TILES)]
                                      ).then_inc(s_idx[p], 1)

            def build_onehot(p, it, h):
                shape = [P, HALF_TILES, WINDOW]
                nc.vector.tensor_tensor(
                    onehot[:, h, :, :], iota_f[:, 0:WINDOW].unsqueeze(1).broadcast_to(shape),
                    dst_local[:, ds(it * ITER_TILES + h * HALF_TILES, HALF_TILES)].unsqueeze(2).broadcast_to(shape),
                    ALU.is_equal).then_inc(s_onehot[p], 1)

            def same_source(it, h, signal):
                shape = [P, HALF_TILES, P]
                nc.vector.tensor_tensor(
                    same_src[:, h, :, :], src_bc[:, h, :].rearrange("p (t n) -> p t n", t=HALF_TILES),
                    src_idx[:, ds(it * ITER_TILES + h * HALF_TILES, HALF_TILES)].unsqueeze(2).broadcast_to(shape),
                    ALU.is_equal).then_inc(signal, 1)

            def output_rows(r, h):
                k = r * 2 + h
                src = src_idx[:, ds(r * ITER_TILES + h * HALF_TILES, HALF_TILES)]
                nc.vector.tensor_scalar(to_trash, src, -1.0, trash_row[:, 0:1], ALU.mult, ALU.add).then_inc(s_uniq, 1)
                dve.wait_ge(s_first, k + 1)
                dve.wait_ge(s_uniq, k * 3 + 2)
                nc.vector.scalar_tensor_tensor(out=to_trash, in0=ps_first, scalar=first_w[:, 1:2], in1=to_trash,
                                               op0=ALU.is_ge, op1=ALU.mult).then_inc(s_uniq, 1)
                dve.wait_ge(s_uniq, k * 3 + 3)
                nc.vector.tensor_tensor(uniq_idx[:, ds(r * ITER_TILES + h * HALF_TILES, HALF_TILES)], src, to_trash,
                                        ALU.add).then_inc(s_uniq, 1)
                dve.wait_ge(s_uniq, k * 3 + 4)

            def accumulate(p, acc, r, h, bases):
                for j in range(2):
                    g = r * 4 + (2 * h + j)
                    dve.wait_ge(s_agg[p], g + 1)
                    dve.wait_ge(s_acc[p], g + SLOT2)
                    at = acc[:, ds(bases[2 * h + j], WINDOW)]
                    nc.vector.tensor_tensor(at, at, ps_agg[j], ALU.add).then_inc(s_acc[p], 1)

            def beyond_window(p, acc, r, h):
                with dve.If(flag > 0):
                    for j in range(2):
                        g = r * 4 + (2 * h + j)
                        cols = dst_local[:, ds(g * GROUP_TILES, GROUP_TILES)]
                        nc.vector.drain()
                        nc.vector.tensor_tensor(x_rem[:, :], cols,
                                                base_bc[:, ds(g, 1)].broadcast_to([P, GROUP_TILES]), ALU.add)
                        nc.vector.drain()
                        nc.vector.tensor_scalar(x_rem[:, :], x_rem[:, :], 1.0, None, ALU.add)
                        nc.vector.drain()
                        nc.vector.scalar_tensor_tensor(out=x_rem[:, :], in0=cols, scalar=float(WINDOW),
                                                       in1=x_rem[:, :], op0=ALU.is_ge, op1=ALU.mult)
                        nc.vector.drain()
                        nc.vector.tensor_scalar(x_rem[:, :], x_rem[:, :], -1.0, None, ALU.add)
                        with dve.Fori(0, WIDE_STEPS) as b:
                            step = g * WIDE_STEPS + b
                            nc.vector.drain()
                            for t in range(GROUP_TILES):
                                last = nc.vector.tensor_scalar(x_onehot[:, t, :], iota_f[:, :], x_rem[:, t:t + 1],
                                                               None, ALU.is_equal)
                            last.then_inc(s_xoh[p], 1)
                            nc.vector.drain()
                            nc.vector.tensor_scalar(x_rem[:, :], x_rem[:, :], float(-WIDE), None, ALU.add)
                            dve.wait_ge(s_xagg[p], step + 1)
                            at = acc[:, ds(b * WIDE, WIDE)]
                            nc.vector.tensor_tensor(at, at, ps_extra[:, :], ALU.add)
                        nc.vector.drain()

            def load_bases(r):
                return nc.values_load_multi_w_load_instructions(
                    base_row[0:1, ds(r * 4, 4)], engines=[mybir.EngineType.DVE], min_val=0, max_val=N - WINDOW,
                    skip_runtime_bounds_check_because="computed as a minimum with N - WINDOW")[1]

            def round_pass(p, acc):
                dve.wait_ge(s_clear[p], 1)
                if p == 1:
                    for h in range(2):
                        stage_indices(p, 0, h)
                build_onehot(p, 0, 0)
                with dve.Fori(0, ITERS) as r:
                    bases = load_bases(r)
                    for h in range(2):
                        build_onehot(p, r + h, 1 - h)
                        if p == 1:
                            dve.wait_ge(s_src_in[h], r * 16 + 16)
                            same_source(r, h, s_dup)
                        accumulate(p, acc, r, h, bases)
                        beyond_window(p, acc, r, h)
                        if p == 1:
                            output_rows(r, h)
                        stage_indices(p, r + 1, h)

            batch_norm(0, buf_x)
            message_rows(0)
            flag = set_up()
            for q in range(SLOTS):
                dve.wait_ge(s_row_out[0][q], 16 * (BLOCKS // SLOTS + 1))
            nc.vector.memset(zeros, 0.0).then_inc(s_zero, 1)
            round_pass(0, buf_a)
            dve.wait_ge(s_acc[0], GROUPS + SLOT2)
            dve.wait_ge(s_zeroed, 16 * COPIES * ZERO_STEPS)
            batch_norm(1, buf_a)
            message_rows(1)
            round_pass(1, buf_x)

            def y_chunk(m, q, loaded):
                dve.wait_ge(s_xt_in[q], loaded)
                chunk = buf_x[:, ds(m * WIDE, WIDE)]
                nc.vector.scalar_tensor_tensor(out=chunk, in0=x_in[:, q, :], scalar=2.0, in1=chunk, op0=ALU.mult,
                                               op1=ALU.add).then_inc(s_y, 1)

            def centre(m, s):
                dve.wait_ge(s_mean, m + 1)
                dve.wait_ge(s_rows, m + 1)
                dve.wait_ge(s_sq, m + 1)
                nc.vector.tensor_tensor(centred[:, s, :], buf_x[:, ds(m * WIDE, WIDE)], ps_mean[s],
                                        ALU.subtract).then_inc(s_yc, 1)

            def scale_rows(m, s, stored):
                dve.wait_ge(s_sd, m + (1 + SLOT2))
                nc.vector.reciprocal(rstd[:, s, :], sd[:, s, :]).then_inc(s_rsd, 1)
                dve.wait_ge(s_rsd, m + (1 + SLOT2))
                dve.wait_ge(s_rows, m + (1 + SLOT2))
                dve.wait_ge(s_hout[s], stored)
                blocks = "p (b n) -> p b n"
                by_row = rstd[:, s, :].unsqueeze(2).broadcast_to([P, 4, D])
                nc.vector.tensor_tensor(h_rows[:, s, :].rearrange(blocks, b=4), ps_hrows[s].rearrange(blocks, b=4), by_row,
                                        ALU.mult).then_inc(s_hrow, 1)
                nc.vector.tensor_tensor(buf_x[:, ds(m * WIDE, WIDE)].rearrange(blocks, b=4),
                                        ps_xrows[s][:, :].rearrange(blocks, b=4), by_row, ALU.mult).then_inc(s_x1, 1)

            dve.wait_ge(s_acc[1], GROUPS + SLOT2)
            y_chunk(0, 0, 16)
            y_chunk(1, 1, 16)
            centre(0, 0)
            with dve.Fori(0, CHUNKS // 4) as r:
                for j in range(4):
                    m = r * 4 + j
                    y_chunk(m + 2, (j + 2) % 4, r * 16 + 16 * ((j + 2) // 4 + 1))
                    centre(m + 1, (j + 1) % 2)
                    scale_rows(m, j % 2, r * 32 + 16 * (j // 2 + 1))
            for m in range(CHUNKS // 4 * 4, CHUNKS):
                if m + 1 < CHUNKS:
                    centre(m + 1, (m + 1) % 2)
                scale_rows(m, m % 2, 16 * (m // 2 + 1))

            def soft_half(k):
                for j in range(2):
                    dve.wait_ge(s_act, k * 6 + (6 + j))
                    nc.vector.scalar_tensor_tensor(out=soft[:, j, :], in0=ps_z[j], scalar=0.0,
                                                   in1=log_z[:, j, :], op0=ALU.max, op1=ALU.add).then_inc(s_soft, 1)

            def spread_half(it, h):
                dve.wait_ge(s_edge_in[h], it * 32 + 32)
                for j in range(2):
                    nc.vector.tensor_scalar(spread[:, h, j * WIDE:(j + 1) * WIDE], dst_bc[:, h, j * WIDE:(j + 1) * WIDE],
                                            part_f[:, 0:1], None, ALU.is_equal).then_inc(s_spread, 1)

            def stage_cutoff(it, h):
                nc.vector.tensor_copy(cut_stage[:, h, :],
                                      cutoff[:, ds(it * ITER_TILES + h * HALF_TILES, HALF_TILES)]).then_inc(s_cut, 1)

            def spread_beyond(r, h):
                with dve.If(flag > 0):
                    with dve.Fori(0, 2) as j:
                        g = r * 4 + 2 * h + j
                        dst = dst_bc[:, h, ds(j * WIDE, WIDE)]
                        nc.vector.drain()
                        nc.vector.tensor_scalar(x_rem[:, 0:1], base_bc[:, ds(g, 1)], 1.0, None, ALU.add)
                        nc.vector.drain()
                        nc.vector.tensor_scalar(x_onehot[:, 0, :], dst, x_rem[:, 0:1], None, ALU.add)
                        nc.vector.drain()
                        nc.vector.scalar_tensor_tensor(out=x_dst, in0=dst, scalar=float(WINDOW), in1=x_onehot[:, 0, :],
                                                       op0=ALU.is_ge, op1=ALU.mult)
                        nc.vector.drain()
                        nc.vector.tensor_scalar(x_dst, x_dst, -1.0, None, ALU.add)
                        with dve.Fori(0, BLOCKS) as b:
                            step = g * BLOCKS + b
                            nc.vector.drain()
                            nc.vector.tensor_scalar(x_onehot[:, 0, :], x_dst, part_f[:, 0:1], None,
                                                    ALU.is_equal).then_inc(s_xoh[2], 1)
                            nc.vector.drain()
                            nc.vector.tensor_scalar(x_dst, x_dst, float(-P), None, ALU.add)
                            dve.wait_ge(s_xagg[2], step + 2)
                            at = h_edge[:, ds(j, 1), :].rearrange("p o n -> p (o n)")
                            nc.vector.tensor_tensor(at, at, ps_c[0][:, :], ALU.add).then_inc(s_xadd, 1)
                    nc.vector.drain()

            def convolution_step(r, first):
                for h in range(2):
                    k = r * 2 + h
                    spread_half(r + h, 1 - h)
                    dve.wait_ge(s_comb, k * 2 + SLOT2)
                    same_source(r + h, 1 - h, s_same)
                    dve.wait_ge(s_hcopy, k * 2 + (2 + SLOT2))
                    stage_cutoff(r + h, 1 - h)
                    spread_beyond(r, h)
                    dve.wait_ge(s_cut, k + 2)
                    for j in range(2):
                        dve.wait_ge(s_w, k * 2 + (j + 1))
                        for t in range(GROUP_TILES):
                            tile = slice(t * D, (t + 1) * D)
                            last = nc.vector.scalar_tensor_tensor(
                                out=msg[:, j, tile], in0=ps_w[j][:, tile],
                                scalar=cut_stage[:, h, j * GROUP_TILES + t:j * GROUP_TILES + t + 1],
                                in1=h_edge[:, j, tile], op0=ALU.mult, op1=ALU.mult)
                        last.then_inc(s_msg, 1)
                    if not first:
                        for j in range(2):
                            dve.wait_ge(s_scat[h][j], r * 64)
                    stage_indices(2, r, h)
                    soft_half(k + 1)

            nc.vector.memset(f_sb[RBF:RBF + 1, :, :, :], 1.0).then_inc(s_cut, 1)
            stage_cutoff(0, 0)
            dve.wait_ge(s_cut, 2)
            for s in s_hout:
                dve.wait_ge(s, 16 * (CHUNKS // 2 + 1))
            spread_half(0, 0)
            same_source(0, 0, s_same)
            soft_half(0)
            convolution_step(0, True)
            with dve.Fori(1, ITERS) as r:
                convolution_step(r, False)

            def sum_copies(m, q, loaded):
                dve.wait_ge(s_cp_in[q], loaded)
                half, step = COPIES, 0
                while half > 2:
                    half //= 2
                    step += 1
                    if step > 1:
                        dve.wait_ge(s_cp_sum, m * SUM_STEPS + (step - 1))
                    nc.vector.tensor_tensor(copy_rows[:, q, 0:half, :], copy_rows[:, q, 0:half, :],
                                            copy_rows[:, q, half:2 * half, :], ALU.add).then_inc(s_cp_sum, 1)

            def row_statistics(m):
                dve.wait_ge(s_fy, m + (1 + SLOT2))
                for b in range(4):
                    nc.vector.bn_stats(ln_raw[:, ds(m * 4 + b, 1), :].rearrange("p o s -> p (o s)"),
                                       buf_x[:, ds(m * WIDE + b * P, P)]).then_inc(s_fst, 1)

            def out_soft(m, s):
                dve.wait_ge(s_fact, m * 4 + 5)
                nc.vector.tensor_tensor(soft[:, s, :], log_z[:, s, :], relu_z[:, s, :], ALU.add).then_inc(s_fsoft, 1)

            def output_step(m, j, loaded):
                s = j % 2
                if j + 2 < CHUNKS:
                    sum_copies(m + 2, (j + 2) % 3, loaded)
                row_statistics(m)
                if j + 1 < CHUNKS:
                    out_soft(m + 1, 1 - s)

            LOADED = 16 * COPIES
            sum_copies(0, 0, LOADED)
            sum_copies(1, 1, LOADED)
            out_soft(0, 0)
            with dve.Fori(0, LOOP6) as r:
                for j in range(6):
                    output_step(r * 6 + j, j, r * (2 * LOADED) + LOADED * ((j + 2) // 3 + 1))
            for m in range(6 * LOOP6, CHUNKS):
                output_step(m, m, LOADED * ((m + 2) // 3 + 1))
            dve.wait_ge(s_fst, 4 * CHUNKS)
            begin_chain(s_ln)
            me, mo, qe, qo = (ln_raw[:, :, i] for i in (1, 4, 2, 5))
            a, v = ln_tmp[:, 0, :], ln_tmp[:, 1, :]
            link(nc.vector.tensor_tensor(a, me, mo, ALU.subtract))
            link(nc.vector.tensor_tensor(ln_mean[:, :], me, mo, ALU.add))
            link(nc.vector.tensor_tensor(v, qe, qo, ALU.add))
            link(nc.vector.scalar_tensor_tensor(out=a, in0=a, scalar=D / 4.0, in1=a, op0=ALU.mult, op1=ALU.mult))
            link(nc.vector.tensor_tensor(v, v, a, ALU.add))
            link(nc.vector.tensor_scalar(v, v, 1.0 / D, None, ALU.mult))
            dve.wait_ge(s_ln_sd, 1)
            link(nc.vector.reciprocal(ln_rstd[:, :], a))
            link(nc.vector.tensor_scalar(ln_mean[:, :], ln_mean[:, :], 0.5, None, ALU.mult))
            link(nc.vector.scalar_tensor_tensor(out=ln_shift[:, :], in0=ln_mean[:, :], scalar=-1.0, in1=ln_rstd[:, :],
                                                op0=ALU.mult, op1=ALU.mult))

            def normalise(m, q, stored):
                dve.wait_ge(s_fin_out[q], stored)
                for b in range(4):
                    last = nc.vector.tensor_scalar(final_rows[:, q, b * P:(b + 1) * P], buf_x[:, ds(m * WIDE + b * P, P)],
                                                   ln_mean[:, ds(m * 4 + b, 1)], ln_rstd[:, ds(m * 4 + b, 1)],
                                                   ALU.subtract, ALU.mult)
                last.then_inc(s_fin[0], 1)

            with dve.Fori(0, CHUNKS // 4) as r:
                for q in (0, 2):
                    normalise(r * 4 + q, q, r * 16 + 16)
            for m in range(CHUNKS // 4 * 4, CHUNKS, 2):
                normalise(m, m % 4, 16 * (m // 4 + 1))

        @block.tensor
        def _(pe):
            for rnd in range(2):
                pe.sem_inc(s_mm_done[rnd], SLOT2)
                pe.sem_inc(s_row_ready[rnd], SLOT2)
                for q in range(SLOTS):
                    pe.sem_inc(s_row_out[rnd][q], 16)
            for p in range(2):
                pe.sem_inc(s_acc[p], SLOT2)
            for s in s_hout + s_fin_out:
                pe.sem_inc(s, 16)
            for s in (s_yc, s_sq, s_var, s_sd, s_rsd, s_rows, s_x1, s_hrow, s_soft, s_fsoft, s_msg, s_hcopy, s_comb_out, s_comb,
                      s_fz, s_fo, s_fy, s_cp_out):
                pe.sem_inc(s, SLOT2)
            for s in (s_act, s_fact, s_xagg[2], s_xadd, s_uniq):
                pe.sem_inc(s, 1)
            pe.wait_ge(s_const_in, 18 * 16)

            def transform(rnd):
                with pe.Fori(0, TRANS_ITERS) as r:
                    for j in range(BODY):
                        n = r * BODY + j
                        pe.wait_ge(s_h_ready[rnd], n + 1)
                        pe.wait_ge(s_row_ready[rnd], n + 1)
                        nc.tensor.matmul(ps_a[j % 2][:, 0:WIDE], h_stage[:, j % 2, :], w_types[rnd][:, 0:WIDE],
                                         start=True, stop=True)
                        nc.tensor.matmul(ps_a[j % 2][:, WIDE:TD], h_stage[:, j % 2, :], w_types[rnd][:, WIDE:TD],
                                         start=True, stop=True).then_inc(s_mm_done[rnd], 1)

            def aggregate(p, r, h):
                for j in range(2):
                    g = r * 4 + (2 * h + j)
                    pe.wait_ge(s_gather[p][h][j], r * (16 * GROUP_TILES) + 16 * GROUP_TILES)
                    pe.wait_ge(s_onehot[p], r * 2 + (h + 1))
                    pe.wait_ge(s_acc[p], g + 1)
                    for t in range(GROUP_TILES):
                        last = nc.tensor.matmul(ps_agg[j], gathered[:, h, j * GROUP_TILES + t, :], onehot[:, h, j * GROUP_TILES + t, :],
                                                start=(t == 0), stop=(t == GROUP_TILES - 1))
                    last.then_inc(s_agg[p], 1)
                with pe.If(flag > 0):
                    for j in range(2):
                        g = r * 4 + (2 * h + j)
                        with pe.Fori(0, WIDE_STEPS) as b:
                            pe.wait_ge(s_xoh[p], g * WIDE_STEPS + b + 1)
                            for t in range(GROUP_TILES):
                                last = nc.tensor.matmul(ps_extra[:, :], gathered[:, h, j * GROUP_TILES + t, :], x_onehot[:, t, :],
                                                        start=(t == 0), stop=(t == GROUP_TILES - 1))
                            last.then_inc(s_xagg[p], 1)

            def first_of_source(k, h):
                pe.wait_ge(s_dup, k + 1)
                pe.wait_ge(s_uniq, k * 3 + 1)
                for t in range(HALF_TILES):
                    last = nc.tensor.matmul(ps_first[:, t:t + 1], same_src[:, h, t, :], first_w[:, 0:1], start=True,
                                            stop=True)
                last.then_inc(s_first, 1)

            for rnd in range(2):
                transform(rnd)
                if rnd == 0:
                    pe.wait_ge(s_setup, 18)
                    pe.wait_ge(s_parts_in, 48)
                    flag = nc.tensor.value_load(flag_i[0:1, 0:1], min_val=0, max_val=1)
                with pe.Fori(0, ITERS) as r:
                    for h in range(2):
                        aggregate(rnd, r, h)
                        if rnd == 1:
                            first_of_source(r * 2 + h, h)

            def mean(m, s):
                pe.wait_ge(s_y, m + 1)
                pe.wait_ge(s_yc, m + 1)
                nc.tensor.matmul(ps_mean[s], ones_d[:, :], buf_x[:, ds(m * WIDE, WIDE)], start=True,
                                 stop=True).then_inc(s_mean, 1)

            def rows(m, s):
                pe.wait_ge(s_yc, m + (1 + SLOT2))
                pe.wait_ge(s_hrow, m + 1)
                pe.wait_ge(s_x1, m + 1)
                for b in range(4):
                    tile = slice(b * P, (b + 1) * P)
                    nc.tensor.matmul(ps_hrows[s][:, tile], centred[:, s, tile], w_in[:, :], start=True, stop=True)
                    last = nc.tensor.matmul(ps_xrows[s][:, tile], centred[:, s, tile], ident[:, :], start=True, stop=True)
                last.then_inc(s_rows, 1)

            def variance(m, s):
                pe.wait_ge(s_sq, m + (1 + SLOT2))
                pe.wait_ge(s_sd, m + 1)
                for b in range(4):
                    last = nc.tensor.matmul(ps_var[s][:, b:b + 1], squares[:, s, b * P:(b + 1) * P], ones_d[:, 0:1],
                                            start=True, stop=True)
                last.then_inc(s_var, 1)

            mean(0, 0)
            mean(1, 1)
            rows(0, 0)
            variance(0, 0)
            with pe.Fori(0, CHUNKS // 4) as r:
                for j in range(4):
                    m = r * 4 + j
                    mean(m + 2, j % 2)
                    rows(m + 1, (j + 1) % 2)
                    variance(m + 1, (j + 1) % 2)
            for m in range(CHUNKS // 4 * 4 + 1, CHUNKS):
                rows(m, m % 2)
                variance(m, m % 2)

            def filter_in(k, h, f_count):
                for j in range(2):
                    pe.wait_ge(s_f_in[h], f_count)
                    pe.wait_ge(s_soft, k * 2 + (j - 1 + SLOT2))
                    nc.tensor.matmul(ps_z[j], wf1[:, :], f_sb[:, h, j, :], start=True, stop=True).then_inc(s_z, 1)

            pe.wait_ge(s_cut, 1)
            filter_in(0, 0, 16)
            with pe.Fori(0, ITERS) as r:
                for h in range(2):
                    k = r * 2 + h
                    for j in range(2):
                        pe.wait_ge(s_win_in[h], r * 32 + 32)
                        pe.wait_ge(s_spread, k * 2 + (j + 1))
                        pe.wait_ge(s_hcopy, k * 2 + (j + 1))
                        for t in range(GROUP_TILES):
                            tile = slice(t * P, (t + 1) * P)
                            last = nc.tensor.matmul(ps_h[j][:, tile], spread[:, h, j * WIDE + t * P:j * WIDE + (t + 1) * P],
                                                    h_win[:, h, j, :], start=True, stop=True)
                        last.then_inc(s_hexp, 1)
                    with pe.If(flag > 0):
                        with pe.Fori(0, 2) as j:
                            with pe.Fori(0, BLOCKS) as b:
                                step = (k * 2 + j) * BLOCKS + b
                                pe.wait_ge(s_comb_out, k * 2 + SLOT2)
                                pe.wait_ge(s_xh_in, step * 16 + 16)
                                pe.wait_ge(s_xoh[2], step + 1)
                                pe.wait_ge(s_xadd, step + 1)
                                for t in range(GROUP_TILES):
                                    tile = slice(t * P, (t + 1) * P)
                                    last = nc.tensor.matmul(ps_c[0][:, tile], x_onehot[:, 0, tile], x_h, start=True,
                                                            stop=True)
                                last.then_inc(s_xagg[2], 1)
                    filter_in(k + 1, 1 - h, (r + h) * 16 + 16)
                    for j in range(2):
                        pe.wait_ge(s_soft, k * 2 + (j + 1 + SLOT2))
                        nc.tensor.matmul(ps_w[j], ones_rows[:, :],
                                         bias_rows[:, 0, :].unsqueeze(1).broadcast_to([3, GROUP_TILES, D]),
                                         start=True, stop=False)
                        for t in range(GROUP_TILES):
                            last = nc.tensor.matmul(ps_w[j][:, t * D:(t + 1) * D], soft[:, j, t * P:(t + 1) * P],
                                                    wf2[:, :], start=False, stop=(t == GROUP_TILES - 1))
                        last.then_inc(s_w, 1)
                    for j in range(2):
                        pe.wait_ge(s_msg, k * 2 + (j + 1 + SLOT2))
                        pe.wait_ge(s_same, k + 1)
                        pe.wait_ge(s_comb_out, k * 2 + (j + 1))
                        for t in range(GROUP_TILES):
                            last = nc.tensor.matmul(ps_c[j][:, t * D:(t + 1) * D], same_src[:, h, j * GROUP_TILES + t, :],
                                                    msg[:, j, t * D:(t + 1) * D], start=True, stop=True)
                        last.then_inc(s_comb, 1)

            def turn_sums(m, q, s):
                pe.wait_ge(s_cp_sum, m * SUM_STEPS + SUM_STEPS)
                pe.wait_ge(s_cp_out, m + 1)
                for b in range(4):
                    for c in range(2):
                        last = nc.tensor.matmul(ps_b[s][:, b * P:(b + 1) * P], copy_rows[:, q, c, b * P:(b + 1) * P],
                                                ident[:, :], start=(c == 0), stop=(c == 1))
                last.then_inc(s_cp_t, 1)

            def out_z(m, s):
                pe.wait_ge(s_cp_out, m + (1 + SLOT2))
                nc.tensor.matmul(ps_z[s], wo1[:, :], out_t[:, s, :], start=True, stop=True).then_inc(s_fz, 1)

            def out_rows_sum(m, s):
                pe.wait_ge(s_fy, m + 1)
                nc.tensor.matmul(ps_w[s], ones_rows[:, :], bias_rows[:, 1, :].unsqueeze(1).broadcast_to([3, 4, D]),
                                 start=True, stop=False)
                nc.tensor.matmul(ps_w[s], ident[:, :], buf_x[:, ds(m * WIDE, WIDE)], start=False, stop=False)
                pe.wait_ge(s_fsoft, m + (1 + SLOT2))
                for t in range(4):
                    tile = slice(t * P, (t + 1) * P)
                    last = nc.tensor.matmul(ps_w[s][:, tile], soft[:, s, tile], wo2[:, :], start=False, stop=(t == 3))
                last.then_inc(s_fo, 1)

            def output_step(m, j):
                s = j % 2
                if j + 1 < CHUNKS:
                    out_z(m + 1, 1 - s)
                out_rows_sum(m, s)
                if j + 2 < CHUNKS:
                    turn_sums(m + 2, (j + 2) % 3, s)

            turn_sums(0, 0, 0)
            turn_sums(1, 1, 1)
            out_z(0, 0)
            with pe.Fori(0, LOOP6) as r:
                for j in range(6):
                    output_step(r * 6 + j, j)
            for m in range(6 * LOOP6, CHUNKS):
                output_step(m, m)


def kernel(**inputs):
    import concourse.bacc as bacc
    from concourse.bass_utils import run_bass_kernel_spmd

    def tiles(name, padding=0):
        a = np.asarray(inputs[name]).reshape(E)
        return np.ascontiguousarray(np.pad(a, (0, COLS * P - E), constant_values=padding).reshape(COLS, P).T)

    x = np.pad(np.asarray(inputs["x"]), ((0, NBUF - N), (0, 0)))
    dst = np.asarray(inputs["dst"])
    attr = np.pad(np.asarray(inputs["edge_attr3_1x32"]).reshape(E, RBF), ((0, HALVES * 2 * GROUP_EDGES - E), (0, 0)))
    arrays = {
        "xT": np.ascontiguousarray(x.T),
        "src": tiles("src", NPAD - 1), "dst": tiles("dst"), "etype": tiles("edge_type_5"), "cutoff": tiles("edge_weight1"),
        "dst_groups": np.pad(dst, (0, GROUPS * GROUP_EDGES - E), mode="edge").reshape(RANGE_PARTS, 4 * GROUP_EDGES),
        "src_groups": np.pad(np.asarray(inputs["src"]), (0, GROUPS * GROUP_EDGES - E), constant_values=NPAD - 1
                             ).reshape(RANGE_PARTS, 4 * GROUP_EDGES),
        "first_w": np.array([[3.0 ** (P // 2 - p), 2 * 3.0 ** (P // 2 - p)] for p in range(P)], np.float32),
        "attr": np.ascontiguousarray(attr.reshape(HALVES, 2, GROUP_EDGES, RBF).transpose(0, 1, 3, 2)
                                     ).reshape(HALVES * 2 * RBF, GROUP_EDGES),
    }
    for i in (1, 2):
        arrays[f"w{i}T"] = np.ascontiguousarray(np.asarray(inputs[f"L0_gnn_w{i}"]).T)
        arrays[f"b{i}"] = np.asarray(inputs[f"L0_gnn_b{i}"]).reshape(1, TD)
        arrays[f"g{i}"] = np.asarray(inputs[f"L0_gnn_g{i}"]).reshape(D, 1)
        arrays[f"be{i}"] = np.asarray(inputs[f"L0_gnn_be{i}"]).reshape(D, 1)
    for name in ("W_in", "Wf1", "Wf2", "Wo1", "Wo2"):
        arrays[name] = np.asarray(inputs[f"L1_gnn_{name}"])
    for name, shape in (("bf1", (1, D)), ("bo1", (D, 1)), ("bf2", (1, D)), ("bo2", (1, D))):
        arrays[name] = np.asarray(inputs[f"L1_gnn_{name}"]).reshape(shape)

    nc = bacc.Bacc("TRN2", target_bir_lowering=False, num_devices=1)
    dram = {n: nc.dram_tensor(f"in_{n}", a.shape, mybir.dt.from_np(a.dtype), kind="ExternalInput").ap()
            for n, a in arrays.items()}
    out = nc.dram_tensor("out", (NBUF, D), mybir.dt.float32, kind="ExternalOutput").ap()
    gnn_program(nc, dram, out)
    ran = run_bass_kernel_spmd(nc, [{f"in_{n}": a for n, a in arrays.items()}], core_ids=[0])
    return ran.results[0]["out"][:N]
```
